# Optimizing a Trainium2 kernel written in Bass

```python
import numpy as np
import jax
import jax.numpy as jnp

def _softmax(x, axis=-1):
    return jax.nn.softmax(x, axis=axis)

def _gelu(x):
    return jax.nn.gelu(x, approximate=True)

def _silu(x):
    return jax.nn.silu(x)

def _sigmoid(x):
    return jax.nn.sigmoid(x)

def _layernorm(x, axis=-1, eps=1e-05):
    m = jnp.mean(x, axis=axis, keepdims=True)
    v = jnp.var(x, axis=axis, keepdims=True)
    return (x - m) / jnp.sqrt(v + eps)

def _scatter_add(tgt, idx, src, axis=0):
    return tgt.at[idx].add(src)

def _segment_sum(src, seg, n):
    return jax.ops.segment_sum(src, seg, n)
kernel_name = 'mk_gnn_resnorm_d4_gnn_r32_497488'

def setup_inputs(seed: int=0):
    np.random.seed(seed)
    _w = jnp.asarray

    def _rec_inputs():
        import jax
        import jax.numpy as jnp
        _gk = jax.random.key(seed)
        x = -0.0003713 + 1 * jax.random.normal(jax.random.fold_in(_gk, 1), (3125, 128), jnp.float32)
        src = jax.random.randint(jax.random.fold_in(_gk, 2), (50000,), 0, 3125, jnp.int32)
        dst = jnp.minimum((3125 * jax.random.uniform(jax.random.fold_in(_gk, 3), (50000,)) ** 2.0).astype(jnp.int32), 99999)
        _o = jnp.argsort(dst, stable=True)
        src = src[_o]
        dst = dst[_o]
        edge_type_16 = jax.random.randint(jax.random.fold_in(_gk, 13), (50000,), 0, 16, jnp.int32)
        edge_weight = jax.random.uniform(jax.random.fold_in(_gk, 14), (50000,), jnp.float32, 0.0, 1)
        return (x, src, dst, edge_type_16, edge_weight)
    x, src, dst, edge_type_16, edge_weight = _rec_inputs()

    def _L0_gnn_setup():
        import jax, jax.numpy as jnp
        import numpy as np
        N_NODES = 3125
        N_EDGES = 100000
        D = 128
        LN_EPS = 1e-05
        key = jax.random.key(seed)
        k1, k2, k3, k4, k5 = jax.random.split(key, 5)
        X = jax.random.normal(k1, (N_NODES, D), dtype=jnp.float32)
        edge_src = jax.random.randint(k2, (N_EDGES,), 0, N_NODES, dtype=jnp.int64)
        edge_dst = jax.random.randint(k3, (N_EDGES,), 0, N_NODES, dtype=jnp.int64)
        edge_w = jax.random.uniform(k4, (N_EDGES,), dtype=jnp.float32)
        ln_gamma = jnp.ones((D,), dtype=jnp.float32)
        ln_beta = jnp.zeros((D,), dtype=jnp.float32)
        W = jax.random.normal(k5, (D, D), dtype=jnp.float32) * (1.0 / np.sqrt(D))
        b = jnp.zeros((D,), dtype=jnp.float32)
        return {'X': X, 'edge_src': edge_src, 'edge_dst': edge_dst, 'edge_w': edge_w, 'ln_gamma': ln_gamma, 'ln_beta': ln_beta, 'W': W, 'b': b}
    _L0_gnn_all = _L0_gnn_setup()
    _L0_gnn_in = {k: v for k, v in _L0_gnn_all.items() if k in ('ln_gamma', 'ln_beta', 'W', 'b')}
    del _L0_gnn_all

    def _L1_gnn_setup():
        import jax, jax.numpy as jnp
        import numpy as np
        N = 50000
        E = 20000
        D = 128
        NUM_LAYERS = 2
        key = jax.random.key(seed)
        k1, k2 = jax.random.split(key)
        emb = jax.random.normal(k1, (N, D), dtype=jnp.float32)
        edge_index = jax.random.randint(k2, (2, E), 0, N, dtype=jnp.int64)
        return {'emb': emb, 'edge_index': edge_index}
    _L1_gnn_all = _L1_gnn_setup()
    _L1_gnn_in = {k: v for k, v in _L1_gnn_all.items() if k in ()}
    del _L1_gnn_all

    def _L2_gnn_setup():
        import jax, jax.numpy as jnp
        import numpy as np
        N, E, D, R, H, L = (30000, 15000, 128, 16, 4, 3)
        DH = D // H
        key = jax.random.key(seed)
        ks = jax.random.split(key, 16)
        s = 1.0 / np.sqrt(D)
        return {'feat': jax.random.normal(ks[0], (N, D), jnp.float32), 'src': jax.random.randint(ks[1], (E,), 0, N, jnp.int32), 'dst': jax.random.randint(ks[2], (E,), 0, N, jnp.int32), 'etype': jax.random.randint(ks[3], (E,), 0, R, jnp.int32), 'temporal_weight': jax.random.uniform(ks[4], (E,), jnp.float32), 'W_rel': jax.random.normal(ks[5], (L, R, D, D), jnp.float32) * s, 'b_rel': jnp.zeros((L, D), jnp.float32), 'W_loop': jax.random.normal(ks[6], (L, D, D), jnp.float32) * s, 'W_gat': jax.random.normal(ks[7], (L, D, D), jnp.float32) * s, 'attn_l': jax.random.normal(ks[8], (L, H, DH), jnp.float32) * s, 'attn_r': jax.random.normal(ks[9], (L, H, DH), jnp.float32) * s, 'b_gat': jnp.zeros((L, D), jnp.float32), 'W_fuse': jax.random.normal(ks[10], (2 * D, D), jnp.float32) * (1.0 / np.sqrt(2 * D)), 'b_fuse': jnp.zeros((D,), jnp.float32), 'W_gate': jax.random.normal(ks[11], (D + 1, D), jnp.float32) * s, 'b_gate': jnp.zeros((D,), jnp.float32)}
    _L2_gnn_all = _L2_gnn_setup()
    _L2_gnn_in = {k: v for k, v in _L2_gnn_all.items() if k in ('W_rel', 'b_rel', 'W_loop', 'W_gat', 'attn_l', 'attn_r', 'b_gat', 'W_fuse', 'b_fuse', 'W_gate', 'b_gate')}
    del _L2_gnn_all

    def _L3_gnn_setup():
        import jax, jax.numpy as jnp
        import numpy as np
        N_NODES = 50000
        N_EDGES = 50000
        D = 128

        def _degree_norm(idx, n_nodes, dtype):
            deg = jax.ops.segment_sum(jnp.ones((idx.shape[0],), dtype=dtype), idx, num_segments=n_nodes)
            return jax.lax.rsqrt(jnp.maximum(deg, 1.0))

        def _graph_conv(h, e_weight, src, dst, W, b, out_norm, in_norm):
            feat_src = h * out_norm[:, None]
            msg = feat_src[src] * e_weight[:, None]
            agg = jax.ops.segment_sum(msg, dst, num_segments=h.shape[0])
            agg = agg * in_norm[:, None]
            return jax.nn.relu(agg @ W + b)
        key = jax.random.key(seed)
        ks = jax.random.split(key, 6)
        x = jax.random.normal(ks[0], (N_NODES, D), dtype=jnp.float32)
        e_weight = jax.random.uniform(ks[1], (N_EDGES,), dtype=jnp.float32)
        src = jax.random.randint(ks[2], (N_EDGES,), 0, N_NODES)
        dst = jax.random.randint(ks[3], (N_EDGES,), 0, N_NODES)
        scale = 1.0 / np.sqrt(D)
        W1 = jax.random.normal(ks[4], (D, D), dtype=jnp.float32) * scale
        W2 = jax.random.normal(ks[5], (D, D), dtype=jnp.float32) * scale
        b1 = jnp.zeros((D,), dtype=jnp.float32)
        b2 = jnp.zeros((D,), dtype=jnp.float32)
        return {'x': x, 'e_weight': e_weight, 'src': src, 'dst': dst, 'W1': W1, 'b1': b1, 'W2': W2, 'b2': b2}
    _L3_gnn_all = _L3_gnn_setup()
    _L3_gnn_in = {k: v for k, v in _L3_gnn_all.items() if k in ('W1', 'b1', 'W2', 'b2')}
    del _L3_gnn_all
    return {'x': x, 'src': src, 'dst': dst, 'edge_type_16': edge_type_16, 'edge_weight': edge_weight, 'L0_gnn_ln_gamma': _L0_gnn_in['ln_gamma'], 'L0_gnn_ln_beta': _L0_gnn_in['ln_beta'], 'L0_gnn_W': _L0_gnn_in['W'], 'L0_gnn_b': _L0_gnn_in['b'], 'L2_gnn_W_rel': _L2_gnn_in['W_rel'], 'L2_gnn_b_rel': _L2_gnn_in['b_rel'], 'L2_gnn_W_loop': _L2_gnn_in['W_loop'], 'L2_gnn_W_gat': _L2_gnn_in['W_gat'], 'L2_gnn_attn_l': _L2_gnn_in['attn_l'], 'L2_gnn_attn_r': _L2_gnn_in['attn_r'], 'L2_gnn_b_gat': _L2_gnn_in['b_gat'], 'L2_gnn_W_fuse': _L2_gnn_in['W_fuse'], 'L2_gnn_b_fuse': _L2_gnn_in['b_fuse'], 'L2_gnn_W_gate': _L2_gnn_in['W_gate'], 'L2_gnn_b_gate': _L2_gnn_in['b_gate'], 'L3_gnn_W1': _L3_gnn_in['W1'], 'L3_gnn_b1': _L3_gnn_in['b1'], 'L3_gnn_W2': _L3_gnn_in['W2'], 'L3_gnn_b2': _L3_gnn_in['b2']}

def reference(x, src, dst, edge_type_16, edge_weight, L0_gnn_ln_gamma, L0_gnn_ln_beta, L0_gnn_W, L0_gnn_b, L2_gnn_W_rel, L2_gnn_b_rel, L2_gnn_W_loop, L2_gnn_W_gat, L2_gnn_attn_l, L2_gnn_attn_r, L2_gnn_b_gat, L2_gnn_W_fuse, L2_gnn_b_fuse, L2_gnn_W_gate, L2_gnn_b_gate, L3_gnn_W1, L3_gnn_b1, L3_gnn_W2, L3_gnn_b2):
    import jax
    import jax.numpy as jnp

    def _L0_gnn_ref(X, edge_src, edge_dst, edge_w, ln_gamma, ln_beta, W, b):
        import jax, jax.numpy as jnp
        import numpy as np
        N_NODES = 3125
        N_EDGES = 100000
        D = 128
        LN_EPS = 1e-05
        mu = jnp.mean(X, axis=-1, keepdims=True)
        var = jnp.mean(jnp.square(X - mu), axis=-1, keepdims=True)
        H = (X - mu) * jax.lax.rsqrt(var + LN_EPS) * ln_gamma + ln_beta
        H = jnp.einsum('nd,od->no', H, W) + b
        msg = edge_w[:, None] * H[edge_src]
        H = jax.ops.segment_sum(msg, edge_dst, num_segments=N_NODES)
        return jax.nn.relu(H) + X

    def _L1_gnn_ref(emb, edge_index):
        import jax, jax.numpy as jnp
        import numpy as np
        N = 50000
        E = 20000
        D = 128
        NUM_LAYERS = 2
        row, col = (edge_index[0], edge_index[1])
        n = emb.shape[0]
        ones = jnp.ones(row.shape[0], dtype=emb.dtype)
        deg = jax.ops.segment_sum(ones, col, num_segments=n)
        deg_inv_sqrt = jnp.where(deg > 0, jax.lax.rsqrt(deg), 0.0).astype(emb.dtype)
        norm = deg_inv_sqrt[row] * deg_inv_sqrt[col]
        x = emb
        out = x
        for _ in range(NUM_LAYERS):
            msgs = x[row] * norm[:, None]
            x = jax.ops.segment_sum(msgs, col, num_segments=n)
            out = out + x
        return out / (NUM_LAYERS + 1)

    def _L2_gnn_ref(feat, src, dst, etype, temporal_weight, W_rel, b_rel, W_loop, W_gat, attn_l, attn_r, b_gat, W_fuse, b_fuse, W_gate, b_gate):
        import jax, jax.numpy as jnp
        import numpy as np
        N, E, D, R, H, L = (30000, 15000, 128, 16, 4, 3)
        DH = D // H
        n = feat.shape[0]
        h = feat
        tw_mean = jnp.mean(temporal_weight)
        for l in range(L):
            ht = jnp.einsum('nd,rdo->nro', h, W_rel[l])
            msg = ht[src, etype]
            h_rel = jax.ops.segment_sum(msg, dst, num_segments=n)
            h_rel = h_rel + h @ W_loop[l] + b_rel[l]
            z = (h @ W_gat[l]).reshape(n, H, DH)
            el = jnp.sum(z * attn_l[l], axis=-1)
            er = jnp.sum(z * attn_r[l], axis=-1)
            e = jax.nn.leaky_relu(el[src] + er[dst], 0.2)
            m = jax.ops.segment_max(e, dst, num_segments=n)
            ex = jnp.exp(e - m[dst])
            denom = jax.ops.segment_sum(ex, dst, num_segments=n)
            alpha = ex / denom[dst]
            h_gat = jax.ops.segment_sum(alpha[:, :, None] * z[src], dst, num_segments=n)
            h_gat = h_gat.reshape(n, D) + b_gat[l]
            hc = jnp.concatenate([h_rel, h_gat], axis=1) @ W_fuse + b_fuse
            if l == 0:
                avg = jnp.full((n, 1), tw_mean, dtype=hc.dtype)
                gate = jax.nn.sigmoid(jnp.concatenate([hc, avg], axis=1) @ W_gate + b_gate)
                hc = hc * gate
            h = jax.nn.relu(hc)
        return h

    def _L3_gnn_ref(x, e_weight, src, dst, W1, b1, W2, b2):
        import jax, jax.numpy as jnp
        import numpy as np
        N_NODES = 50000
        N_EDGES = 50000
        D = 128

        def _degree_norm(idx, n_nodes, dtype):
            deg = jax.ops.segment_sum(jnp.ones((idx.shape[0],), dtype=dtype), idx, num_segments=n_nodes)
            return jax.lax.rsqrt(jnp.maximum(deg, 1.0))

        def _graph_conv(h, e_weight, src, dst, W, b, out_norm, in_norm):
            feat_src = h * out_norm[:, None]
            msg = feat_src[src] * e_weight[:, None]
            agg = jax.ops.segment_sum(msg, dst, num_segments=h.shape[0])
            agg = agg * in_norm[:, None]
            return jax.nn.relu(agg @ W + b)
        n = x.shape[0]
        out_norm = _degree_norm(src, n, x.dtype)
        in_norm = _degree_norm(dst, n, x.dtype)
        h = x
        for W, b in ((W1, b1), (W2, b2)):
            h_nxt = _graph_conv(h, e_weight, src, dst, W, b, out_norm, in_norm)
            h = h_nxt + h
        return h
    edge_index = jnp.stack([src, dst])
    x = _layernorm(x + _L0_gnn_ref(x, src, dst, edge_weight, L0_gnn_ln_gamma, L0_gnn_ln_beta, L0_gnn_W, L0_gnn_b), axis=-1)
    x = _layernorm(x + _L1_gnn_ref(x, edge_index), axis=-1)
    x = _layernorm(x + _L2_gnn_ref(x, src, dst, edge_type_16, edge_weight, L2_gnn_W_rel, L2_gnn_b_rel, L2_gnn_W_loop, L2_gnn_W_gat, L2_gnn_attn_l, L2_gnn_attn_r, L2_gnn_b_gat, L2_gnn_W_fuse, L2_gnn_b_fuse, L2_gnn_W_gate, L2_gnn_b_gate), axis=-1)
    x = _layernorm(x + _L3_gnn_ref(x, edge_weight, src, dst, L3_gnn_W1, L3_gnn_b1, L3_gnn_W2, L3_gnn_b2), axis=-1)
    return x

_drawn_inputs = setup_inputs


def setup_inputs(seed=0):
    import zlib

    import numpy as np

    out = dict(_drawn_inputs(seed))
    spreads = {'L0_gnn_ln_gamma': (1.0, 0.2),
     'L0_gnn_ln_beta': (0.0, 0.1),
     'L0_gnn_b': (0.0, 0.1),
     'L2_gnn_b_rel': (0.0, 0.1),
     'L2_gnn_b_gat': (0.0, 0.1),
     'L2_gnn_b_fuse': (0.0, 0.1),
     'L2_gnn_b_gate': (0.0, 0.396),
     'L3_gnn_b1': (0.0, 0.1),
     'L3_gnn_b2': (0.0, 0.1)}
    factors = {}
    for name, (base, spread) in spreads.items():
        noise = np.random.default_rng([zlib.crc32(name.encode()), seed]).standard_normal(out[name].shape)
        drawn = base * np.exp(spread * noise) if base else spread * noise
        out[name] = jnp.asarray(drawn.astype(out[name].dtype))
    for name, factor in factors.items():
        out[name] = (out[name] * factor).astype(out[name].dtype)
    return out
```

```python
import concourse.bass as bass
from concourse import mybir
from contextlib import ExitStack

N, D, E, R, L, HEADS = 3125, 128, 50000, 16, 3, 4
P = 128
DH = D // HEADS
NT = -(-N // P)
NPAD = NT * P
EP = 125
EC = E // EP
G = 8
TILES = -(-((E + NT * (P - 1)) // P) // (2 * G)) * 2 * G
ITERS = TILES // (2 * G)
MSG_SLOTS = 4
DEG_ITERS = EC // (2 * G)
ZW = D + HEADS
BIG = float(2.0 ** 100)
LN_EPS = 1e-5


class Steps:

    def __init__(self, sem):
        self.sem, self.now, self.made = sem, 0, 0

    def add(self, k=1):
        self.now, self.made = self.now + k, self.made + k
        return self.now

    def rounds(self, eng, count, each):
        start = self.now
        with eng.Fori(0, count) as i:
            self.now, self.made = i * each + start, 0
            yield i
            assert self.made == each, (self.made, each)
        self.now = start + count * each


def gnn_stack(nc, a, out):
    f32, bf16, i32, u32 = mybir.dt.float32, mybir.dt.bfloat16, mybir.dt.int32, mybir.dt.uint32
    ALU, ACT, AX = mybir.AluOpType, mybir.ActivationFunctionType, mybir.AxisListType

    def dram(name, shape, dt):
        return nc.dram_tensor(name, shape, dt, kind="Internal").ap()

    records = dram("records", [P * TILES, 4], f32)
    node_rows = dram("node_rows", [NPAD, D], f32)
    attention_rows = dram("attention_rows", [NPAD, ZW], f32)
    relation_rows = dram("relation_rows", [NPAD * R, D], f32)
    edge_z = dram("edge_z", [P, TILES * ZW], f32)
    local_rows = dram("local_rows", [TILES * P], f32)
    member_d = dram("member_d", [P, TILES * P], bf16)
    mask_d = dram("mask_d", [P, TILES * P], bf16)

    with ExitStack() as ctx:
        def sb(name, shape, dt=f32):
            return ctx.enter_context(nc.sbuf_tensor(name, shape, dt))

        def sem(name):
            return ctx.enter_context(nc.semaphore(name))

        def pair(name):
            return [sem(name + "_even"), sem(name + "_odd")]

        lane = sb("lane", [P, P])
        part = sb("part", [P, 1])
        ident = sb("ident", [P, P])
        ident_b = sb("ident_b", [P, P], bf16)
        below = sb("below", [P, P])
        ones = sb("ones", [P, P])
        zeros_b = sb("zeros_b", [P, 4 * P], bf16)
        tile_no = sb("tile_no", [P, TILES])
        pick = sb("pick", [3 * G * HEADS, G * HEADS, P], bf16)
        x = sb("x", [P, NT, D])
        h = sb("h", [P, NT, D])
        agg = sb("agg", [P, NT, D + ZW])
        agg_flat = agg[:, :, :].rearrange("p b c -> p (b c)")
        tmp = agg_flat[:, 0:NPAD].rearrange("p (b d) -> p b d", d=D)
        tmp2 = agg_flat[:, NPAD:2 * NPAD].rearrange("p (b d) -> p b d", d=D)
        self_term = sb("self_term", [P, NT, D])
        hT = sb("hT", [P, NT, D])
        gat = sb("gat", [P, NT, ZW])
        local = sb("local", [P, TILES])
        weight = sb("weight", [P, TILES])
        src_row = sb("src_row", [P, TILES], u32)
        rel_row = sb("rel_row", [P, TILES], u32)
        dst_tile = sb("dst_tile", [P, TILES])
        dst_tile_i = sb("dst_tile_i", [P, TILES], i32)
        ring = [sb(f"ring{k}", [P, G, ZW]) for k in range(2)]
        index = [sb(f"index{k}", [P, G], u32) for k in range(2)]
        onehot = [sb(f"onehot{k}", [P, G, P]) for k in range(2)]
        work = [sb(f"work{k}", [P, 2 * G * ZW]) for k in range(2)]
        z_in = [w[:, 0:G * ZW].rearrange("p (g c) -> p g c", c=ZW) for w in work]
        z_msg = [w[:, G * ZW:2 * G * ZW].rearrange("p (g c) -> p g c", c=ZW) for w in work]
        stage = [w[:, 0:R * D] for w in work]
        member = [sb(f"member{k}", [P, G, P], bf16) for k in range(2)]
        score = [sb(f"score{k}", [P, G, HEADS]) for k in range(2)]
        el_parts = [sb(f"el_parts{k}", [P, 3, G, HEADS], bf16) for k in range(2)]
        elT = [sb(f"elT{k}", [3 * G * HEADS, P], bf16) for k in range(2)]
        stat = sb("stat", [P, 8, NT])
        er = sb("er", [P, NT, HEADS])
        el = sb("el", [P, NT, HEADS])
        top = sb("top", [P, NT, HEADS])
        top_tile = sb("top_tile", [P, HEADS])
        er_top = sb("er_top", [P, NT, 3, 2 * HEADS], bf16)
        sc = sb("sc", [P, NT, HEADS])
        in_norm = sb("in_norm", [P, NT])
        in_norm0 = sb("in_norm0", [P, NT])
        out_norm = sb("out_norm", [P, NT])
        w_names = ["L0_gnn_W", "L3_gnn_W1", "L3_gnn_W2"]
        wt = {n: sb("s_" + n, [D, D]) for n in w_names}
        w0T = sb("w0T", [D, D])
        w_rel = sb("w_rel", [D, R, D])
        w_loop = sb("w_loop", [D, L, D])
        w_gat = sb("w_gat", [D, L, D])
        w_fuse = sb("w_fuse", [D, 2, D])
        w_gate = sb("w_gate", [D, D])
        LATE_LOADS = 2 + 3 + 7 + 5
        rows = ["L0_gnn_ln_gamma", "L0_gnn_ln_beta", "L0_gnn_b", "L2_gnn_b_fuse", "L2_gnn_b_gate",
                "L3_gnn_b1", "L3_gnn_b2"]
        row = {n: sb("r_" + n, [P, D]) for n in rows}
        gate_row = sb("gate_row", [P, D])
        b_rel = sb("b_rel", [P, D])
        b_gat = sb("b_gat", [P, D])
        attn_l = sb("attn_l", [P, D])
        attn_r = sb("attn_r", [P, D])
        weight_sum = sb("weight_sum", [P, 1])
        weight_mean = sb("weight_mean", [P, 1])

        def flat(t):
            return t[:, :, :].rearrange("p a b -> p (a b)")

        raw = agg_flat[:, 0:NPAD]
        src_i = raw[0:EP, 0:EC].bitcast(i32)
        dst_i = raw[0:EP, EC:2 * EC].bitcast(i32)
        typ_i = raw[0:EP, 2 * EC:3 * EC].bitcast(i32)
        w_in = raw[0:EP, 3 * EC:4 * EC]
        dtile_i = raw[0:EP, 4 * EC:5 * EC].bitcast(i32)
        dtile = raw[0:EP, 5 * EC:6 * EC]
        stile = raw[0:EP, 6 * EC:7 * EC]
        slow = raw[0:EP, 7 * EC:8 * EC]
        raw2 = agg_flat[:, NPAD:2 * NPAD]
        dlow = raw2[0:EP, 0:EC]
        hit = raw2[0:EP, EC:2 * EC]
        run = raw2[0:EP, 2 * EC:3 * EC]
        pos = raw2[0:EP, 3 * EC:4 * EC]
        slot_i = raw2[0:EP, 4 * EC:5 * EC].bitcast(i32)
        hi_i = raw2[0:EP, 5 * EC:6 * EC].bitcast(i32)
        slot = raw2[0:EP, 6 * EC:7 * EC].bitcast(u32)
        tmp_i = raw2[0:EP, 7 * EC:8 * EC].bitcast(i32)
        rec = flat(hT)[0:EP, 0:4 * EC].rearrange("p (c f) -> p c f", f=4)
        blank = flat(self_term)[:, 0:4 * TILES].rearrange("p (c f) -> p c f", f=4)
        grouped = flat(h)[:, 0:4 * TILES].rearrange("p (c f) -> p c f", f=4)
        local_T = flat(gat)[0:TILES // 4, 0:4 * P].rearrange("p (k e) -> p k e", k=4)
        put_rec = [sb(f"put_rec{k}", [P, G, 4]) for k in range(2)]
        src_low = [flat(onehot[k]).bitcast(bf16)[0:EP, 0:G * P].rearrange("p (g n) -> p g n", g=G)
                   for k in range(2)]
        dst_low = [flat(onehot[k]).bitcast(bf16)[0:EP, G * P:2 * G * P].rearrange("p (g n) -> p g n", g=G)
                   for k in range(2)]
        src_high = [flat(z_in[k]).bitcast(bf16)[0:EP, 0:G * NT].rearrange("p (g n) -> p g n", g=G)
                    for k in range(2)]
        dst_high = [flat(z_in[k]).bitcast(bf16)[0:EP, G * NT:2 * G * NT].rearrange("p (g n) -> p g n", g=G)
                    for k in range(2)]
        mask = [flat(onehot[k]).bitcast(bf16)[:, 0:G * P] for k in range(2)]
        total = sb("total", [P, NT])
        tiles_i = sb("tiles_i", [P, NT], i32)
        tiles = sb("tiles", [P, NT])
        first_tile = sb("first_tile", [P, NT])
        before = sb("before", [P, NT])
        wide = [w[:, 0:G * P] for w in work]

        ps = ctx.enter_context(nc.psum_tensor("ps", [P, 4096], f32))
        sums = ps[:, 0:NPAD]
        sums3 = sums.rearrange("p (b d) -> p b d", d=D)
        er_top_ps = [ps[:, 3072 + 512 * k:3072 + 512 * k + 2 * G * HEADS]
                     .rearrange("p (g c) -> p g c", c=2 * HEADS) for k in range(2)]
        msg_ps = [ps[:, 512 * k:512 * k + D + ZW] for k in range(MSG_SLOTS)]
        el_ps = [ps[:, 512 * k:512 * (k + 1)].rearrange("p (h e) -> p h e", h=HEADS) for k in range(4)]
        elT_ps = [ps[0:3 * G * HEADS, 2048 + 512 * k:2048 + 512 * k + P // 2].bitcast(bf16) for k in range(2)]

        loads = sem("loads")
        late_loads = sem("late_loads")
        constants = sem("constants")
        blank_ready = sem("blank_ready")
        blank_stored = sem("blank_stored")
        slots_ready = sem("slots_ready")
        put_staged = sem("put_staged")
        put_done = pair("put_done")
        grouped_loaded = sem("grouped_loaded")
        degree_hot = pair("degree_hot")
        degree_used = pair("degree_used")
        pe_go = sem("pe_go")
        pe_done = sem("pe_done")
        act_go = sem("act_go")
        act_done = sem("act_done")
        dve = sem("dve")
        local_ready = sem("local_ready")
        local_stored = sem("local_stored")
        wide_in = pair("wide_in")
        wide_used = pair("wide_used")
        member_made = pair("member_made")
        member_free = pair("member_free")
        member_out = pair("member_out")
        gathered = pair("gathered")
        half_free = pair("half_free")
        index_staged = sem("index_staged")
        onehot_ready = pair("onehot_ready")
        pass_go = sem("pass_go")
        rows_ready = sem("rows_ready")
        rows_stored = sem("rows_stored")
        rel_full = [pair("rel_full"), pair("rel_full_dve")]
        rel_ps_full = pair("rel_ps_full")
        rel_stored = pair("rel_stored")
        member_in = pair("member_in")
        z_stored = pair("z_stored")
        z_loaded = pair("z_loaded")
        el_split = pair("el_split")
        elT_ps_ready = pair("elT_ps_ready")
        elT_ready = pair("elT_ready")
        el_wide = sem("el_wide")
        el_taken = sem("el_taken")
        half_maxed = pair("half_maxed")
        er_top_ready = pair("er_top_ready")
        er_top_taken = pair("er_top_taken")
        score_ready = pair("score_ready")
        exp_ready = pair("exp_ready")
        msg_ready = pair("msg_ready")
        z_sum = sem("z_sum")
        z_added = sem("z_added")
        pool_passed = sem("pool_passed")
        layer_loads = sem("layer_loads")
        layer_free = sem("layer_free")
        stored = sem("stored")
        grouped_ready = sem("grouped_ready")
        act_passed = sem("act_passed")
        dve_passed = sem("dve_passed")

        block = ctx.enter_context(nc.Block())

        def spread(ap, n):
            return ap.unsqueeze(len(ap.shape)).to_broadcast([*ap.shape, n])

        def across(row_ap, n):
            return row_ap.unsqueeze(1).to_broadcast([row_ap.shape[0], n, row_ap.shape[1]])

        HALVES = range(2)
        LINEAR, MAXIMA, SUMS = "linear", "maxima", "sums"
        ORDER = [LINEAR] * 3 + [MAXIMA, SUMS] * L + [LINEAR] * 2
        WEIGHTED = [True, False, False] + [False, False] * L + [True, True]

        def rounds_before(p, *kinds):
            return sum(ITERS for k in ORDER[:p] if k in kinds)

        def rel_rounds(l, b):
            return l * ((NT + 1 - b % 2) // 2) + b // 2 + 1

        @block.sync
        def _(sp):
            e_view = lambda ap: ap.rearrange("(p c) -> p c", p=EP)
            sp.dma_start(dst_i, e_view(a["dst"])).then_inc(loads, 16)
            sp.dma_start(src_i, e_view(a["src"])).then_inc(loads, 16)
            sp.dma_start(typ_i, e_view(a["edge_type_16"])).then_inc(loads, 16)
            sp.dma_start(w_in, e_view(a["edge_weight"])).then_inc(loads, 16)
            full = (NT - 1) * P
            sp.dma_start(x[:, 0:NT - 1, :], a["x"][0:full, :].rearrange("(b p) d -> p b d", p=P)).then_inc(late_loads, 16)
            sp.wait_ge(constants, 1)
            sp.dma_start(x[0:N - full, NT - 1, :], a["x"][full:N, :]).then_inc(late_loads, 16)
            for n in w_names:
                sp.dma_start(wt[n][:, :], a[n]).then_inc(late_loads, 16)
            for n in rows:
                sp.dma_start(row[n][:, :], a[n].partition_broadcast(P)).then_inc(late_loads, 16)
            sp.dma_start(w_loop[:, :, :], a["L2_gnn_W_loop"].rearrange("l d o -> d l o")).then_inc(late_loads, 16)
            sp.dma_start(w_gat[:, :, :], a["L2_gnn_W_gat"].rearrange("l d o -> d l o")).then_inc(late_loads, 16)
            sp.dma_start(w_fuse[:, :, :], a["L2_gnn_W_fuse"].rearrange("(k d) o -> d k o", k=2)).then_inc(late_loads, 16)
            sp.dma_start(w_gate[:, :], a["L2_gnn_W_gate"][0:D, :]).then_inc(late_loads, 16)
            sp.dma_start(gate_row[:, :], a["L2_gnn_W_gate"][D:D + 1, :].squeeze(0).partition_broadcast(P)).then_inc(late_loads, 16)
            sp.wait_ge(blank_ready, 1)
            sp.dma_start(records.rearrange("(e t) f -> e t f", e=P), blank).then_inc(blank_stored, 16)
            sp.wait_ge(put_done[0], DEG_ITERS * G * 16)
            sp.wait_ge(put_done[1], DEG_ITERS * G * 16)
            sp.dma_start(grouped, records.rearrange("(e t) f -> e t f", e=P)).then_inc(grouped_loaded, 16)
            sp.wait_ge(local_ready, 1)
            sp.dma_start(local_rows.rearrange("(k t e) -> t k e", k=4, e=P), local_T).then_inc(local_stored, 16)
            sp.wait_ge(local_stored, 16)
            with sp.Fori(0, ITERS) as i:
                for k in HALVES:
                    sp.wait_ge(wide_used[k], i + 1)
                    sp.dma_start(wide[k], local_rows[bass.ds((i * 2 + k) * (G * P), G * P)].partition_broadcast(P)).then_inc(wide_in[k], 16)

            def store_rows(table, view, k):
                sp.wait_ge(rows_ready, k)
                sp.dma_start(table.rearrange("(b p) d -> p b d", p=P), view).then_inc(rows_stored, 16)

            count = 0
            for p, kind in enumerate(ORDER):
                if kind == LINEAR:
                    count += 1
                    store_rows(node_rows, tmp[:, :, :], count)
                if kind == MAXIMA:
                    l = rounds_before(p, MAXIMA) // ITERS
                    sp.wait_ge(layer_free, l + 1)
                    sp.dma_start(w_rel[:, :, :], a["L2_gnn_W_rel"][l].rearrange("r d o -> d r o")).then_inc(layer_loads, 16)
                    sp.dma_start(b_rel[:, :], a["L2_gnn_b_rel"][l].partition_broadcast(P)).then_inc(layer_loads, 16)
                    sp.dma_start(b_gat[:, :], a["L2_gnn_b_gat"][l].partition_broadcast(P)).then_inc(layer_loads, 16)
                    sp.dma_start(attn_l[:, :], a["L2_gnn_attn_l"][l].rearrange("h d -> (h d)").partition_broadcast(P)).then_inc(layer_loads, 16)
                    sp.dma_start(attn_r[:, :], a["L2_gnn_attn_r"][l].rearrange("h d -> (h d)").partition_broadcast(P)).then_inc(layer_loads, 16)
                    count += 1
                    store_rows(attention_rows, gat[:, :, :], count)
                    for b in range(NT):
                        k, seen = b % 2, rel_rounds(l, b)
                        sp.wait_ge(rel_full[0][k], seen)
                        sp.wait_ge(rel_full[1][k], seen)
                        sp.dma_start(relation_rows[b * P * R:(b + 1) * P * R, :].rearrange("(p r) d -> p (r d)", p=P),
                                     stage[k]).then_inc(rel_stored[k], 16)
                    with sp.Fori(0, ITERS) as i:
                        for k in HALVES:
                            cols = bass.ds((i * 2 + k) * (G * P), G * P)
                            sp.wait_ge(half_free[k], i + (rounds_before(p, LINEAR, MAXIMA, SUMS) + 1))
                            sp.dma_start(flat(member[k]), mask_d[:, cols]).then_inc(member_in[k], 16)
                        for k in HALVES:
                            sp.wait_ge(gathered[k], i * (16 * G) + (rounds_before(p, LINEAR, MAXIMA, SUMS) + 1) * 16 * G)
                            sp.dma_start(edge_z[:, bass.ds((i * 2 + k) * (G * ZW), G * ZW)], flat(ring[k])).then_inc(z_stored[k], 16)
                if kind == SUMS:
                    for k in HALVES:
                        sp.wait_ge(z_stored[k], (rounds_before(p, MAXIMA)) * 16)
                    with sp.Fori(0, ITERS) as i:
                        for k in HALVES:
                            sp.wait_ge(half_free[k], i + (rounds_before(p, LINEAR, MAXIMA, SUMS) + 1))
                            sp.dma_start(flat(member[k]), member_d[:, bass.ds((i * 2 + k) * (G * P), G * P)]).then_inc(member_in[k], 16)
                            sp.dma_start(flat(z_in[k]), edge_z[:, bass.ds((i * 2 + k) * (G * ZW), G * ZW)]).then_inc(z_loaded[k], 16)
            sp.wait_ge(rows_ready, count + 1)
            sp.dma_start(out[0:full, :].rearrange("(b p) d -> p b d", p=P), x[:, 0:NT - 1, :]).then_inc(stored, 16)
            sp.dma_start(out[full:N, :], x[0:N - full, NT - 1, :]).then_inc(stored, 16)
            sp.wait_ge(stored, 32)


        @block.gpsimd
        def _(pool):
            def passed():
                nc.gpsimd.sem_inc(pool_passed, 1)

            nc.gpsimd.iota(lane[:, :], [[1, P]], base=0, channel_multiplier=0, allow_small_or_imprecise_dtypes=True)
            nc.gpsimd.iota(part[:, :], [[0, 1]], base=0, channel_multiplier=1, allow_small_or_imprecise_dtypes=True)
            nc.gpsimd.iota(tile_no[:, :], [[1, TILES]], base=0, channel_multiplier=0, allow_small_or_imprecise_dtypes=True)
            nc.gpsimd.memset(x[:, NT - 1, :], 0.0)
            nc.gpsimd.memset(blank, 0.0)
            nc.gpsimd.drain()
            nc.gpsimd.memset(blank[:, :, 1:2], -1.0)
            nc.gpsimd.drain().then_inc(constants, 1)
            pool.wait_ge(constants, 1)
            pool.wait_ge(blank_stored, 16)
            pool.wait_ge(slots_ready, 1)
            staged = Steps(index_staged)

            def stage_put(i, k):
                cols = bass.ds(i * (2 * G) + k * G, G)
                nc.gpsimd.tensor_copy(index[k][0:EP, :], slot[:, cols]).then_inc(index_staged, 1)
                nc.gpsimd.tensor_copy(put_rec[k][0:EP, :, :], rec[:, cols, :]).then_inc(index_staged, 1)
                pool.wait_ge(index_staged, staged.add(2))
                passed()
                for g in range(G):
                    nc.gpsimd.indirect_dma_start(
                        out=records, out_offset=bass.IndirectOffsetOnAxis(ap=index[k][0:EP, g:g + 1], axis=0),
                        in_=put_rec[k][0:EP, g, :], in_offset=None).then_inc(put_done[k], 16)

            for k in HALVES:
                stage_put(0, k)
            staged_first = staged.now
            with pool.Fori(1, DEG_ITERS) as i:
                staged.now = i * 4
                for k in HALVES:
                    pool.wait_ge(put_done[k], i * (16 * G))
                    passed()
                    stage_put(i, k)
            staged.now = staged_first * DEG_ITERS

            def gather(i, k, table, rows_of, width):
                nc.gpsimd.tensor_copy(index[k][:, :], rows_of[:, bass.ds((i * 2 + k) * G, G)]).then_inc(index_staged, 1)
                pool.wait_ge(index_staged, staged.add())
                passed()
                for g in range(G):
                    nc.gpsimd.indirect_dma_start(
                        out=ring[k][:, g, 0:width], out_offset=None, in_=table,
                        in_offset=bass.IndirectOffsetOnAxis(ap=index[k][:, g:g + 1], axis=0)).then_inc(gathered[k], 16)

            pool.wait_ge(grouped_ready, 1)
            stores = 0
            for p, kind in enumerate(ORDER):
                before_p = rounds_before(p, LINEAR, MAXIMA, SUMS)
                before_m = rounds_before(p, MAXIMA)
                table, rows_of, width = {LINEAR: (node_rows, src_row, D), MAXIMA: (attention_rows, src_row, ZW),
                                         SUMS: (relation_rows, rel_row, D)}[kind]
                if kind in (LINEAR, MAXIMA):
                    stores += 1
                    pool.wait_ge(rows_stored, 16 * stores)
                if kind == SUMS:
                    for k in HALVES:
                        pool.wait_ge(rel_stored[k], 16 * rel_rounds(rounds_before(p, SUMS) // ITERS, NT - 1 - (NT - 1 + k) % 2))
                        pool.wait_ge(z_stored[k], 16 * before_m)
                for k in HALVES:
                    pool.wait_ge(half_free[k], before_p + 1)
                    gather(0, k, table, rows_of, width)
                base = staged.now - 2
                with pool.Fori(1, ITERS) as i:
                    staged.now = i * 2 + base
                    for k in HALVES:
                        pool.wait_ge(half_free[k], i + (before_p + 1))
                        passed()
                        if kind == MAXIMA:
                            pool.wait_ge(z_stored[k], i * 16 + before_m * 16)
                            passed()
                        gather(i, k, table, rows_of, width)
                staged.now = base + 2 * ITERS

        @block.scalar
        def _(act):
            def passed():
                nc.scalar.sem_inc(act_passed, 1)

            asked = [0]

            def asked_for():
                asked[0] += 1
                act.wait_ge(act_go, asked[0])

            def norm_root():
                asked_for()
                nc.scalar.activation(stat[:, 3, :], stat[:, 2, :], ACT.Sqrt).then_inc(act_done, 1)

            asked_for()
            nc.scalar.activation(stat[:, 4:6, :], stat[:, 6:8, :], ACT.Sqrt).then_inc(act_done, 1)
            with act.Fori(0, ITERS) as i:
                for k in HALVES:
                    cols = bass.ds((i * 2 + k) * (G * P), G * P)
                    act.wait_ge(member_made[k], i + 1)
                    passed()
                    act.dma_start(member_d[:, cols], flat(member[k])).then_inc(member_out[k], 16)
                    act.dma_start(mask_d[:, cols], mask[k]).then_inc(member_out[k], 16)
                for k in HALVES:
                    act.wait_ge(member_out[k], i * 32 + 32)
                    nc.scalar.sem_inc(member_free[k], 1)
            norm_root()
            for p, kind in enumerate(ORDER):
                l = rounds_before(p, MAXIMA) // ITERS
                if kind == MAXIMA:
                    for b in range(NT):
                        k = b % 2
                        act.wait_ge(rel_ps_full[k], rel_rounds(l, b))
                        if rel_rounds(l, b) > 1:
                            act.wait_ge(rel_stored[k], 16 * (rel_rounds(l, b) - 1))
                        nc.scalar.copy(stage[k][:, 0:R * D // 2], ps[:, 2048 * k:2048 * k + R * D // 2]).then_inc(rel_full[0][k], 1)
                    before_m = rounds_before(p, MAXIMA)
                    with act.Fori(0, ITERS) as i:
                        for k in HALVES:
                            act.wait_ge(elT_ps_ready[k], i + (before_m + 1))
                            nc.scalar.copy(elT[k][:, :], elT_ps[k]).then_inc(elT_ready[k], 1)
                if kind == SUMS:
                    before_s = rounds_before(p, SUMS)
                    with act.Fori(0, ITERS) as i:
                        for k in HALVES:
                            act.wait_ge(score_ready[k], i + (before_s + 1))
                            nc.scalar.activation(z_msg[k][:, :, D:ZW], score[k][:, :, :], ACT.Exp).then_inc(exp_ready[k], 1)
                    if l == 1:
                        asked_for()
                        nc.scalar.activation(tmp2[:, :, :], tmp2[:, :, :], ACT.Sigmoid).then_inc(act_done, 1)
                    if l == L:
                        norm_root()
                if kind == LINEAR and p in (0, 2, len(ORDER) - 1):
                    norm_root()

        @block.tensor
        def _(pe):
            asked = [0]

            def asked_for():
                asked[0] += 1
                pe.wait_ge(pe_go, asked[0])

            def transpose_nodes(src):
                asked_for()
                for b in range(NT):
                    last = nc.tensor.transpose(sums3[:, b, :], src[:, b, 0:D], ident[:, :])
                last.then_inc(pe_done, 1)

            def multiply_nodes(*pairs):
                asked_for()
                for b in range(NT):
                    for n, (turned, w) in enumerate(pairs):
                        last = nc.tensor.matmul(sums3[:, b, :], turned[:, b, :], w, start=n == 0, stop=n == len(pairs) - 1)
                last.then_inc(pe_done, 1)

            def clear(width):
                for at in range(0, width, 512):
                    n = min(512, width - at)
                    last = nc.tensor.matmul(ps[:, at:at + n], zeros_b[:, 0:P], zeros_b[:, 0:n], start=True, stop=True)
                return last

            asked_for()
            nc.tensor.matmul(ps[0:EP, 0:NT], below[0:EP, 0:EP], total[0:EP, :], start=True, stop=True)
            nc.tensor.matmul(ps[:, 512:512 + NT], ones[0:EP, :], total[0:EP, :], start=True, stop=True).then_inc(pe_done, 1)
            asked_for()
            for at in (0, 512):
                nc.tensor.matmul(ps[:, at:at + NT], zeros_b[:, 0:P], zeros_b[:, 0:NT], start=True, stop=True)
            with pe.Fori(0, DEG_ITERS) as i:
                for k in HALVES:
                    pe.wait_ge(degree_hot[k], i + 1)
                    for g in range(G):
                        nc.tensor.matmul(ps[:, 0:NT], src_low[k][:, g, :], src_high[k][:, g, :], start=False, stop=True, skip_group_check=True)
                        last = nc.tensor.matmul(ps[:, 512:512 + NT], dst_low[k][:, g, :], dst_high[k][:, g, :], start=False, stop=True, skip_group_check=True)
                    last.then_inc(degree_used[k], 1)
            nc.tensor.matmul(ps[:, 1024:1025], ones[0:EP, :], weight_sum[0:EP, :], start=True, stop=True).then_inc(pe_done, 1)
            asked_for()
            quarter = TILES // 4
            for q in range(4):
                last = nc.tensor.transpose(ps[0:quarter, P * q:P * (q + 1)], local[:, quarter * q:quarter * (q + 1)], ident[:, :])
            last.then_inc(pe_done, 1)
            asked_for()
            nc.tensor.transpose(ps[:, 0:P], wt["L0_gnn_W"][:, :], ident[:, :]).then_inc(pe_done, 1)

            def tile_of(t):
                return pe.value_load(dst_tile_i[0:1, bass.ds(t, 1)], min_val=0, max_val=NT - 1)

            passes = [0]

            def start_pass():
                passes[0] += 1
                pe.wait_ge(pass_go, passes[0])

            transpose_nodes(tmp)
            multiply_nodes((hT, w0T[:, :]))
            for p, kind in enumerate(ORDER):
                before_p = rounds_before(p, LINEAR, MAXIMA, SUMS)
                before_m, before_s = rounds_before(p, MAXIMA), rounds_before(p, SUMS)
                before_hot = rounds_before(p, LINEAR, SUMS)
                l = before_m // ITERS
                if kind == MAXIMA:
                    transpose_nodes(h)
                    pe.wait_ge(layer_loads, 16 * 5 * (l + 1))
                    multiply_nodes((hT, w_gat[:, l, :]))
                    multiply_nodes((hT, w_loop[:, l, :]))
                    asked_for()
                    for b in range(NT):
                        k = b % 2
                        if rel_rounds(l, b) > 1:
                            pe.wait_ge(rel_full[0][k], rel_rounds(l, b) - 1)
                            pe.wait_ge(rel_full[1][k], rel_rounds(l, b) - 1)
                        for q in range(4):
                            last = nc.tensor.matmul(ps[:, 2048 * k + 512 * q:2048 * k + 512 * (q + 1)], hT[:, b, :],
                                                    w_rel[:, 4 * q:4 * (q + 1), :], start=True, stop=True)
                        last.then_inc(rel_ps_full[k], 1)
                start_pass()
                if kind == LINEAR:
                    clear(NPAD)
                    with pe.Fori(0, ITERS) as i:
                        for k in HALVES:
                            pe.wait_ge(gathered[k], i * (16 * G) + (before_p + 1) * 16 * G)
                            pe.wait_ge(onehot_ready[k], i + (before_hot + 1))
                            for g in range(G):
                                b = tile_of((i * 2 + k) * G + g)
                                last = nc.tensor.matmul(sums[:, bass.ds(b * D, D)], onehot[k][:, g, :], ring[k][:, g, 0:D],
                                                        start=False, stop=True, skip_group_check=True)
                            last.then_inc(half_free[k], 1)
                if kind == MAXIMA:
                    with pe.Fori(0, ITERS) as i:
                        for k in HALVES:
                            pe.wait_ge(el_split[k], i + (before_m + 1))
                            nc.tensor.transpose(elT_ps[k], el_parts[k][:, :, :, :].rearrange("p a b c -> p (a b c)"), ident_b[:, :]).then_inc(elT_ps_ready[k], 1)
                            pe.wait_ge(member_in[k], i * 16 + (before_m + before_s + 1) * 16)
                            pe.wait_ge(elT_ready[k], i + (before_m + 1))
                            for g in range(G):
                                pe.wait_ge(el_taken, i * (2 * G) + (before_m * 2 * G + k * G + g + 1))
                                nc.tensor.matmul(el_ps[g % 4], ident_b[:, :], across(member[k][:, g, :], HEADS), start=True, stop=True)
                                for j in range(HEADS):
                                    last = nc.tensor.matmul(el_ps[g % 4][:, j, :], pick[:, g * HEADS + j, :], elT[k][:, :],
                                                            start=False, stop=True, skip_group_check=True)
                                last.then_inc(el_wide, 1)
                if kind == SUMS:
                    with pe.Fori(0, ITERS) as i:
                        for k in HALVES:
                            pe.wait_ge(member_in[k], i * 16 + (before_m + before_s + 1) * 16)
                            pe.wait_ge(er_top_taken[k], i + (before_s + 1))
                            for g in range(G):
                                b = tile_of((i * 2 + k) * G + g)
                                for n in range(3):
                                    last = nc.tensor.matmul(er_top_ps[k][:, g, :], member[k][:, g, :], er_top[:, bass.ds(b, 1), n, :],
                                                            start=n == 0, stop=n == 2)
                            last.then_inc(er_top_ready[k], 1)
                            pe.wait_ge(gathered[k], i * (16 * G) + (before_p + 1) * 16 * G)
                            pe.wait_ge(onehot_ready[k], i + (before_hot + 1))
                            pe.wait_ge(msg_ready[k], i + (before_s + 1))
                            for g in range(G):
                                pe.wait_ge(z_added, i * (2 * G) + (before_s * 2 * G + k * G + g + 1))
                                slot_ps = msg_ps[g % MSG_SLOTS]
                                nc.tensor.matmul(slot_ps[:, 0:D], onehot[k][:, g, :], ring[k][:, g, 0:D], start=True, stop=True)
                                last = nc.tensor.matmul(slot_ps[:, D:D + ZW], onehot[k][:, g, :], z_msg[k][:, g, :], start=True, stop=True)
                                last.then_inc(z_sum, 1)
                    transpose_nodes(self_term)
                    transpose_nodes(gat)
                    multiply_nodes((hT, w_fuse[:, 0, :]), (tmp, w_fuse[:, 1, :]))
                    if l == 1:
                        transpose_nodes(tmp)
                        multiply_nodes((hT, w_gate[:, :]))
                if kind == LINEAR and p > 2:
                    transpose_nodes(tmp)
                    multiply_nodes((hT, wt[f"L3_gnn_W{p - len(ORDER) + 3}"][:, :]))

        @block.vector
        def _(dve_):
            v = nc.vector
            steps = Steps(dve)

            def link(ins):
                ins.then_inc(dve, 1)
                dve_.wait_ge(dve, steps.add())

            def tell(s, k=1):
                v.sem_inc(s, k)

            asked = {"pe": 0, "act": 0}

            def ask_pe():
                tell(pe_go)
                asked["pe"] += 1
                dve_.wait_ge(pe_done, asked["pe"])

            def ask_act():
                tell(act_go)
                asked["act"] += 1
                dve_.wait_ge(act_done, asked["act"])

            for k in HALVES:
                for s in (half_free, wide_used, degree_used, member_free, er_top_taken):
                    v.sem_inc(s[k], 1)
            v.sem_inc(el_taken, 4)
            v.sem_inc(z_added, MSG_SLOTS)

            dve_.wait_ge(constants, 1)
            tell(blank_ready)
            v.memset(zeros_b[:, :], 0.0)
            v.memset(ones[:, :], 1.0)
            v.tensor_scalar(ident[:, :], lane[:, :], part[:, :], None, ALU.is_equal)
            v.tensor_scalar(ident_b[:, :], lane[:, :], part[:, :], None, ALU.is_equal)
            v.tensor_scalar(below[:, :], lane[:, :], part[:, :], None, ALU.is_gt)
            K = 3 * G * HEADS
            kmod = stat[0:K, 0, 0:1]
            link(v.tensor_scalar(kmod, part[0:K, :], float(G * HEADS), float(-G * HEADS), ALU.is_ge, ALU.mult))
            link(v.tensor_tensor(kmod, kmod, part[0:K, :], ALU.add))
            link(v.tensor_scalar(stat[0:K, 1, 0:1], part[0:K, :], float(2 * G * HEADS), float(-G * HEADS), ALU.is_ge, ALU.mult))
            link(v.tensor_tensor(kmod, kmod, stat[0:K, 1, 0:1], ALU.add))
            link(v.tensor_scalar(pick[:, :, :], spread(lane[0:K, 0:G * HEADS], P), kmod, None, ALU.is_equal))

            dve_.wait_ge(loads, 64)
            v.tensor_copy(rec[:, :, 0], src_i)
            v.tensor_copy(rec[:, :, 1], dst_i)
            v.tensor_copy(rec[:, :, 2], typ_i)
            v.tensor_copy(rec[:, :, 3], w_in)
            v.tensor_scalar(dtile_i, dst_i, 7, None, ALU.logical_shift_right)
            v.tensor_scalar(tmp_i, src_i, 7, None, ALU.logical_shift_right)
            v.memset(pos, 0.0)
            link(v.tensor_reduce(weight_sum[0:EP, :], w_in, AX.X, ALU.add))
            v.tensor_copy(dtile, dtile_i)
            link(v.tensor_copy(stile, tmp_i))
            v.scalar_tensor_tensor(dlow, dtile, -float(P), rec[:, :, 1], ALU.mult, ALU.add)
            link(v.scalar_tensor_tensor(slow, stile, -float(P), rec[:, :, 0], ALU.mult, ALU.add))
            for b in steps.rounds(dve_, NT, 5):
                link(v.tensor_scalar(hit, dtile, tile_no[0:EP, bass.ds(b, 1)], None, ALU.is_equal))
                link(v.tensor_tensor_scan(run, ones[0:EP, 0:1].to_broadcast([EP, EC]), hit, 0.0, ALU.mult, ALU.add))
                link(v.tensor_scalar(total[0:EP, bass.ds(b, 1)], run[:, EC - 1:EC], 1.0, None, ALU.mult))
                link(v.tensor_tensor(hit, hit, run, ALU.mult))
                link(v.tensor_tensor(pos, pos, hit, ALU.add))
            ask_pe()
            link(v.tensor_scalar(tiles_i[:, :], ps[:, 512:512 + NT], float(P - 1), None, ALU.add))
            link(v.tensor_scalar(tiles_i[:, :], tiles_i[:, :], 7, None, ALU.logical_shift_right))
            link(v.tensor_copy(tiles[:, :], tiles_i[:, :]))
            link(v.tensor_tensor_scan(first_tile[:, :], ones[:, 0:1].to_broadcast([P, NT]), tiles[:, :], 0.0, ALU.mult, ALU.add))
            link(v.tensor_tensor(first_tile[:, :], first_tile[:, :], tiles[:, :], ALU.subtract))
            link(v.scalar_tensor_tensor(before[0:EP, :], first_tile[0:EP, :], float(P), ps[0:EP, 0:NT], ALU.mult, ALU.add))
            link(v.tensor_scalar(before[0:EP, :], before[0:EP, :], -1.0, None, ALU.add))
            for b in steps.rounds(dve_, NT, 2):
                cols = bass.ds(b, 1)
                link(v.tensor_scalar(hit, dtile, tile_no[0:EP, cols], before[0:EP, cols], ALU.is_equal, ALU.mult))
                link(v.tensor_tensor(pos, pos, hit, ALU.add))
            link(v.tensor_copy(slot_i, pos))
            v.tensor_scalar(hi_i, slot_i, 7, None, ALU.logical_shift_right)
            link(v.tensor_scalar(tmp_i, slot_i, P - 1, None, ALU.bitwise_and))
            link(v.scalar_tensor_tensor(slot, tmp_i, float(TILES), hi_i, ALU.mult, ALU.add))
            tell(slots_ready)
            link(v.memset(dst_tile[:, :], 0.0))
            for b in steps.rounds(dve_, NT - 1, 1):
                link(v.scalar_tensor_tensor(dst_tile[:, :], tile_no[:, :], first_tile[:, bass.ds(b + 1, 1)], dst_tile[:, :], ALU.is_ge, ALU.add))
            link(v.tensor_copy(dst_tile_i[:, :], dst_tile[:, :]))
            tell(pe_go)
            asked["pe"] += 1
            for i in steps.rounds(dve_, DEG_ITERS, 2):
                for k in HALVES:
                    cols = bass.ds((i * 2 + k) * G, G)
                    dve_.wait_ge(degree_used[k], i + 1)
                    v.tensor_tensor(src_low[k], spread(slow[:, cols], P), across(lane[0:EP, :], G), ALU.is_equal)
                    v.tensor_tensor(dst_low[k], spread(dlow[:, cols], P), across(lane[0:EP, :], G), ALU.is_equal)
                    v.tensor_tensor(src_high[k], spread(stile[:, cols], NT), across(lane[0:EP, 0:NT], G), ALU.is_equal)
                    link(v.tensor_tensor(dst_high[k], spread(dtile[:, cols], NT), across(lane[0:EP, 0:NT], G), ALU.is_equal))
                    tell(degree_hot[k])
            dve_.wait_ge(pe_done, asked["pe"])
            v.tensor_scalar(stat[:, 6, :], ps[:, 0:NT], 1.0, None, ALU.max)
            v.tensor_scalar(stat[:, 7, :], ps[:, 512:512 + NT], 1.0, None, ALU.max)
            v.tensor_scalar(in_norm0[:, :], ps[:, 512:512 + NT], 0.0, None, ALU.is_gt)
            link(v.tensor_scalar(weight_mean[:, :], ps[:, 1024:1025], 1.0 / E, None, ALU.mult))
            ask_act()
            v.reciprocal(out_norm[:, :], stat[:, 4, :])
            link(v.reciprocal(in_norm[:, :], stat[:, 5, :]))
            link(v.tensor_tensor(in_norm0[:, :], in_norm0[:, :], in_norm[:, :], ALU.mult))

            dve_.wait_ge(grouped_loaded, 16)
            v.scalar_tensor_tensor(local[:, :], dst_tile[:, :], -float(P), grouped[:, :, 1], ALU.mult, ALU.add)
            v.tensor_copy(src_row[:, :], grouped[:, :, 0])
            v.scalar_tensor_tensor(rel_row[:, :], grouped[:, :, 0], float(R), grouped[:, :, 2], ALU.mult, ALU.add)
            link(v.tensor_copy(weight[:, :], grouped[:, :, 3]))
            tell(grouped_ready)
            ask_pe()
            link(v.tensor_copy(local_T, ps[0:TILES // 4, 0:4 * P].rearrange("p (k e) -> p k e", k=4)))
            tell(local_ready)
            for i in steps.rounds(dve_, ITERS, 4):
                for k in HALVES:
                    dve_.wait_ge(wide_in[k], i * 16 + 16)
                    v.sem_inc(dve_passed, 1)
                    dve_.wait_ge(member_free[k], i + 1)
                    link(v.tensor_scalar(flat(member[k]), wide[k], part[:, :], None, ALU.is_equal))
                    tell(wide_used[k])
                    link(v.tensor_scalar(mask[k], flat(member[k]), -1.0, BIG, ALU.add, ALU.mult))
                    tell(member_made[k])

            dve_.wait_ge(late_loads, LATE_LOADS * 16)
            ask_pe()
            link(v.tensor_copy(w0T[:, :], ps[:, 0:P]))
            link(v.scalar_tensor_tensor(gate_row[:, :], gate_row[:, :], weight_mean[:, :], row["L2_gnn_b_gate"][:, :], ALU.mult, ALU.add))

            def layer_norm(src, to):
                link(v.tensor_reduce(stat[:, 0, :], src[:, :, :], AX.X, ALU.add))
                link(v.tensor_scalar(stat[:, 0, :], stat[:, 0, :], 1.0 / D, None, ALU.mult))
                link(v.tensor_tensor(src[:, :, :], src[:, :, :], spread(stat[:, 0, :], D), ALU.subtract))
                link(v.tensor_tensor(to[:, :, :], src[:, :, :], src[:, :, :], ALU.mult))
                link(v.tensor_reduce(stat[:, 1, :], to[:, :, :], AX.X, ALU.add))
                link(v.tensor_scalar(stat[:, 2, :], stat[:, 1, :], 1.0 / D, LN_EPS, ALU.mult, ALU.add))
                ask_act()
                link(v.reciprocal(stat[:, 1, :], stat[:, 3, :]))
                link(v.tensor_tensor(to[:, :, :], src[:, :, :], spread(stat[:, 1, :], D), ALU.mult))

            def scaled(to, src, norm):
                link(v.tensor_tensor(to[:, :, :], src, spread(norm[:, :], D), ALU.mult))

            def plus_row(to, src, r, op=ALU.add):
                link(v.tensor_tensor(to[:, :, :], src, across(r[:, :], NT), op))

            def add(to, one, other):
                link(v.tensor_tensor(to[:, :, :], one[:, :, :], other[:, :, :], ALU.add))

            def split(parts, src, rest):
                link(v.tensor_copy(parts[0], src))
                link(v.tensor_tensor(rest, src, parts[0], ALU.subtract))
                link(v.tensor_copy(parts[1], rest))
                link(v.tensor_tensor(rest, rest, parts[1], ALU.subtract))
                link(v.tensor_copy(parts[2], rest))

            def tile_of(t):
                return dve_.value_load(dst_tile_i[0:1, bass.ds(t, 1)], min_val=0, max_val=NT - 1)

            def make_onehot(i, k, p, before_hot, before_p, weighted):
                dve_.wait_ge(half_free[k], i + (before_p + 1))
                v.sem_inc(dve_passed, 1)
                cols = bass.ds((i * 2 + k) * G, G)
                link(v.tensor_tensor(onehot[k][:, :, :], spread(local[:, cols], P), across(lane[:, :], G), ALU.is_equal))
                if weighted:
                    link(v.tensor_tensor(onehot[k][:, :, :], onehot[k][:, :, :], spread(weight[:, cols], P), ALU.mult))
                tell(onehot_ready[k])

            def end_pass(p):
                for k in HALVES:
                    dve_.wait_ge(half_free[k], rounds_before(p + 1, LINEAR, MAXIMA, SUMS) + 1)

            def edge_sums(p):
                tell(rows_ready)
                tell(pass_go)
                n = 4 if WEIGHTED[p] else 2
                for i in steps.rounds(dve_, ITERS, n):
                    for k in HALVES:
                        make_onehot(i, k, p, rounds_before(p, LINEAR, SUMS), rounds_before(p, LINEAR, MAXIMA, SUMS), WEIGHTED[p])
                end_pass(p)

            def turn(src_to):
                ask_pe()
                link(v.tensor_copy(src_to[:, :, :], sums3))

            link(v.tensor_copy(tmp2[:, :, :], x[:, :, :]))
            layer_norm(tmp2, tmp)
            plus_row(tmp, tmp[:, :, :], row["L0_gnn_ln_gamma"], ALU.mult)
            plus_row(tmp, tmp[:, :, :], row["L0_gnn_ln_beta"])
            turn(hT)
            ask_pe()
            plus_row(tmp, sums3, row["L0_gnn_b"])
            edge_sums(0)
            link(v.scalar_tensor_tensor(flat(tmp2), sums, 0.0, flat(x), ALU.max, ALU.add))
            add(tmp2, tmp2, x)
            layer_norm(tmp2, x)

            scaled(tmp, x[:, :, :], in_norm0)
            edge_sums(1)
            scaled(h, sums3, in_norm0)
            scaled(tmp, h[:, :, :], in_norm0)
            add(self_term, x, h)
            edge_sums(2)
            scaled(tmp2, sums3, in_norm0)
            add(tmp2, tmp2, self_term)
            link(v.scalar_tensor_tensor(flat(tmp2), flat(tmp2), 1.0 / 3, flat(x), ALU.mult, ALU.add))
            layer_norm(tmp2, x)
            link(v.tensor_copy(h[:, :, :], x[:, :, :]))

            for l in range(L):
                p = 3 + 2 * l
                before_p, before_m, before_s = rounds_before(p, LINEAR, MAXIMA, SUMS), l * ITERS, l * ITERS
                tell(layer_free)
                turn(hT)
                ask_pe()
                dve_.wait_ge(layer_loads, 16 * 5 * (l + 1))
                link(v.tensor_copy(gat[:, :, 0:D], sums3))
                by_head = tmp[:, :, :].rearrange("p b (h d) -> p b h d", h=HEADS)
                for w, to in ((attn_l, gat[:, :, D:ZW]), (attn_r, er[:, :, :])):
                    plus_row(tmp, gat[:, :, 0:D], w, ALU.mult)
                    link(v.tensor_reduce(to, by_head, AX.X, ALU.add))
                tell(rows_ready)
                ask_pe()
                plus_row(self_term, sums3, b_rel)
                link(v.memset(top[:, :, :], -BIG))
                tell(pe_go)
                half = R * D // 2
                for b in range(NT):
                    k = b % 2
                    dve_.wait_ge(rel_ps_full[k], rel_rounds(l, b))
                    if rel_rounds(l, b) > 1:
                        dve_.wait_ge(rel_stored[k], 16 * (rel_rounds(l, b) - 1))
                    v.tensor_copy(stage[k][:, half:2 * half], ps[:, 2048 * k + half:2048 * k + 2 * half]).then_inc(rel_full[1][k], 1)
                for k in HALVES:
                    for e in range(2):
                        dve_.wait_ge(rel_full[e][k], rel_rounds(l, NT - 1 - (NT - 1 + k) % 2))
                tell(pass_go)
                for i in steps.rounds(dve_, ITERS, 2 * (5 + 2 * G)):
                    for k in HALVES:
                        dve_.wait_ge(gathered[k], i * (16 * G) + (before_p + 1) * 16 * G)
                        v.sem_inc(dve_passed, 1)
                        dve_.wait_ge(half_free[k], i + (before_p + 1))
                        v.sem_inc(dve_passed, 1)
                        split([el_parts[k][:, n, :, :] for n in range(3)], ring[k][:, :, D:ZW], score[k][:, :, :])
                        tell(el_split[k])
                        for g in range(G):
                            b = tile_of((i * 2 + k) * G + g)
                            dve_.wait_ge(el_wide, i * (2 * G) + (before_m * 2 * G + k * G + g + 1))
                            link(v.tensor_reduce(top_tile[:, :], el_ps[g % 4], AX.X, ALU.max))
                            tell(el_taken)
                            at = top[:, :, :].rearrange("p b h -> p (b h)")[:, bass.ds(b * HEADS, HEADS)]
                            link(v.tensor_tensor(at, at, top_tile[:, :], ALU.max))
                        tell(half_free[k])
                end_pass(p)
                link(v.tensor_tensor(top[:, :, :], top[:, :, :], er[:, :, :], ALU.add))
                link(v.scalar_tensor_tensor(top[:, :, :], top[:, :, :], 0.2, top[:, :, :], ALU.mult, ALU.max))
                split([er_top[:, :, n, 0:HEADS] for n in range(3)], er[:, :, :], sc[:, :, :])
                split([er_top[:, :, n, HEADS:2 * HEADS] for n in range(3)], top[:, :, :], sc[:, :, :])
                link(v.memset(agg_flat, 0.0))
                p += 1
                before_p, before_hot = rounds_before(p, LINEAR, MAXIMA, SUMS), rounds_before(p, LINEAR, SUMS)
                tell(pass_go)
                for i in steps.rounds(dve_, ITERS, 2 * (1 + 4 + 1 + G)):
                    for k in HALVES:
                        make_onehot(i, k, p, before_hot, before_p, False)
                        dve_.wait_ge(z_loaded[k], i * 16 + (before_s + 1) * 16)
                        v.sem_inc(dve_passed, 1)
                        dve_.wait_ge(er_top_ready[k], i + (before_s + 1))
                        e = score[k][:, :, :]
                        link(v.tensor_tensor(e, z_in[k][:, :, D:ZW], er_top_ps[k][:, :, 0:HEADS], ALU.add))
                        link(v.scalar_tensor_tensor(e, e, 0.2, e, ALU.mult, ALU.max))
                        link(v.tensor_tensor(e, e, er_top_ps[k][:, :, HEADS:2 * HEADS], ALU.subtract))
                        tell(er_top_taken[k])
                        link(v.tensor_scalar(e, e, 0.0, None, ALU.min))
                        tell(score_ready[k])
                        dve_.wait_ge(exp_ready[k], i + (before_s + 1))
                        link(v.tensor_tensor(z_msg[k][:, :, 0:D].rearrange("p g (h d) -> p g h d", h=HEADS),
                                             z_in[k][:, :, 0:D].rearrange("p g (h d) -> p g h d", h=HEADS),
                                             spread(z_msg[k][:, :, D:ZW], DH), ALU.mult))
                        tell(msg_ready[k])
                        for g in range(G):
                            b = tile_of((i * 2 + k) * G + g)
                            dve_.wait_ge(z_sum, i * (2 * G) + (before_s * 2 * G + k * G + g + 1))
                            at = agg_flat[:, bass.ds(b * (D + ZW), D + ZW)]
                            link(v.tensor_tensor(at, at, msg_ps[g % MSG_SLOTS], ALU.add))
                            tell(z_added)
                        tell(half_free[k])
                end_pass(p)
                link(v.tensor_scalar(sc[:, :, :], agg[:, :, 2 * D:D + ZW], 1e-30, None, ALU.max))
                link(v.reciprocal(sc[:, :, :], sc[:, :, :]))
                link(v.tensor_tensor(gat[:, :, 0:D].rearrange("p b (h d) -> p b h d", h=HEADS),
                                     agg[:, :, D:2 * D].rearrange("p b (h d) -> p b h d", h=HEADS), spread(sc[:, :, :], DH), ALU.mult))
                link(v.tensor_tensor(gat[:, :, 0:D], gat[:, :, 0:D], across(b_gat[:, :], NT), ALU.add))
                link(v.tensor_tensor(self_term[:, :, :], agg[:, :, 0:D], self_term[:, :, :], ALU.add))
                turn(hT)
                turn(tmp)
                ask_pe()
                plus_row(tmp, sums3, row["L2_gnn_b_fuse"])
                if l == 0:
                    turn(hT)
                    ask_pe()
                    plus_row(tmp2, sums3, gate_row)
                    ask_act()
                    link(v.tensor_tensor(tmp[:, :, :], tmp[:, :, :], tmp2[:, :, :], ALU.mult))
                link(v.tensor_scalar(h[:, :, :], tmp[:, :, :], 0.0, None, ALU.max))
            add(tmp2, x, h)
            layer_norm(tmp2, x)

            link(v.tensor_copy(h[:, :, :], x[:, :, :]))
            for c in range(2):
                scaled(tmp, h[:, :, :], out_norm)
                edge_sums(3 + 2 * L + c)
                scaled(tmp, sums3, in_norm)
                turn(hT)
                ask_pe()
                plus_row(tmp, sums3, row[f"L3_gnn_b{c + 1}"])
                link(v.scalar_tensor_tensor(flat(h), flat(tmp), 0.0, flat(h), ALU.max, ALU.add))
            add(tmp2, x, h)
            layer_norm(tmp2, x)
            tell(rows_ready)


_INS = ["x", "src", "dst", "edge_type_16", "edge_weight", "L0_gnn_ln_gamma", "L0_gnn_ln_beta", "L0_gnn_W", "L0_gnn_b",
        "L2_gnn_W_rel", "L2_gnn_b_rel", "L2_gnn_W_loop", "L2_gnn_W_gat", "L2_gnn_attn_l", "L2_gnn_attn_r",
        "L2_gnn_b_gat", "L2_gnn_W_fuse", "L2_gnn_b_fuse", "L2_gnn_W_gate", "L2_gnn_b_gate", "L3_gnn_W1", "L3_gnn_b1",
        "L3_gnn_W2", "L3_gnn_b2"]


def kernel(**inputs):
    import numpy as _np
    import concourse.bacc as _bacc
    from concourse import mybir as _mybir
    from concourse.bass_utils import run_bass_kernel_spmd as _run

    nc = _bacc.Bacc("TRN2", target_bir_lowering=False, num_devices=1)
    arrays, args = {}, {}
    for name in _INS:
        a = _np.ascontiguousarray(inputs[name])
        arrays[f"in_{name}"] = a
        args[name] = nc.dram_tensor(f"in_{name}", a.shape, _mybir.dt.from_np(a.dtype), kind="ExternalInput").ap()
    out = nc.dram_tensor("out_0", (N, D), _mybir.dt.float32, kind="ExternalOutput").ap()
    gnn_stack(nc, args, out)
    r = _run(nc, [arrays], core_ids=[0])
    return r.results[0]["out_0"]
```

```python
import concourse.bass as bass
from concourse import mybir
from contextlib import ExitStack

N, D, E, R, L, HEADS = 3125, 128, 50000, 16, 3, 4
P = 128
DH = D // HEADS
NT = -(-N // P)
NPAD = NT * P
EP = 125
EC = E // EP
G = 8
RING = 4
TILES = -(-((E + NT * (P - 1)) // P) // (RING * G)) * RING * G
ROUNDS = TILES // (RING * G)
MSG_SLOTS = 4
PAIRS = 2
DEG_ITERS = EC // (2 * G)
ZW = D + HEADS
BIG = float(2.0 ** 100)
LN_EPS = 1e-5


class Steps:

    def __init__(self, sem):
        self.sem, self.now, self.made = sem, 0, 0

    def add(self, k=1):
        self.now, self.made = self.now + k, self.made + k
        return self.now

    def rounds(self, eng, count, each):
        start = self.now
        with eng.Fori(0, count) as i:
            self.now, self.made = i * each + start, 0
            yield i
            assert self.made == each, (self.made, each)
        self.now = start + count * each


def gnn_stack(nc, a, out):
    f32, bf16, i32, u32 = mybir.dt.float32, mybir.dt.bfloat16, mybir.dt.int32, mybir.dt.uint32
    ALU, ACT, AX = mybir.AluOpType, mybir.ActivationFunctionType, mybir.AxisListType

    def dram(name, shape, dt):
        return nc.dram_tensor(name, shape, dt, kind="Internal").ap()

    records = dram("records", [P * TILES, 4], f32)
    node_rows = dram("node_rows", [NPAD, D], f32)
    attention_rows = dram("attention_rows", [NPAD, ZW], f32)
    relation_rows = dram("relation_rows", [2 * ROUNDS * P * R, D], f32)
    edge_z = dram("edge_z", [P, TILES * ZW], f32)
    local_rows = dram("local_rows", [TILES * P], f32)
    member_d = dram("member_d", [P, TILES * P], bf16)
    mask_d = dram("mask_d", [P, TILES * P], bf16)

    with ExitStack() as ctx:
        def sb(name, shape, dt=f32):
            return ctx.enter_context(nc.sbuf_tensor(name, shape, dt))

        def sem(name):
            return ctx.enter_context(nc.semaphore(name))

        def pair(name):
            return [sem(name + "_even"), sem(name + "_odd")]

        lane = sb("lane", [P, P])
        part = sb("part", [P, 1])
        ident = sb("ident", [P, P])
        ident_b = sb("ident_b", [P, P], bf16)
        below = sb("below", [P, P])
        ones = sb("ones", [P, P])
        zeros_b = sb("zeros_b", [P, 4 * P], bf16)
        tile_no = sb("tile_no", [P, TILES])
        assert 2 * ROUNDS >= NT
        pick = sb("pick", [3 * G * HEADS, G * HEADS, P], bf16)
        x = sb("x", [P, NT, D])
        h = sb("h", [P, NT, D])
        agg = sb("agg", [P, NT, D + ZW])
        agg_flat = agg[:, :, :].rearrange("p b c -> p (b c)")
        tmp = agg_flat[:, 0:NPAD].rearrange("p (b d) -> p b d", d=D)
        tmp2 = agg_flat[:, NPAD:2 * NPAD].rearrange("p (b d) -> p b d", d=D)
        self_term = sb("self_term", [P, NT, D])
        hT = sb("hT", [P, 2 * ROUNDS, D])
        hT_tile = [sb(f"hT_tile{k}", [P, D]) for k in range(2)]
        gat = sb("gat", [P, NT, ZW])
        local = sb("local", [P, TILES])
        minus_local = sb("minus_local", [P, TILES])
        weight = sb("weight", [P, TILES])
        src_row = sb("src_row", [P, TILES + G], u32)
        rel_row = sb("rel_row", [P, TILES + G], u32)
        dst_tile = sb("dst_tile", [P, TILES])
        at_sums = sb("at_sums", [P, TILES], i32)
        at_er_top = sb("at_er_top", [P, TILES], i32)
        at_agg = sb("at_agg", [P, TILES], i32)
        ring = [sb(f"ring{j}", [P, G, ZW]) for j in range(RING)]
        index = [sb(f"index{j}", [P, G], u32) for j in range(RING)]
        onehot = [sb(f"onehot{k}", [P, G, P]) for k in range(2)]
        work = [sb(f"work{k}", [P, 2 * G * ZW]) for k in range(2)]
        z_in = [w[:, 0:G * ZW].rearrange("p (g c) -> p g c", c=ZW) for w in work]
        z_msg = [w[:, G * ZW:2 * G * ZW].rearrange("p (g c) -> p g c", c=ZW) for w in work]
        stage = [w[:, 0:R * D] for w in work]
        member = [sb(f"member{k}", [P, G, P], bf16) for k in range(2)]
        score = [sb(f"score{k}", [P, G, HEADS]) for k in range(2)]
        el_parts = [sb(f"el_parts{k}", [P, 3, G, HEADS], bf16) for k in range(2)]
        elT = [sb(f"elT{k}", [3 * G * HEADS, P], bf16) for k in range(2)]
        stat = sb("stat", [P, 8, NT])
        er = sb("er", [P, NT, HEADS])
        el = sb("el", [P, NT, HEADS])
        top = sb("top", [P, NT, HEADS])
        tile_top = sb("tile_top", [P, TILES, HEADS])
        run_top = agg_flat[:, 0:TILES * HEADS].rearrange("p (t h) -> p t h", h=HEADS)
        new_tile = sb("new_tile", [P, TILES])
        last_tile_i = sb("last_tile_i", [P, NT], i32)
        er_top = sb("er_top", [P, NT, 3, 2 * HEADS], bf16)
        er_top_flat = er_top[:, :, :, :].rearrange("p b n c -> p (b n c)")
        sc = sb("sc", [P, NT, HEADS])
        in_norm = sb("in_norm", [P, NT])
        in_norm0 = sb("in_norm0", [P, NT])
        out_norm = sb("out_norm", [P, NT])
        w_names = ["L0_gnn_W", "L3_gnn_W1", "L3_gnn_W2"]
        wt = {n: sb("s_" + n, [D, D]) for n in w_names}
        w0T = sb("w0T", [D, D])
        w_rel = sb("w_rel", [D, R, D])
        w_loop = sb("w_loop", [D, L, D])
        w_gat = sb("w_gat", [D, L, D])
        w_fuse = sb("w_fuse", [D, 2, D])
        w_gate = sb("w_gate", [D, D])
        LATE_LOADS = 2 + 3 + 7 + 5
        rows = ["L0_gnn_ln_gamma", "L0_gnn_ln_beta", "L0_gnn_b", "L2_gnn_b_fuse", "L2_gnn_b_gate",
                "L3_gnn_b1", "L3_gnn_b2"]
        row = {n: sb("r_" + n, [P, D]) for n in rows}
        gate_row = sb("gate_row", [P, D])
        b_rel = sb("b_rel", [P, D])
        b_gat = sb("b_gat", [P, D])
        attn_l = sb("attn_l", [P, D])
        attn_r = sb("attn_r", [P, D])
        weight_sum = sb("weight_sum", [P, 1])
        weight_mean = sb("weight_mean", [P, 1])

        def flat(t):
            return t[:, :, :].rearrange("p a b -> p (a b)")

        raw = agg_flat[:, 0:NPAD]
        src_i = raw[0:EP, 0:EC].bitcast(i32)
        dst_i = raw[0:EP, EC:2 * EC].bitcast(i32)
        typ_i = raw[0:EP, 2 * EC:3 * EC].bitcast(i32)
        w_in = raw[0:EP, 3 * EC:4 * EC]
        dtile_i = raw[0:EP, 4 * EC:5 * EC].bitcast(i32)
        dtile = raw[0:EP, 5 * EC:6 * EC]
        stile = raw[0:EP, 6 * EC:7 * EC]
        slow = raw[0:EP, 7 * EC:8 * EC]
        raw2 = agg_flat[:, NPAD:2 * NPAD]
        dlow = raw2[0:EP, 0:EC]
        hit = raw2[0:EP, EC:2 * EC]
        run = raw2[0:EP, 2 * EC:3 * EC]
        pos = raw2[0:EP, 3 * EC:4 * EC]
        slot_i = raw2[0:EP, 4 * EC:5 * EC].bitcast(i32)
        hi_i = raw2[0:EP, 5 * EC:6 * EC].bitcast(i32)
        slot = flat(gat)[0:EP, 4 * EC:5 * EC].bitcast(u32)
        tmp_i = raw2[0:EP, 7 * EC:8 * EC].bitcast(i32)
        rec = flat(gat)[0:EP, 0:4 * EC].rearrange("p (c f) -> p c f", f=4)
        blank = flat(self_term)[:, 0:4 * TILES].rearrange("p (c f) -> p c f", f=4)
        grouped = flat(h)[:, 0:4 * TILES].rearrange("p (c f) -> p c f", f=4)
        local_T = flat(gat)[0:TILES // 4, 0:4 * P].rearrange("p (k e) -> p k e", k=4)
        put_rec = [sb(f"put_rec{k}", [P, G, 4]) for k in range(2)]
        src_low = [flat(onehot[k]).bitcast(bf16)[0:EP, 0:G * P].rearrange("p (g n) -> p g n", g=G)
                   for k in range(2)]
        dst_low = [flat(onehot[k]).bitcast(bf16)[0:EP, G * P:2 * G * P].rearrange("p (g n) -> p g n", g=G)
                   for k in range(2)]
        src_high = [flat(z_in[k]).bitcast(bf16)[0:EP, 0:G * NT].rearrange("p (g n) -> p g n", g=G)
                    for k in range(2)]
        dst_high = [flat(z_in[k]).bitcast(bf16)[0:EP, G * NT:2 * G * NT].rearrange("p (g n) -> p g n", g=G)
                    for k in range(2)]
        mask = [w[:, G * P:2 * G * P].bitcast(bf16)[:, 0:G * P] for w in work]
        total = sb("total", [P, NT])
        tiles_i = sb("tiles_i", [P, NT], i32)
        tiles = sb("tiles", [P, NT])
        first_tile = sb("first_tile", [P, NT])
        before = sb("before", [P, NT])
        wide = [w[:, 0:G * P] for w in work]

        ps = ctx.enter_context(nc.psum_tensor("ps", [P, 4096], f32))
        sums = ps[:, 0:NPAD]
        sums3 = sums.rearrange("p (b d) -> p b d", d=D)
        er_top_ps = [ps[:, 3072 + 512 * k:3072 + 512 * k + 2 * G * HEADS]
                     .rearrange("p (g c) -> p g c", c=2 * HEADS) for k in range(2)]
        msg_ps = [ps[:, 512 * k:512 * k + D + ZW] for k in range(MSG_SLOTS)]
        el_ps = [ps[:, 1024 * s:1024 * (s + 1)].rearrange("p (g h e) -> p g h e", g=2, h=HEADS) for s in range(PAIRS)]
        elT_ps = [ps[0:3 * G * HEADS, 2048 + 256 * k:2048 + 256 * k + P // 2].bitcast(bf16) for k in range(2)]
        rel_ps = ps[:, 3072:4096]

        loads = sem("loads")
        late_loads = sem("late_loads")
        constants = sem("constants")
        blank_ready = sem("blank_ready")
        blank_stored = sem("blank_stored")
        slots_ready = sem("slots_ready")
        put_staged = sem("put_staged")
        put_done = pair("put_done")
        grouped_loaded = sem("grouped_loaded")
        degree_hot = pair("degree_hot")
        degree_used = pair("degree_used")
        pe_go = sem("pe_go")
        pe_done = sem("pe_done")
        act_go = sem("act_go")
        act_done = sem("act_done")
        dve = sem("dve")
        local_ready = sem("local_ready")
        local_stored = sem("local_stored")
        wide_in = pair("wide_in")
        wide_used = pair("wide_used")
        member_made = pair("member_made")
        member_free = pair("member_free")
        member_out = pair("member_out")
        gathered = [sem(f"gathered{j}") for j in range(RING)]
        group_done = [sem(f"group_done{j}") for j in range(RING)]
        index_staged = sem("index_staged")
        onehot_ready = pair("onehot_ready")
        pass_go = sem("pass_go")
        rows_ready = sem("rows_ready")
        rows_stored = sem("rows_stored")
        hT_staged = sem("hT_staged")
        rel_ps_full = sem("rel_ps_full")
        rel_taken = sem("rel_taken")
        rel_stored = pair("rel_stored")
        member_in = pair("member_in")
        z_stored = [sem(f"z_stored{j}") for j in range(RING)]
        z_loaded = pair("z_loaded")
        el_split = pair("el_split")
        elT_ps_ready = pair("elT_ps_ready")
        elT_ready = pair("elT_ready")
        el_wide = sem("el_wide")
        el_taken = sem("el_taken")
        er_top_ready = pair("er_top_ready")
        er_top_taken = pair("er_top_taken")
        score_ready = pair("score_ready")
        exp_ready = pair("exp_ready")
        msg_ready = pair("msg_ready")
        z_sum = sem("z_sum")
        z_added = sem("z_added")
        pool_passed = sem("pool_passed")
        layer_loads = sem("layer_loads")
        layer_free = sem("layer_free")
        stored = sem("stored")
        grouped_ready = sem("grouped_ready")
        act_passed = sem("act_passed")
        squared = sem("squared")
        dve_passed = sem("dve_passed")

        block = ctx.enter_context(nc.Block())

        def spread(ap, n):
            return ap.unsqueeze(len(ap.shape)).to_broadcast([*ap.shape, n])

        def across(row_ap, n):
            return row_ap.unsqueeze(1).to_broadcast([row_ap.shape[0], n, row_ap.shape[1]])

        HALVES = range(2)
        def destinations(engine, columns, width, i, j):
            _, found = nc.values_load_multi_w_load_instructions(
                columns[0:1, bass.ds((i * RING + j) * G, G)], engines=[engine], min_val=0, max_val=width * (NT - 1),
                skip_runtime_bounds_check_because="a count of at most NT - 1 starts of tiles, times the width")
            return found

        LINEAR, MAXIMA, SUMS = "linear", "maxima", "sums"
        ORDER = [LINEAR] * 3 + [MAXIMA, SUMS] * L + [LINEAR] * 2
        WEIGHTED = [True, False, False] + [False, False] * L + [True, True]

        def rounds_before(p, *kinds):
            return sum(ROUNDS for k in ORDER[:p] if k in kinds)

        def half_before(i, j, before_p):
            if j >= 2:
                return group_done[j - 2], i + (before_p + 2)
            return group_done[j + 2], i + (before_p + 1)

        @block.sync
        def _(sp):
            e_view = lambda ap: ap.rearrange("(p c) -> p c", p=EP)
            sp.dma_start(dst_i, e_view(a["dst"])).then_inc(loads, 16)
            sp.dma_start(src_i, e_view(a["src"])).then_inc(loads, 16)
            sp.dma_start(typ_i, e_view(a["edge_type_16"])).then_inc(loads, 16)
            sp.dma_start(w_in, e_view(a["edge_weight"])).then_inc(loads, 16)
            full = (NT - 1) * P
            sp.dma_start(x[:, 0:NT - 1, :], a["x"][0:full, :].rearrange("(b p) d -> p b d", p=P)).then_inc(late_loads, 16)
            sp.wait_ge(constants, 1)
            sp.dma_start(x[0:N - full, NT - 1, :], a["x"][full:N, :]).then_inc(late_loads, 16)
            for n in w_names:
                sp.dma_start(wt[n][:, :], a[n]).then_inc(late_loads, 16)
            for n in rows:
                sp.dma_start(row[n][:, :], a[n].partition_broadcast(P)).then_inc(late_loads, 16)
            sp.dma_start(w_loop[:, :, :], a["L2_gnn_W_loop"].rearrange("l d o -> d l o")).then_inc(late_loads, 16)
            sp.dma_start(w_gat[:, :, :], a["L2_gnn_W_gat"].rearrange("l d o -> d l o")).then_inc(late_loads, 16)
            sp.dma_start(w_fuse[:, :, :], a["L2_gnn_W_fuse"].rearrange("(k d) o -> d k o", k=2)).then_inc(late_loads, 16)
            sp.dma_start(w_gate[:, :], a["L2_gnn_W_gate"][0:D, :]).then_inc(late_loads, 16)
            sp.dma_start(gate_row[:, :], a["L2_gnn_W_gate"][D:D + 1, :].squeeze(0).partition_broadcast(P)).then_inc(late_loads, 16)
            sp.wait_ge(blank_ready, 1)
            sp.dma_start(records.rearrange("(e t) f -> e t f", e=P), blank).then_inc(blank_stored, 16)
            sp.wait_ge(put_done[0], DEG_ITERS * G * 16)
            sp.wait_ge(put_done[1], DEG_ITERS * G * 16)
            sp.dma_start(grouped, records.rearrange("(e t) f -> e t f", e=P)).then_inc(grouped_loaded, 16)
            sp.wait_ge(local_ready, 1)
            sp.dma_start(local_rows.rearrange("(k t e) -> t k e", k=4, e=P), local_T).then_inc(local_stored, 16)

            def store_rows(table, view, k):
                sp.wait_ge(rows_ready, k)
                sp.dma_start(table.rearrange("(b p) d -> p b d", p=P), view).then_inc(rows_stored, 16)

            count = 0
            for p, kind in enumerate(ORDER):
                if kind == LINEAR:
                    count += 1
                    store_rows(node_rows, tmp[:, :, :], count)
                if p == 0:
                    sp.wait_ge(local_stored, 16)
                    with sp.Fori(0, 2 * ROUNDS) as i:
                        for k in HALVES:
                            sp.wait_ge(wide_used[k], i + 1)
                            sp.dma_start(wide[k], local_rows[bass.ds((i * 2 + k) * (G * P), G * P)].partition_broadcast(P)).then_inc(wide_in[k], 16)
                if kind == MAXIMA:
                    l = rounds_before(p, MAXIMA) // ROUNDS
                    sp.wait_ge(layer_free, l + 1)
                    sp.dma_start(w_rel[:, :, :], a["L2_gnn_W_rel"][l].rearrange("r d o -> d r o")).then_inc(layer_loads, 16)
                    sp.dma_start(b_rel[:, :], a["L2_gnn_b_rel"][l].partition_broadcast(P)).then_inc(layer_loads, 16)
                    sp.dma_start(b_gat[:, :], a["L2_gnn_b_gat"][l].partition_broadcast(P)).then_inc(layer_loads, 16)
                    sp.dma_start(attn_l[:, :], a["L2_gnn_attn_l"][l].rearrange("h d -> (h d)").partition_broadcast(P)).then_inc(layer_loads, 16)
                    sp.dma_start(attn_r[:, :], a["L2_gnn_attn_r"][l].rearrange("h d -> (h d)").partition_broadcast(P)).then_inc(layer_loads, 16)
                    count += 1
                    store_rows(attention_rows, gat[:, :, :], count)
                    before_p = rounds_before(p, LINEAR, MAXIMA, SUMS)
                    before_m = rounds_before(p, MAXIMA)
                    with sp.Fori(0, ROUNDS) as i:
                        for j in range(RING):
                            sp.wait_ge(*half_before(i, j, before_p))
                            sp.dma_start(flat(member[j % 2]), mask_d[:, bass.ds((i * RING + j) * (G * P), G * P)]).then_inc(member_in[j % 2], 16)
                            sp.wait_ge(gathered[j], i * (16 * G) + (before_p + 1) * 16 * G)
                            sp.dma_start(edge_z[:, bass.ds((i * RING + j) * (G * ZW), G * ZW)], flat(ring[j])).then_inc(z_stored[j], 16)
                            if j % 2:
                                sp.wait_ge(rel_taken, i * RING + (before_m * RING + j + 2))
                                sp.dma_start(relation_rows[bass.ds((i * 2 + j // 2) * (P * R), P * R), :].rearrange("(p r) d -> p (r d)", p=P),
                                             stage[j // 2]).then_inc(rel_stored[j // 2], 16)
                if kind == SUMS:
                    before_p = rounds_before(p, LINEAR, MAXIMA, SUMS)
                    for j in range(RING):
                        sp.wait_ge(z_stored[j], rounds_before(p, MAXIMA) * 16)
                    for k in HALVES:
                        sp.wait_ge(rel_stored[k], rounds_before(p, MAXIMA) * 16)
                    for j in range(RING):
                        sp.wait_ge(group_done[j], before_p + 1)
                    before_s = rounds_before(p, SUMS)
                    with sp.Fori(0, ROUNDS) as i:
                        for j in range(RING):
                            sp.wait_ge(er_top_ready[j % 2], i * 2 + (before_s * 2 + j // 2 + 1))
                            sp.wait_ge(msg_ready[j % 2], i * 2 + (before_s * 2 + j // 2 + 1))
                            sp.dma_start(flat(member[j % 2]), member_d[:, bass.ds((i * RING + j) * (G * P), G * P)]).then_inc(member_in[j % 2], 16)
                            sp.dma_start(flat(z_in[j % 2]), edge_z[:, bass.ds((i * RING + j) * (G * ZW), G * ZW)]).then_inc(z_loaded[j % 2], 16)
            sp.wait_ge(rows_ready, count + 1)
            sp.dma_start(out[0:full, :].rearrange("(b p) d -> p b d", p=P), x[:, 0:NT - 1, :]).then_inc(stored, 16)
            sp.dma_start(out[full:N, :], x[0:N - full, NT - 1, :]).then_inc(stored, 16)
            sp.wait_ge(stored, 32)


        @block.gpsimd
        def _(pool):
            def passed():
                nc.gpsimd.sem_inc(pool_passed, 1)

            nc.gpsimd.iota(lane[:, :], [[1, P]], base=0, channel_multiplier=0, allow_small_or_imprecise_dtypes=True)
            nc.gpsimd.iota(part[:, :], [[0, 1]], base=0, channel_multiplier=1, allow_small_or_imprecise_dtypes=True)
            nc.gpsimd.iota(tile_no[:, :], [[1, TILES]], base=0, channel_multiplier=0, allow_small_or_imprecise_dtypes=True)
            nc.gpsimd.memset(x[:, NT - 1, :], 0.0)
            nc.gpsimd.memset(blank, 0.0)
            nc.gpsimd.drain()
            nc.gpsimd.memset(blank[:, :, 1:2], -1.0)
            nc.gpsimd.drain().then_inc(constants, 1)
            pool.wait_ge(constants, 1)
            pool.wait_ge(blank_stored, 16)
            pool.wait_ge(slots_ready, 1)
            staged = Steps(index_staged)

            def stage_put(i, k):
                cols = bass.ds(i * (2 * G) + k * G, G)
                nc.gpsimd.tensor_copy(index[k][0:EP, :], slot[:, cols]).then_inc(index_staged, 1)
                nc.gpsimd.tensor_copy(put_rec[k][0:EP, :, :], rec[:, cols, :]).then_inc(index_staged, 1)
                pool.wait_ge(index_staged, staged.add(2))
                passed()
                for g in range(G):
                    nc.gpsimd.indirect_dma_start(
                        out=records, out_offset=bass.IndirectOffsetOnAxis(ap=index[k][0:EP, g:g + 1], axis=0),
                        in_=put_rec[k][0:EP, g, :], in_offset=None).then_inc(put_done[k], 16)

            for k in HALVES:
                stage_put(0, k)
            staged_first = staged.now
            with pool.Fori(1, DEG_ITERS) as i:
                staged.now = i * 4
                for k in HALVES:
                    pool.wait_ge(put_done[k], i * (16 * G))
                    passed()
                    stage_put(i, k)
            staged.now = staged_first * DEG_ITERS

            pool.wait_ge(grouped_ready, 1)
            stores = 0
            for p, kind in enumerate(ORDER):
                before_p = rounds_before(p, LINEAR, MAXIMA, SUMS)
                before_m = rounds_before(p, MAXIMA)
                table, rows_of, width = {LINEAR: (node_rows, src_row, D), MAXIMA: (attention_rows, src_row, ZW),
                                         SUMS: (relation_rows, rel_row, D)}[kind]

                def stage_index(group, j):
                    nc.gpsimd.tensor_copy(index[j][:, :], rows_of[:, bass.ds(group * G, G)]).then_inc(index_staged, 1)
                    return staged.add()

                def gather_round(i, first):
                    for j in range(RING):
                        ahead = (j + 1) % RING
                        pool.wait_ge(group_done[ahead], i + (before_p + 1 + (j + 1) // RING))
                        passed()
                        if kind == MAXIMA and not (first and ahead):
                            pool.wait_ge(z_stored[ahead], i * 16 + (before_m + (j + 1) // RING) * 16)
                            passed()
                        here = staged.now
                        stage_index(i * RING + (j + 1), ahead)
                        pool.wait_ge(index_staged, here)
                        passed()
                        for g in range(G):
                            nc.gpsimd.indirect_dma_start(
                                out=ring[j][:, g, 0:width], out_offset=None, in_=table,
                                in_offset=bass.IndirectOffsetOnAxis(ap=index[j][:, g:g + 1], axis=0)).then_inc(gathered[j], 16)

                if kind in (LINEAR, MAXIMA):
                    stores += 1
                    pool.wait_ge(rows_stored, 16 * stores)
                if kind == SUMS:
                    for k in HALVES:
                        pool.wait_ge(rel_stored[k], 16 * before_m)
                    for j in range(RING):
                        pool.wait_ge(z_stored[j], 16 * before_m)
                pool.wait_ge(group_done[0], before_p + 1)
                if p:
                    pool.wait_ge(index_staged, staged.now)
                stage_index(0, 0)
                base = staged.now
                first = 0
                if kind == MAXIMA:
                    gather_round(0, True)
                    first = 1
                with pool.Fori(first, ROUNDS) as i:
                    staged.now = i * RING + base
                    gather_round(i, False)
                staged.now = base + RING * ROUNDS

        @block.scalar
        def _(act):
            def passed():
                nc.scalar.sem_inc(act_passed, 1)

            asked = [0]

            def asked_for():
                asked[0] += 1
                act.wait_ge(act_go, asked[0])

            def norm_root():
                asked_for()
                nc.scalar.activation(stat[:, 3, :], stat[:, 2, :], ACT.Sqrt).then_inc(act_done, 1)

            asked_for()
            nc.scalar.activation(stat[:, 4:6, :], stat[:, 6:8, :], ACT.Sqrt).then_inc(act_done, 1)
            norm_root()
            with act.Fori(0, 2 * ROUNDS) as i:
                for k in HALVES:
                    cols = bass.ds((i * 2 + k) * (G * P), G * P)
                    act.wait_ge(member_made[k], i + 1)
                    passed()
                    act.dma_start(member_d[:, cols], flat(member[k])).then_inc(member_out[k], 16)
                    act.dma_start(mask_d[:, cols], mask[k]).then_inc(member_out[k], 16)
                for k in HALVES:
                    act.wait_ge(member_out[k], i * 32 + 32)
                    nc.scalar.sem_inc(member_free[k], 1)
            for p, kind in enumerate(ORDER):
                l = rounds_before(p, MAXIMA) // ROUNDS
                before_p = rounds_before(p, LINEAR, MAXIMA, SUMS)
                before_m, before_s = rounds_before(p, MAXIMA), rounds_before(p, SUMS)
                if kind == MAXIMA:
                    def first_pass_round(i, first):
                        for j in range(RING):
                            k, s = j % 2, j // 2
                            if k == 0:
                                nc.scalar.copy(hT_tile[s][:, :], hT[:, bass.ds(i * 2 + s, 1), :].squeeze(1)
                                               if not isinstance(i, int) else hT[:, i * 2 + s, :]).then_inc(hT_staged, 1)
                            act.wait_ge(elT_ps_ready[k], i * 2 + (before_m * 2 + s + 1))
                            nc.scalar.copy(elT[k][:, :], elT_ps[k]).then_inc(elT_ready[k], 1)
                            if k == 0 and not first:
                                act.wait_ge(rel_stored[s], i * 16 + before_m * 16)
                                passed()
                            elif k == 0 and before_m:
                                act.wait_ge(rel_stored[s], before_m * 16)
                            act.wait_ge(rel_ps_full, i * RING + (before_m * RING + j + 1))
                            nc.scalar.copy(stage[s][:, 1024 * k:1024 * (k + 1)], rel_ps).then_inc(rel_taken, 1)

                    act.wait_ge(pass_go, p + 1)
                    first_pass_round(0, True)
                    with act.Fori(1, ROUNDS) as i:
                        first_pass_round(i, False)
                if kind == SUMS:
                    with act.Fori(0, ROUNDS) as i:
                        for j in range(RING):
                            k = j % 2
                            act.wait_ge(score_ready[k], i * 2 + (before_s * 2 + j // 2 + 1))
                            nc.scalar.activation(z_msg[k][:, :, D:ZW], score[k][:, :, :], ACT.Exp).then_inc(exp_ready[k], 1)
                            act.wait_ge(*half_before(i, j, before_p))
                            passed()
                            for g in range(G):
                                nc.scalar.activation(onehot[k][:, g, :], lane[:, :], ACT.Square,
                                                     bias=minus_local[:, bass.ds((i * RING + j) * G + g, 1)]).then_inc(squared, 1)
                            act.wait_ge(squared, i * (RING * G) + (before_s * RING * G + (j + 1) * G))
                            nc.scalar.activation(flat(onehot[k]), flat(onehot[k]), ACT.Relu, bias=ones[:, 0:1], scale=-1.0).then_inc(onehot_ready[k], 1)
                    if l == 1:
                        asked_for()
                        nc.scalar.activation(tmp2[:, :, :], tmp2[:, :, :], ACT.Sigmoid).then_inc(act_done, 1)
                    if l == L:
                        norm_root()
                if kind == LINEAR and p in (0, 2, len(ORDER) - 1):
                    norm_root()

        @block.tensor
        def _(pe):
            asked = [0]

            def asked_for():
                asked[0] += 1
                pe.wait_ge(pe_go, asked[0])

            def transpose_nodes(src):
                asked_for()
                for b in range(NT):
                    last = nc.tensor.transpose(sums3[:, b, :], src[:, b, 0:D], ident[:, :])
                last.then_inc(pe_done, 1)

            def multiply_nodes(*pairs):
                asked_for()
                for b in range(NT):
                    for n, (turned, w) in enumerate(pairs):
                        last = nc.tensor.matmul(sums3[:, b, :], turned[:, b, :], w, start=n == 0, stop=n == len(pairs) - 1)
                last.then_inc(pe_done, 1)

            def clear(width):
                for at in range(0, width, 512):
                    n = min(512, width - at)
                    last = nc.tensor.matmul(ps[:, at:at + n], zeros_b[:, 0:P], zeros_b[:, 0:n], start=True, stop=True)
                return last

            asked_for()
            nc.tensor.matmul(ps[0:EP, 0:NT], below[0:EP, 0:EP], total[0:EP, :], start=True, stop=True)
            nc.tensor.matmul(ps[:, 512:512 + NT], ones[0:EP, :], total[0:EP, :], start=True, stop=True).then_inc(pe_done, 1)
            asked_for()
            for at in (0, 512):
                nc.tensor.matmul(ps[:, at:at + NT], zeros_b[:, 0:P], zeros_b[:, 0:NT], start=True, stop=True)
            with pe.Fori(0, DEG_ITERS) as i:
                for k in HALVES:
                    pe.wait_ge(degree_hot[k], i + 1)
                    for g in range(G):
                        nc.tensor.matmul(ps[:, 0:NT], src_low[k][:, g, :], src_high[k][:, g, :], start=False, stop=True, skip_group_check=True)
                        last = nc.tensor.matmul(ps[:, 512:512 + NT], dst_low[k][:, g, :], dst_high[k][:, g, :], start=False, stop=True, skip_group_check=True)
                    last.then_inc(degree_used[k], 1)
            nc.tensor.matmul(ps[:, 1024:1025], ones[0:EP, :], weight_sum[0:EP, :], start=True, stop=True).then_inc(pe_done, 1)
            asked_for()
            nc.tensor.transpose(ps[:, 0:P], wt["L0_gnn_W"][:, :], ident[:, :]).then_inc(pe_done, 1)

            def tiles_of(i, j):
                return destinations(mybir.EngineType.PE, *((at_sums, D) if kind == LINEAR else (at_er_top, 6 * HEADS)), i, j)

            passes = [0]

            def start_pass():
                passes[0] += 1
                pe.wait_ge(pass_go, passes[0])

            transpose_nodes(tmp)
            multiply_nodes((hT, w0T[:, :]))
            asked_for()
            quarter = TILES // 4
            for q in range(4):
                last = nc.tensor.transpose(ps[0:quarter, P * q:P * (q + 1)], local[:, quarter * q:quarter * (q + 1)], ident[:, :])
            last.then_inc(pe_done, 1)
            for p, kind in enumerate(ORDER):
                before_p = rounds_before(p, LINEAR, MAXIMA, SUMS)
                before_m, before_s = rounds_before(p, MAXIMA), rounds_before(p, SUMS)
                before_hot = rounds_before(p, LINEAR, SUMS)
                l = before_m // ROUNDS
                if kind == MAXIMA:
                    transpose_nodes(h)
                    pe.wait_ge(layer_loads, 16 * 5 * (l + 1))
                    multiply_nodes((hT, w_gat[:, l, :]))
                    multiply_nodes((hT, w_loop[:, l, :]))
                start_pass()
                if kind == LINEAR:
                    clear(NPAD)
                    with pe.Fori(0, ROUNDS) as i:
                        for j in range(RING):
                            k = j % 2
                            columns = tiles_of(i, j)
                            pe.wait_ge(gathered[j], i * (16 * G) + (before_p + 1) * 16 * G)
                            pe.wait_ge(onehot_ready[k], i * 2 + (before_hot * 2 + j // 2 + 1))
                            for g in range(G):
                                last = nc.tensor.matmul(sums[:, bass.ds(columns[g], D)], onehot[k][:, g, :], ring[j][:, g, 0:D],
                                                        start=False, stop=True, skip_group_check=True)
                            last.then_inc(group_done[j], 1)
                if kind == MAXIMA:
                    with pe.Fori(0, ROUNDS) as i:
                        for j in range(RING):
                            k = j % 2
                            use = i * 2 + (before_m * 2 + j // 2 + 1)
                            pe.wait_ge(el_split[k], use)
                            nc.tensor.transpose(elT_ps[k], el_parts[k][:, :, :, :].rearrange("p a b c -> p (a b c)"), ident_b[:, :]).then_inc(elT_ps_ready[k], 1)
                            pe.wait_ge(hT_staged, i * 2 + (before_m * 2 + j // 2 + 1))
                            pe.wait_ge(rel_taken, i * RING + (before_m * RING + j + 1))
                            for q in range(2):
                                last = nc.tensor.matmul(rel_ps[:, 512 * q:512 * (q + 1)], hT_tile[j // 2][:, :],
                                                        w_rel[:, 8 * k + 4 * q:8 * k + 4 * (q + 1), :], start=True, stop=True)
                            last.then_inc(rel_ps_full, 1)
                            pe.wait_ge(member_in[k], i * 32 + (before_m + before_s) * 32 + (j // 2 + 1) * 16)
                            pe.wait_ge(elT_ready[k], use)
                            for g in range(G):
                                pair, s = el_ps[g // 2 % PAIRS], g % 2
                                if s == 0:
                                    pe.wait_ge(el_taken, i * (RING * G // 2) + ((before_m * RING + j) * G // 2 + g // 2 + 1))
                                nc.tensor.matmul(pair[:, s, :, :], ident_b[:, :], across(member[k][:, g, :], HEADS), start=True, stop=True)
                                for head in range(HEADS):
                                    last = nc.tensor.matmul(pair[:, s, head, :], pick[:, g * HEADS + head, :], elT[k][:, :],
                                                            start=False, stop=True, skip_group_check=True)
                                if s == 1:
                                    last.then_inc(el_wide, 1)
                if kind == SUMS:
                    def edge_terms(i, j):
                        k = j % 2
                        use = i * 2 + (before_s * 2 + j // 2 + 1)
                        columns = tiles_of(i, j)
                        pe.wait_ge(member_in[k], i * 32 + ((before_m + before_s) * 32 + (j // 2 + 1) * 16))
                        pe.wait_ge(er_top_taken[k], use)
                        for g in range(G):
                            for n in range(3):
                                last = nc.tensor.matmul(er_top_ps[k][:, g, :], member[k][:, g, :],
                                                        er_top_flat[:, bass.ds(columns[g] + n * 2 * HEADS, 2 * HEADS)],
                                                        start=n == 0, stop=n == 2)
                        last.then_inc(er_top_ready[k], 1)

                    def sums_round(i, last_round):
                        for j in range(RING):
                            k = j % 2
                            if j < RING - 1:
                                edge_terms(i, j + 1)
                            elif not last_round:
                                edge_terms(i + 1, 0)
                            pe.wait_ge(gathered[j], i * (16 * G) + (before_p + 1) * 16 * G)
                            pe.wait_ge(onehot_ready[k], i * 2 + (before_hot * 2 + j // 2 + 1))
                            pe.wait_ge(msg_ready[k], i * 2 + (before_s * 2 + j // 2 + 2))
                            for g in range(G):
                                pe.wait_ge(z_added, i * (RING * G) + ((before_s * RING + j) * G + g + 1))
                                slot_ps = msg_ps[g % MSG_SLOTS]
                                nc.tensor.matmul(slot_ps[:, 0:D], onehot[k][:, g, :], ring[j][:, g, 0:D], start=True, stop=True)
                                nc.tensor.matmul(slot_ps[:, D:D + ZW], onehot[k][:, g, :], z_msg[k][:, g, :], start=True, stop=True).then_inc(z_sum, 1)

                    edge_terms(0, 0)
                    with pe.Fori(0, ROUNDS - 1) as i:
                        sums_round(i, False)
                    sums_round(ROUNDS - 1, True)
                    transpose_nodes(self_term)
                    transpose_nodes(gat)
                    multiply_nodes((hT, w_fuse[:, 0, :]), (tmp, w_fuse[:, 1, :]))
                    if l == 1:
                        transpose_nodes(tmp)
                        multiply_nodes((hT, w_gate[:, :]))
                if kind == LINEAR and p > 2:
                    transpose_nodes(tmp)
                    multiply_nodes((hT, wt[f"L3_gnn_W{p - len(ORDER) + 3}"][:, :]))

        @block.vector
        def _(dve_):
            v = nc.vector
            steps = Steps(dve)

            def link(ins):
                ins.then_inc(dve, 1)
                dve_.wait_ge(dve, steps.add())

            def tell(s, k=1):
                v.sem_inc(s, k)

            asked = {"pe": 0, "act": 0}

            def ask_pe():
                tell(pe_go)
                asked["pe"] += 1
                dve_.wait_ge(pe_done, asked["pe"])

            def ask_act():
                tell(act_go)
                asked["act"] += 1
                dve_.wait_ge(act_done, asked["act"])

            for k in HALVES:
                for s in (wide_used, degree_used, member_free, er_top_taken, er_top_ready, msg_ready):
                    v.sem_inc(s[k], 1)
            for j in range(RING):
                v.sem_inc(group_done[j], 1)
            v.sem_inc(rel_taken, 1)
            v.sem_inc(el_taken, PAIRS)
            v.sem_inc(z_added, MSG_SLOTS)

            dve_.wait_ge(constants, 1)
            tell(blank_ready)
            v.memset(zeros_b[:, :], 0.0)
            v.memset(ones[:, :], 1.0)
            v.memset(hT[:, NT:2 * ROUNDS, :], 0.0)
            v.memset(src_row[:, TILES:TILES + G], 0)
            v.memset(rel_row[:, TILES:TILES + G], 0)
            v.tensor_scalar(ident[:, :], lane[:, :], part[:, :], None, ALU.is_equal)
            v.tensor_scalar(ident_b[:, :], lane[:, :], part[:, :], None, ALU.is_equal)
            v.tensor_scalar(below[:, :], lane[:, :], part[:, :], None, ALU.is_gt)
            K = 3 * G * HEADS
            kmod = stat[0:K, 0, 0:1]
            link(v.tensor_scalar(kmod, part[0:K, :], float(G * HEADS), float(-G * HEADS), ALU.is_ge, ALU.mult))
            link(v.tensor_tensor(kmod, kmod, part[0:K, :], ALU.add))
            link(v.tensor_scalar(stat[0:K, 1, 0:1], part[0:K, :], float(2 * G * HEADS), float(-G * HEADS), ALU.is_ge, ALU.mult))
            link(v.tensor_tensor(kmod, kmod, stat[0:K, 1, 0:1], ALU.add))
            link(v.tensor_scalar(pick[:, :, :], spread(lane[0:K, 0:G * HEADS], P), kmod, None, ALU.is_equal))

            dve_.wait_ge(loads, 64)
            v.tensor_copy(rec[:, :, 0], src_i)
            v.tensor_copy(rec[:, :, 1], dst_i)
            v.tensor_copy(rec[:, :, 2], typ_i)
            v.tensor_copy(rec[:, :, 3], w_in)
            v.tensor_scalar(dtile_i, dst_i, 7, None, ALU.logical_shift_right)
            v.tensor_scalar(tmp_i, src_i, 7, None, ALU.logical_shift_right)
            v.memset(pos, 0.0)
            link(v.tensor_reduce(weight_sum[0:EP, :], w_in, AX.X, ALU.add))
            v.tensor_copy(dtile, dtile_i)
            link(v.tensor_copy(stile, tmp_i))
            v.scalar_tensor_tensor(dlow, dtile, -float(P), rec[:, :, 1], ALU.mult, ALU.add)
            link(v.scalar_tensor_tensor(slow, stile, -float(P), rec[:, :, 0], ALU.mult, ALU.add))
            for b in steps.rounds(dve_, NT, 5):
                link(v.tensor_scalar(hit, dtile, tile_no[0:EP, bass.ds(b, 1)], None, ALU.is_equal))
                link(v.tensor_tensor_scan(run, ones[0:EP, 0:1].to_broadcast([EP, EC]), hit, 0.0, ALU.mult, ALU.add))
                link(v.tensor_scalar(total[0:EP, bass.ds(b, 1)], run[:, EC - 1:EC], 1.0, None, ALU.mult))
                link(v.tensor_tensor(hit, hit, run, ALU.mult))
                link(v.tensor_tensor(pos, pos, hit, ALU.add))
            ask_pe()
            link(v.tensor_scalar(tiles_i[:, :], ps[:, 512:512 + NT], float(P - 1), None, ALU.add))
            link(v.tensor_scalar(tiles_i[:, :], tiles_i[:, :], 7, None, ALU.logical_shift_right))
            link(v.tensor_copy(tiles[:, :], tiles_i[:, :]))
            link(v.tensor_tensor_scan(first_tile[:, :], ones[:, 0:1].to_broadcast([P, NT]), tiles[:, :], 0.0, ALU.mult, ALU.add))
            link(v.tensor_tensor(first_tile[:, :], first_tile[:, :], tiles[:, :], ALU.subtract))
            link(v.scalar_tensor_tensor(before[0:EP, :], first_tile[0:EP, :], float(P), ps[0:EP, 0:NT], ALU.mult, ALU.add))
            link(v.tensor_scalar(before[0:EP, :], before[0:EP, :], -1.0, None, ALU.add))
            for b in steps.rounds(dve_, NT, 2):
                cols = bass.ds(b, 1)
                link(v.tensor_scalar(hit, dtile, tile_no[0:EP, cols], before[0:EP, cols], ALU.is_equal, ALU.mult))
                link(v.tensor_tensor(pos, pos, hit, ALU.add))
            link(v.tensor_copy(slot_i, pos))
            v.tensor_scalar(hi_i, slot_i, 7, None, ALU.logical_shift_right)
            link(v.tensor_scalar(tmp_i, slot_i, P - 1, None, ALU.bitwise_and))
            link(v.scalar_tensor_tensor(slot, tmp_i, float(TILES), hi_i, ALU.mult, ALU.add))
            tell(slots_ready)
            link(v.memset(dst_tile[:, :], 0.0))
            for b in steps.rounds(dve_, NT - 1, 1):
                link(v.scalar_tensor_tensor(dst_tile[:, :], tile_no[:, :], first_tile[:, bass.ds(b + 1, 1)], dst_tile[:, :], ALU.is_ge, ALU.add))
            v.tensor_scalar(at_sums[:, :], dst_tile[:, :], float(D), None, ALU.mult)
            v.tensor_scalar(at_er_top[:, :], dst_tile[:, :], float(6 * HEADS), None, ALU.mult)
            v.tensor_scalar(at_agg[:, :], dst_tile[:, :], float(D + ZW), None, ALU.mult)
            v.memset(new_tile[:, 0:1], -BIG)
            link(v.tensor_tensor(new_tile[:, 1:TILES], dst_tile[:, 1:TILES], dst_tile[:, 0:TILES - 1], ALU.not_equal))
            link(v.tensor_scalar(new_tile[:, 1:TILES], new_tile[:, 1:TILES], -BIG, None, ALU.mult))
            link(v.tensor_tensor(before[:, :], first_tile[:, :], tiles[:, :], ALU.add))
            link(v.tensor_scalar(before[:, :], before[:, :], -1.0, 0.0, ALU.add, ALU.max))
            link(v.tensor_scalar(last_tile_i[:, :], before[:, :], float(HEADS), None, ALU.mult))
            tell(pe_go)
            asked["pe"] += 1
            for i in steps.rounds(dve_, DEG_ITERS, 2):
                for k in HALVES:
                    cols = bass.ds((i * 2 + k) * G, G)
                    dve_.wait_ge(degree_used[k], i + 1)
                    v.tensor_tensor(src_low[k], spread(slow[:, cols], P), across(lane[0:EP, :], G), ALU.is_equal)
                    v.tensor_tensor(dst_low[k], spread(dlow[:, cols], P), across(lane[0:EP, :], G), ALU.is_equal)
                    v.tensor_tensor(src_high[k], spread(stile[:, cols], NT), across(lane[0:EP, 0:NT], G), ALU.is_equal)
                    link(v.tensor_tensor(dst_high[k], spread(dtile[:, cols], NT), across(lane[0:EP, 0:NT], G), ALU.is_equal))
                    tell(degree_hot[k])
            dve_.wait_ge(pe_done, asked["pe"])
            v.tensor_scalar(stat[:, 6, :], ps[:, 0:NT], 1.0, None, ALU.max)
            v.tensor_scalar(stat[:, 7, :], ps[:, 512:512 + NT], 1.0, None, ALU.max)
            v.tensor_scalar(in_norm0[:, :], ps[:, 512:512 + NT], 0.0, None, ALU.is_gt)
            link(v.tensor_scalar(weight_mean[:, :], ps[:, 1024:1025], 1.0 / E, None, ALU.mult))
            ask_act()
            v.reciprocal(out_norm[:, :], stat[:, 4, :])
            link(v.reciprocal(in_norm[:, :], stat[:, 5, :]))
            link(v.tensor_tensor(in_norm0[:, :], in_norm0[:, :], in_norm[:, :], ALU.mult))

            dve_.wait_ge(late_loads, LATE_LOADS * 16)
            ask_pe()
            link(v.tensor_copy(w0T[:, :], ps[:, 0:P]))
            link(v.scalar_tensor_tensor(gate_row[:, :], gate_row[:, :], weight_mean[:, :], row["L2_gnn_b_gate"][:, :], ALU.mult, ALU.add))

            def layer_norm(src, to):
                link(v.tensor_reduce(stat[:, 0, :], src[:, :, :], AX.X, ALU.add))
                link(v.tensor_scalar(stat[:, 0, :], stat[:, 0, :], 1.0 / D, None, ALU.mult))
                link(v.tensor_tensor(src[:, :, :], src[:, :, :], spread(stat[:, 0, :], D), ALU.subtract))
                link(v.tensor_tensor(to[:, :, :], src[:, :, :], src[:, :, :], ALU.mult))
                link(v.tensor_reduce(stat[:, 1, :], to[:, :, :], AX.X, ALU.add))
                link(v.tensor_scalar(stat[:, 2, :], stat[:, 1, :], 1.0 / D, LN_EPS, ALU.mult, ALU.add))
                ask_act()
                link(v.reciprocal(stat[:, 1, :], stat[:, 3, :]))
                link(v.tensor_tensor(to[:, :, :], src[:, :, :], spread(stat[:, 1, :], D), ALU.mult))

            def scaled(to, src, norm):
                link(v.tensor_tensor(to[:, :, :], src, spread(norm[:, :], D), ALU.mult))

            def plus_row(to, src, r, op=ALU.add):
                link(v.tensor_tensor(to[:, :, :], src, across(r[:, :], NT), op))

            def add(to, one, other):
                link(v.tensor_tensor(to[:, :, :], one[:, :, :], other[:, :, :], ALU.add))

            def split(parts, src, rest):
                link(v.tensor_copy(parts[0], src))
                link(v.tensor_tensor(rest, src, parts[0], ALU.subtract))
                link(v.tensor_copy(parts[1], rest))
                link(v.tensor_tensor(rest, rest, parts[1], ALU.subtract))
                link(v.tensor_copy(parts[2], rest))

            def make_onehot(i, j, before_hot, before_p, weighted):
                k = j % 2
                dve_.wait_ge(*half_before(i, j, before_p))
                v.sem_inc(dve_passed, 1)
                cols = bass.ds((i * RING + j) * G, G)
                link(v.tensor_tensor(onehot[k][:, :, :], spread(local[:, cols], P), across(lane[:, :], G), ALU.is_equal))
                if weighted:
                    link(v.tensor_tensor(onehot[k][:, :, :], onehot[k][:, :, :], spread(weight[:, cols], P), ALU.mult))
                tell(onehot_ready[k])

            def make_members(i, j):
                k = j % 2
                dve_.wait_ge(wide_in[k], i * 32 + (16 + 16 * (j // 2)))
                v.sem_inc(dve_passed, 1)
                dve_.wait_ge(member_free[k], i * 2 + (1 + j // 2))
                v.sem_inc(dve_passed, 1)
                link(v.tensor_scalar(flat(member[k]), wide[k], part[:, :], None, ALU.is_equal))
                tell(wide_used[k])
                link(v.tensor_scalar(mask[k], flat(member[k]), -1.0, BIG, ALU.add, ALU.mult))
                tell(member_made[k])

            def end_pass(p):
                for j in range(RING):
                    dve_.wait_ge(group_done[j], rounds_before(p + 1, LINEAR, MAXIMA, SUMS) + 1)

            def edge_sums(p):
                tell(rows_ready)
                tell(pass_go)
                each = (2 if WEIGHTED[p] else 1) + (2 if p == 0 else 0)
                for i in steps.rounds(dve_, ROUNDS, RING * each):
                    for j in range(RING):
                        make_onehot(i, j, rounds_before(p, LINEAR, SUMS), rounds_before(p, LINEAR, MAXIMA, SUMS), WEIGHTED[p])
                        if p == 0:
                            make_members(i, j)
                end_pass(p)

            def turn(src_to):
                ask_pe()
                link(v.tensor_copy(src_to[:, 0:NT, :], sums3))

            link(v.tensor_copy(tmp2[:, :, :], x[:, :, :]))
            layer_norm(tmp2, tmp)
            plus_row(tmp, tmp[:, :, :], row["L0_gnn_ln_gamma"], ALU.mult)
            plus_row(tmp, tmp[:, :, :], row["L0_gnn_ln_beta"])
            turn(hT)
            ask_pe()
            plus_row(tmp, sums3, row["L0_gnn_b"])
            dve_.wait_ge(grouped_loaded, 16)
            v.scalar_tensor_tensor(local[:, :], dst_tile[:, :], -float(P), grouped[:, :, 1], ALU.mult, ALU.add)
            v.scalar_tensor_tensor(minus_local[:, :], dst_tile[:, :], float(P), grouped[:, :, 1], ALU.mult, ALU.subtract)
            v.tensor_copy(src_row[:, 0:TILES], grouped[:, :, 0])
            v.scalar_tensor_tensor(rel_row[:, 0:TILES], grouped[:, :, 0], float(R), grouped[:, :, 2], ALU.mult, ALU.add)
            link(v.tensor_copy(weight[:, :], grouped[:, :, 3]))
            tell(grouped_ready)
            ask_pe()
            link(v.tensor_copy(local_T, ps[0:TILES // 4, 0:4 * P].rearrange("p (k e) -> p k e", k=4)))
            tell(local_ready)
            edge_sums(0)
            link(v.scalar_tensor_tensor(flat(tmp2), sums, 0.0, flat(x), ALU.max, ALU.add))
            add(tmp2, tmp2, x)
            layer_norm(tmp2, x)

            scaled(tmp, x[:, :, :], in_norm0)
            edge_sums(1)
            scaled(h, sums3, in_norm0)
            scaled(tmp, h[:, :, :], in_norm0)
            add(self_term, x, h)
            edge_sums(2)
            scaled(tmp2, sums3, in_norm0)
            add(tmp2, tmp2, self_term)
            link(v.scalar_tensor_tensor(flat(tmp2), flat(tmp2), 1.0 / 3, flat(x), ALU.mult, ALU.add))
            layer_norm(tmp2, x)
            link(v.tensor_copy(h[:, :, :], x[:, :, :]))

            for l in range(L):
                p = 3 + 2 * l
                before_p, before_m, before_s = rounds_before(p, LINEAR, MAXIMA, SUMS), l * ROUNDS, l * ROUNDS
                tell(layer_free)
                turn(hT)
                ask_pe()
                dve_.wait_ge(layer_loads, 16 * 5 * (l + 1))
                link(v.tensor_copy(gat[:, :, 0:D], sums3))
                by_head = tmp[:, :, :].rearrange("p b (h d) -> p b h d", h=HEADS)
                for w, to in ((attn_l, gat[:, :, D:ZW]), (attn_r, er[:, :, :])):
                    plus_row(tmp, gat[:, :, 0:D], w, ALU.mult)
                    link(v.tensor_reduce(to, by_head, AX.X, ALU.add))
                tell(rows_ready)
                ask_pe()
                plus_row(self_term, sums3, b_rel)
                tell(pass_go)

                def split_scores(i, j):
                    k = j % 2
                    dve_.wait_ge(gathered[j], i * (16 * G) + (before_p + 1) * 16 * G)
                    v.sem_inc(dve_passed, 1)
                    dve_.wait_ge(*half_before(i, j, before_p))
                    v.sem_inc(dve_passed, 1)
                    split([el_parts[k][:, n, :, :] for n in range(3)], ring[j][:, :, D:ZW], score[k][:, :, :])
                    tell(el_split[k])

                def maxima_round(i, last_round):
                    for j in range(RING):
                        for g in range(0, G, 2):
                            n = i * (RING * G // 2) + ((before_m * RING + j) * G // 2 + g // 2 + 1)
                            dve_.wait_ge(el_wide, n)
                            v.sem_inc(dve_passed, 1)
                            at = bass.ds(((i * RING + j) * G + g) * HEADS, 2 * HEADS)
                            v.tensor_reduce(flat(tile_top)[:, at], el_ps[g // 2 % PAIRS].rearrange("p g h e -> p (g h) e"), AX.X, ALU.max).then_inc(el_taken, 1)
                            if g == 0:
                                if j < RING - 1:
                                    split_scores(i, j + 1)
                                elif not last_round:
                                    split_scores(i + 1, 0)
                        dve_.wait_ge(el_taken, n + PAIRS)
                        tell(group_done[j])

                split_scores(0, 0)
                for i in steps.rounds(dve_, ROUNDS - 1, RING * 5):
                    maxima_round(i, False)
                maxima_round(ROUNDS - 1, True)
                for head in range(HEADS):
                    v.tensor_tensor_scan(run_top[:, :, head], new_tile[:, :], tile_top[:, :, head], 0.0, ALU.add, ALU.max).then_inc(dve, 1)
                    steps.add()
                dve_.wait_ge(dve, steps.now)
                for b in range(0, NT, 5):
                    _, columns = nc.values_load_multi_w_load_instructions(
                        last_tile_i[0:1, b:b + 5], engines=[mybir.EngineType.DVE], min_val=0, max_val=HEADS * (TILES - 1),
                        skip_runtime_bounds_check_because="the last edge tile of a destination tile, clamped at 0")
                    for n in range(5):
                        v.tensor_copy(top[:, b + n, :], flat(run_top)[:, bass.ds(columns[n], HEADS)]).then_inc(dve, 1)
                        steps.add()
                dve_.wait_ge(dve, steps.now)
                link(v.tensor_tensor(top[:, :, :], top[:, :, :], er[:, :, :], ALU.add))
                link(v.scalar_tensor_tensor(top[:, :, :], top[:, :, :], 0.2, top[:, :, :], ALU.mult, ALU.max))
                split([er_top[:, :, n, 0:HEADS] for n in range(3)], er[:, :, :], sc[:, :, :])
                split([er_top[:, :, n, HEADS:2 * HEADS] for n in range(3)], top[:, :, :], sc[:, :, :])
                link(v.memset(agg_flat, 0.0))
                p += 1
                before_p, before_hot = rounds_before(p, LINEAR, MAXIMA, SUMS), rounds_before(p, LINEAR, SUMS)
                tell(pass_go)


                def messages(i, j):
                    k = j % 2
                    use = i * 2 + (before_s * 2 + j // 2 + 1)
                    dve_.wait_ge(z_loaded[k], i * 32 + (before_s * 32 + 16 * (j // 2 + 1)))
                    v.sem_inc(dve_passed, 1)
                    dve_.wait_ge(er_top_ready[k], use + 1)
                    v.sem_inc(dve_passed, 1)
                    e = score[k][:, :, :]
                    link(v.tensor_tensor(e, z_in[k][:, :, D:ZW], er_top_ps[k][:, :, 0:HEADS], ALU.add))
                    link(v.scalar_tensor_tensor(e, e, 0.2, e, ALU.mult, ALU.max))
                    link(v.tensor_tensor(e, e, er_top_ps[k][:, :, HEADS:2 * HEADS], ALU.subtract))
                    tell(er_top_taken[k])
                    link(v.tensor_scalar(e, e, 0.0, None, ALU.min))
                    tell(score_ready[k])
                    dve_.wait_ge(exp_ready[k], use)
                    link(v.tensor_tensor(z_msg[k][:, :, 0:D].rearrange("p g (h d) -> p g h d", h=HEADS),
                                         z_in[k][:, :, 0:D].rearrange("p g (h d) -> p g h d", h=HEADS),
                                         spread(z_msg[k][:, :, D:ZW], DH), ALU.mult))
                    tell(msg_ready[k])

                def sums_round(i, last_round):
                    for j in range(RING):
                        if j < RING - 1:
                            messages(i, j + 1)
                        elif not last_round:
                            messages(i + 1, 0)
                        columns = destinations(mybir.EngineType.DVE, at_agg, D + ZW, i, j)
                        for g in range(G):
                            n = i * (RING * G) + ((before_s * RING + j) * G + g + 1)
                            dve_.wait_ge(z_sum, n)
                            v.sem_inc(dve_passed, 1)
                            at = agg_flat[:, bass.ds(columns[g], D + ZW)]
                            v.tensor_tensor(at, at, msg_ps[g % MSG_SLOTS], ALU.add).then_inc(z_added, 1)
                            dve_.wait_ge(z_added, n + MSG_SLOTS)
                        tell(group_done[j])

                messages(0, 0)
                for i in steps.rounds(dve_, ROUNDS - 1, RING * 5):
                    sums_round(i, False)
                sums_round(ROUNDS - 1, True)
                end_pass(p)
                link(v.tensor_scalar(sc[:, :, :], agg[:, :, 2 * D:D + ZW], 1e-30, None, ALU.max))
                link(v.reciprocal(sc[:, :, :], sc[:, :, :]))
                link(v.tensor_tensor(gat[:, :, 0:D].rearrange("p b (h d) -> p b h d", h=HEADS),
                                     agg[:, :, D:2 * D].rearrange("p b (h d) -> p b h d", h=HEADS), spread(sc[:, :, :], DH), ALU.mult))
                link(v.tensor_tensor(gat[:, :, 0:D], gat[:, :, 0:D], across(b_gat[:, :], NT), ALU.add))
                link(v.tensor_tensor(self_term[:, :, :], agg[:, :, 0:D], self_term[:, :, :], ALU.add))
                turn(hT)
                turn(tmp)
                ask_pe()
                plus_row(tmp, sums3, row["L2_gnn_b_fuse"])
                if l == 0:
                    turn(hT)
                    ask_pe()
                    plus_row(tmp2, sums3, gate_row)
                    ask_act()
                    link(v.tensor_tensor(tmp[:, :, :], tmp[:, :, :], tmp2[:, :, :], ALU.mult))
                link(v.tensor_scalar(h[:, :, :], tmp[:, :, :], 0.0, None, ALU.max))
            add(tmp2, x, h)
            layer_norm(tmp2, x)

            link(v.tensor_copy(h[:, :, :], x[:, :, :]))
            for c in range(2):
                scaled(tmp, h[:, :, :], out_norm)
                edge_sums(3 + 2 * L + c)
                scaled(tmp, sums3, in_norm)
                turn(hT)
                ask_pe()
                plus_row(tmp, sums3, row[f"L3_gnn_b{c + 1}"])
                link(v.scalar_tensor_tensor(flat(h), flat(tmp), 0.0, flat(h), ALU.max, ALU.add))
            add(tmp2, x, h)
            layer_norm(tmp2, x)
            tell(rows_ready)


_INS = ["x", "src", "dst", "edge_type_16", "edge_weight", "L0_gnn_ln_gamma", "L0_gnn_ln_beta", "L0_gnn_W", "L0_gnn_b",
        "L2_gnn_W_rel", "L2_gnn_b_rel", "L2_gnn_W_loop", "L2_gnn_W_gat", "L2_gnn_attn_l", "L2_gnn_attn_r",
        "L2_gnn_b_gat", "L2_gnn_W_fuse", "L2_gnn_b_fuse", "L2_gnn_W_gate", "L2_gnn_b_gate", "L3_gnn_W1", "L3_gnn_b1",
        "L3_gnn_W2", "L3_gnn_b2"]


def kernel(**inputs):
    import numpy as _np
    import concourse.bacc as _bacc
    from concourse import mybir as _mybir
    from concourse.bass_utils import run_bass_kernel_spmd as _run

    nc = _bacc.Bacc("TRN2", target_bir_lowering=False, num_devices=1)
    arrays, args = {}, {}
    for name in _INS:
        a = _np.ascontiguousarray(inputs[name])
        arrays[f"in_{name}"] = a
        args[name] = nc.dram_tensor(f"in_{name}", a.shape, _mybir.dt.from_np(a.dtype), kind="ExternalInput").ap()
    out = nc.dram_tensor("out_0", (N, D), _mybir.dt.float32, kind="ExternalOutput").ap()
    gnn_stack(nc, args, out)
    r = _run(nc, [arrays], core_ids=[0])
    return r.results[0]["out_0"]
```

```python
import concourse.bass as bass
from concourse import mybir
from contextlib import ExitStack

N, D, E, R, L, HEADS = 3125, 128, 50000, 16, 3, 4
P = 128
DH = D // HEADS
NT = -(-N // P)
NPAD = NT * P
EP = 125
EC = E // EP
G = 8
RING = 4
TILES = -(-((E + NT * (P - 1)) // P) // (RING * G)) * RING * G
ROUNDS = TILES // (RING * G)
MSG_SLOTS = 4
PAIRS = 2
DEG_ITERS = EC // (2 * G)
ZW = D + HEADS
CHUNK = 3
CHUNKS = -(-NT // CHUNK)
FIRST_PART = CHUNKS // 2 * CHUNK
PARTS = [slice(0, FIRST_PART), slice(FIRST_PART, NT)]
BIG = float(2.0 ** 100)
LN_EPS = 1e-5


class Steps:

    def __init__(self, sem):
        self.sem, self.now, self.made = sem, 0, 0

    def add(self, k=1):
        self.now, self.made = self.now + k, self.made + k
        return self.now

    def rounds(self, eng, count, each):
        start = self.now
        with eng.Fori(0, count) as i:
            self.now, self.made = i * each + start, 0
            yield i
            assert self.made == each, (self.made, each)
        self.now = start + count * each


def gnn_stack(nc, a, out):
    f32, bf16, i32, u32 = mybir.dt.float32, mybir.dt.bfloat16, mybir.dt.int32, mybir.dt.uint32
    ALU, ACT, AX = mybir.AluOpType, mybir.ActivationFunctionType, mybir.AxisListType

    def dram(name, shape, dt):
        return nc.dram_tensor(name, shape, dt, kind="Internal").ap()

    records = dram("records", [P * TILES, 4], f32)
    node_rows = dram("node_rows", [NPAD, D], f32)
    attention_rows = dram("attention_rows", [NPAD, ZW], f32)
    relation_rows = dram("relation_rows", [2 * ROUNDS * P * R, D], f32)
    edge_z = dram("edge_z", [P, TILES * ZW], f32)
    local_rows = dram("local_rows", [TILES * P], f32)
    member_d = dram("member_d", [P, TILES * P], bf16)

    with ExitStack() as ctx:
        def sb(name, shape, dt=f32):
            return ctx.enter_context(nc.sbuf_tensor(name, shape, dt))

        def sem(name):
            return ctx.enter_context(nc.semaphore(name))

        def pair(name):
            return [sem(name + "_even"), sem(name + "_odd")]

        lane = sb("lane", [P, P])
        part = sb("part", [P, 1])
        ident = sb("ident", [P, P])
        ident_b = sb("ident_b", [P, P], bf16)
        below = sb("below", [P, P])
        ones = sb("ones", [P, P])
        zeros_b = sb("zeros_b", [P, 4 * P], bf16)
        tile_no = sb("tile_no", [P, TILES])
        assert 2 * ROUNDS >= NT
        SCORES, BITS = 3 * HEADS, 7
        FLAG, NOT_BITS, ROWS = SCORES + BITS, SCORES + BITS + 1, 32
        BLOCKS = P // ROWS
        pick = sb("pick", [P, BLOCKS, P], bf16)
        of_head = sb("of_head", [P, HEADS])
        bits = sb("bits", [P, TILES, BITS + 1], bf16)
        x = sb("x", [P, NT, D])
        h = sb("h", [P, NT, D])
        agg = sb("agg", [P, NT, D + ZW])
        agg_flat = agg[:, :, :].rearrange("p b c -> p (b c)")
        tmp = agg_flat[:, 0:NPAD].rearrange("p (b d) -> p b d", d=D)
        tmp2 = agg_flat[:, NPAD:2 * NPAD].rearrange("p (b d) -> p b d", d=D)
        self_term = sb("self_term", [P, NT, D])
        hT = sb("hT", [P, 2 * ROUNDS, D])
        hT_tile = [sb(f"hT_tile{k}", [P, D]) for k in range(2)]
        gat = sb("gat", [P, NT, ZW])
        local = sb("local", [P, TILES])
        minus_local = sb("minus_local", [P, TILES])
        weight = sb("weight", [P, TILES])
        src_row = sb("src_row", [P, TILES + G], u32)
        rel_row = sb("rel_row", [P, TILES + G], u32)
        dst_tile = sb("dst_tile", [P, TILES])
        at_sums = sb("at_sums", [P, TILES], i32)
        at_er_top = sb("at_er_top", [P, TILES], i32)
        at_agg = sb("at_agg", [P, TILES], i32)
        ring = [sb(f"ring{j}", [P, G, ZW]) for j in range(RING)]
        index = [sb(f"index{j}", [P, G], u32) for j in range(RING)]
        onehot = [sb(f"onehot{k}", [P, G, P]) for k in range(2)]
        work = [sb(f"work{k}", [P, 2 * G * ZW]) for k in range(2)]
        z_in = [w[:, 0:G * ZW].rearrange("p (g c) -> p g c", c=ZW) for w in work]
        z_msg = [w[:, G * ZW:2 * G * ZW].rearrange("p (g c) -> p g c", c=ZW) for w in work]
        stage = [w[:, 0:R * D] for w in work]
        member = [sb(f"member{k}", [P, G, P], bf16) for k in range(2)]
        score = [sb(f"score{k}", [P, G, HEADS]) for k in range(2)]
        el_parts = [sb(f"el_parts{k}", [P, G, ROWS], bf16) for k in range(2)]
        elT = [sb(f"elT{k}", [P, G // BLOCKS, HEADS, P], bf16) for k in range(2)]
        stat = sb("stat", [P, 8, NT])
        er = sb("er", [P, NT, HEADS])
        el = sb("el", [P, NT, HEADS])
        top = sb("top", [P, NT, HEADS])
        tile_top = sb("tile_top", [P, TILES, HEADS])
        run_top = agg_flat[:, 0:TILES * HEADS].rearrange("p (t h) -> p t h", h=HEADS)
        new_tile = sb("new_tile", [P, TILES])
        last_tile_i = sb("last_tile_i", [P, NT], i32)
        er_top = sb("er_top", [P, NT, 3, 2 * HEADS], bf16)
        er_top_flat = er_top[:, :, :, :].rearrange("p b n c -> p (b n c)")
        sc = sb("sc", [P, NT, HEADS])
        in_norm = sb("in_norm", [P, NT])
        in_norm0 = sb("in_norm0", [P, NT])
        out_norm = sb("out_norm", [P, NT])
        w_names = ["L0_gnn_W", "L3_gnn_W1", "L3_gnn_W2"]
        wt = {n: sb("s_" + n, [D, D]) for n in w_names}
        w0T = sb("w0T", [D, D])
        w_rel = sb("w_rel", [D, R, D])
        w_loop = sb("w_loop", [D, L, D])
        w_gat = sb("w_gat", [D, L, D + 2 * HEADS])
        w_fuse = sb("w_fuse", [D, 2, D])
        w_gate = sb("w_gate", [D, D])
        LATE_LOADS = 2 + 3 + 7 + 5 + 5
        rows = ["L0_gnn_ln_gamma", "L0_gnn_ln_beta", "L0_gnn_b", "L2_gnn_b_fuse", "L2_gnn_b_gate",
                "L3_gnn_b1", "L3_gnn_b2"]
        row = {n: sb("r_" + n, [P, D]) for n in rows}
        gate_row = sb("gate_row", [P, D])
        by_layer = ["L2_gnn_b_rel", "L2_gnn_b_gat", "L2_gnn_attn_l", "L2_gnn_attn_r"]
        b_rel, b_gat, attn_l, attn_r = layer_rows = [sb("r_" + n, [P, L, D]) for n in by_layer]
        weight_sum = sb("weight_sum", [P, 1])
        weight_mean = sb("weight_mean", [P, 1])

        def flat(t):
            return t[:, :, :].rearrange("p a b -> p (a b)")

        raw = agg_flat[:, 0:NPAD]
        src_i = raw[0:EP, 0:EC].bitcast(i32)
        dst_i = raw[0:EP, EC:2 * EC].bitcast(i32)
        typ_i = raw[0:EP, 2 * EC:3 * EC].bitcast(i32)
        w_in = raw[0:EP, 3 * EC:4 * EC]
        dtile_i = raw[0:EP, 4 * EC:5 * EC].bitcast(i32)
        dtile = raw[0:EP, 5 * EC:6 * EC]
        stile = raw[0:EP, 6 * EC:7 * EC]
        slow = raw[0:EP, 7 * EC:8 * EC]
        raw2 = agg_flat[:, NPAD:2 * NPAD]
        dlow = raw2[0:EP, 0:EC]
        hit = raw2[0:EP, EC:2 * EC]
        run = raw2[0:EP, 2 * EC:3 * EC]
        pos = raw2[0:EP, 3 * EC:4 * EC]
        slot_i = raw2[0:EP, 4 * EC:5 * EC].bitcast(i32)
        hi_i = raw2[0:EP, 5 * EC:6 * EC].bitcast(i32)
        slot = flat(gat)[0:EP, 4 * EC:5 * EC].bitcast(u32)
        tmp_i = raw2[0:EP, 7 * EC:8 * EC].bitcast(i32)
        rec = flat(gat)[0:EP, 0:4 * EC].rearrange("p (c f) -> p c f", f=4)
        blank = flat(self_term)[:, 0:4 * TILES].rearrange("p (c f) -> p c f", f=4)
        grouped = flat(h)[:, 0:4 * TILES].rearrange("p (c f) -> p c f", f=4)
        local_T = flat(gat)[0:TILES // 4, 0:4 * P].rearrange("p (k e) -> p k e", k=4)
        put_rec = [sb(f"put_rec{k}", [P, G, 4]) for k in range(2)]
        src_low = [flat(onehot[k]).bitcast(bf16)[0:EP, 0:G * P].rearrange("p (g n) -> p g n", g=G)
                   for k in range(2)]
        dst_low = [flat(onehot[k]).bitcast(bf16)[0:EP, G * P:2 * G * P].rearrange("p (g n) -> p g n", g=G)
                   for k in range(2)]
        src_high = [flat(z_in[k]).bitcast(bf16)[0:EP, 0:G * NT].rearrange("p (g n) -> p g n", g=G)
                    for k in range(2)]
        dst_high = [flat(z_in[k]).bitcast(bf16)[0:EP, G * NT:2 * G * NT].rearrange("p (g n) -> p g n", g=G)
                    for k in range(2)]
        total = sb("total", [P, NT])
        tiles_i = sb("tiles_i", [P, NT], i32)
        tiles = sb("tiles", [P, NT])
        first_tile = sb("first_tile", [P, NT])
        before = sb("before", [P, NT])
        wide = [w[:, 0:G * P] for w in work]

        ps = ctx.enter_context(nc.psum_tensor("ps", [P, 4096], f32))
        sums = ps[:, 0:NPAD]
        sums3 = sums.rearrange("p (b d) -> p b d", d=D)
        er_top_ps = [ps[:, 3072 + 512 * k:3072 + 512 * k + 2 * G * HEADS]
                     .rearrange("p (g c) -> p g c", c=2 * HEADS) for k in range(2)]
        msg_ps = [ps[:, 512 * k:512 * k + D + ZW] for k in range(MSG_SLOTS)]
        el_ps = [ps[:, 1024 * s:1024 * (s + 1)].rearrange("p (g h e) -> p g h e", g=2, h=HEADS) for s in range(PAIRS)]
        elT_ps = [ps[:, 2048 + 512 * k:2048 + 512 * k + G // BLOCKS * P // 2].bitcast(bf16)
                  .rearrange("p (q e) -> p q e", e=P) for k in range(2)]
        rel_ps = ps[:, 3072:4096]

        def chunk(c):
            return slice(c * CHUNK, min((c + 1) * CHUNK, NT))

        def chunk_ps(bank, c, width=D):
            tiles_here = min(CHUNK, NT - c * CHUNK)
            return ps[:, 512 * bank:512 * bank + tiles_here * width].rearrange("p (b d) -> p b d", d=width)

        SELF_BANK, GAT_BANK, FUSED_BANK, H_BANK, Z_BANK, GATE_BANK, HC_BANK = range(7)
        turned_sums = [[t[:, n * CHUNK:(n + 1) * CHUNK, :] for n in range(2)] for t in onehot]
        gate = [w[:, 0:CHUNK * D].rearrange("p (b d) -> p b d", d=D) for w in work]

        loads = sem("loads")
        late_loads = sem("late_loads")
        constants = sem("constants")
        blank_ready = sem("blank_ready")
        blank_stored = sem("blank_stored")
        slots_ready = sem("slots_ready")
        put_staged = sem("put_staged")
        put_done = pair("put_done")
        grouped_loaded = sem("grouped_loaded")
        degree_hot = pair("degree_hot")
        degree_used = pair("degree_used")
        pe_go = sem("pe_go")
        pe_done = sem("pe_done")
        act_go = sem("act_go")
        act_done = sem("act_done")
        dve = sem("dve")
        local_ready = sem("local_ready")
        local_stored = sem("local_stored")
        wide_in = pair("wide_in")
        wide_used = pair("wide_used")
        member_made = pair("member_made")
        member_free = pair("member_free")
        member_out = pair("member_out")
        gathered = [sem(f"gathered{j}") for j in range(RING)]
        group_done = [sem(f"group_done{j}") for j in range(RING)]
        index_staged = sem("index_staged")
        onehot_ready = pair("onehot_ready")
        pass_go = sem("pass_go")
        rows_ready = sem("rows_ready")
        rows_stored = sem("rows_stored")
        hT_staged = sem("hT_staged")
        rel_ps_full = sem("rel_ps_full")
        rel_taken = sem("rel_taken")
        rel_stored = pair("rel_stored")
        member_in = pair("member_in")
        z_stored = [sem(f"z_stored{j}") for j in range(RING)]
        z_loaded = pair("z_loaded")
        el_split = pair("el_split")
        elT_ps_ready = pair("elT_ps_ready")
        elT_ready = pair("elT_ready")
        el_wide = sem("el_wide")
        el_taken = sem("el_taken")
        er_top_ready = pair("er_top_ready")
        er_top_taken = pair("er_top_taken")
        score_ready = pair("score_ready")
        exp_ready = pair("exp_ready")
        msg_ready = pair("msg_ready")
        z_sum = sem("z_sum")
        z_added = sem("z_added")
        pool_passed = sem("pool_passed")
        sums_made, sums_turned, sums_back = sem("sums_made"), sem("sums_turned"), sem("sums_back")
        fused = sem("fused")
        hc_made, hc_turned, hc_back = sem("hc_made"), sem("hc_turned"), sem("hc_back")
        gate_sum, gate_in, gate_out = sem("gate_sum"), sem("gate_in"), sem("gate_out")
        h_made, h_turned, h_back = sem("h_made"), sem("h_turned"), sem("h_back")
        z_made, z_taken = sem("z_made"), sem("z_taken")
        layer_loads = sem("layer_loads")
        layer_free = sem("layer_free")
        stored = sem("stored")
        grouped_ready = sem("grouped_ready")
        act_passed = sem("act_passed")
        squared = sem("squared")
        clipped = sem("clipped")
        dve_passed = sem("dve_passed")

        block = ctx.enter_context(nc.Block())

        def spread(ap, n):
            return ap.unsqueeze(len(ap.shape)).to_broadcast([*ap.shape, n])

        def across(row_ap, n):
            return row_ap.unsqueeze(1).to_broadcast([row_ap.shape[0], n, row_ap.shape[1]])

        HALVES = range(2)
        def destinations(engine, columns, width, i, j):
            _, found = nc.values_load_multi_w_load_instructions(
                columns[0:1, bass.ds((i * RING + j) * G, G)], engines=[engine], min_val=0, max_val=width * (NT - 1),
                skip_runtime_bounds_check_because="a count of at most NT - 1 starts of tiles, times the width")
            return found

        LINEAR, MAXIMA, SUMS = "linear", "maxima", "sums"
        ORDER = [LINEAR] * 3 + [MAXIMA, SUMS] * L + [LINEAR] * 2
        WEIGHTED = [True, False, False] + [False, False] * L + [True, True]

        def rounds_before(p, *kinds):
            return sum(ROUNDS for k in ORDER[:p] if k in kinds)

        def half_before(i, j, before_p):
            if j >= 2:
                return group_done[j - 2], i + (before_p + 2)
            return group_done[j + 2], i + (before_p + 1)

        H_LAG = [0, 5, 2]

        @block.sync
        def _(sp):
            e_view = lambda ap: ap.rearrange("(p c) -> p c", p=EP)
            sp.dma_start(dst_i, e_view(a["dst"])).then_inc(loads, 16)
            sp.dma_start(src_i, e_view(a["src"])).then_inc(loads, 16)
            sp.dma_start(typ_i, e_view(a["edge_type_16"])).then_inc(loads, 16)
            sp.dma_start(w_in, e_view(a["edge_weight"])).then_inc(loads, 16)
            full = (NT - 1) * P
            sp.dma_start(x[:, 0:NT - 1, :], a["x"][0:full, :].rearrange("(b p) d -> p b d", p=P)).then_inc(late_loads, 16)
            sp.wait_ge(constants, 1)
            sp.dma_start(x[0:N - full, NT - 1, :], a["x"][full:N, :]).then_inc(late_loads, 16)
            for n in w_names:
                sp.dma_start(wt[n][:, :], a[n]).then_inc(late_loads, 16)
            for n in rows:
                sp.dma_start(row[n][:, :], a[n].partition_broadcast(P)).then_inc(late_loads, 16)
            sp.dma_start(w_loop[:, :, :], a["L2_gnn_W_loop"].rearrange("l d o -> d l o")).then_inc(late_loads, 16)
            for n, to in zip(by_layer, layer_rows):
                of_n = a[n] if len(a[n].shape) == 2 else a[n].rearrange("l h d -> l (h d)")
                sp.dma_start(to[:, :, :].rearrange("p l d -> p (l d)"), of_n.rearrange("l d -> (l d)").partition_broadcast(P)).then_inc(late_loads, 16)
            sp.dma_start(w_rel[:, :, :], a["L2_gnn_W_rel"][0].rearrange("r d o -> d r o")).then_inc(late_loads, 16)
            sp.dma_start(w_gat[:, :, 0:D], a["L2_gnn_W_gat"].rearrange("l d o -> d l o")).then_inc(late_loads, 16)
            sp.dma_start(w_fuse[:, :, :], a["L2_gnn_W_fuse"].rearrange("(k d) o -> d k o", k=2)).then_inc(late_loads, 16)
            sp.dma_start(w_gate[:, :], a["L2_gnn_W_gate"][0:D, :]).then_inc(late_loads, 16)
            sp.dma_start(gate_row[:, :], a["L2_gnn_W_gate"][D:D + 1, :].squeeze(0).partition_broadcast(P)).then_inc(late_loads, 16)
            sp.wait_ge(blank_ready, 1)
            sp.dma_start(records.rearrange("(e t) f -> e t f", e=P), blank).then_inc(blank_stored, 16)
            sp.wait_ge(put_done[0], DEG_ITERS * G * 16)
            sp.wait_ge(put_done[1], DEG_ITERS * G * 16)
            sp.dma_start(grouped, records.rearrange("(e t) f -> e t f", e=P)).then_inc(grouped_loaded, 16)
            sp.wait_ge(local_ready, 1)
            sp.dma_start(local_rows.rearrange("(k t e) -> t k e", k=4, e=P), local_T).then_inc(local_stored, 16)

            def store_rows(table, view, k):
                for n, part_of in enumerate(PARTS):
                    sp.wait_ge(rows_ready, 2 * (k - 1) + n + 1)
                    sp.dma_start(table.rearrange("(b p) d -> p b d", p=P)[:, part_of, :], view[:, part_of, :]).then_inc(rows_stored, 16)

            count = 0
            for p, kind in enumerate(ORDER):
                if kind == LINEAR:
                    count += 1
                    store_rows(node_rows, tmp[:, :, :], count)
                if p == 0:
                    sp.wait_ge(local_stored, 16)
                    with sp.Fori(0, 2 * ROUNDS) as i:
                        for k in HALVES:
                            sp.wait_ge(wide_used[k], i + 1)
                            sp.dma_start(wide[k], local_rows[bass.ds((i * 2 + k) * (G * P), G * P)].partition_broadcast(P)).then_inc(wide_in[k], 16)
                if kind == MAXIMA:
                    count += 1
                    store_rows(attention_rows, gat[:, :, :], count)
                    before_p = rounds_before(p, LINEAR, MAXIMA, SUMS)
                    before_m = rounds_before(p, MAXIMA)
                    with sp.Fori(0, ROUNDS) as i:
                        for j in range(RING):
                            sp.wait_ge(gathered[j], i * (16 * G) + (before_p + 1) * 16 * G)
                            sp.dma_start(edge_z[:, bass.ds((i * RING + j) * (G * ZW), G * ZW)], flat(ring[j])).then_inc(z_stored[j], 16)
                            if j % 2:
                                sp.wait_ge(rel_taken, i * RING + (before_m * RING + j + 2))
                                sp.dma_start(relation_rows[bass.ds((i * 2 + j // 2) * (P * R), P * R), :].rearrange("(p r) d -> p (r d)", p=P),
                                             stage[j // 2]).then_inc(rel_stored[j // 2], 16)
                if kind == SUMS:
                    before_p = rounds_before(p, LINEAR, MAXIMA, SUMS)
                    l = rounds_before(p, SUMS) // ROUNDS
                    if l < L - 1:
                        sp.wait_ge(layer_free, l + 1)
                        sp.dma_start(w_rel[:, :, :], a["L2_gnn_W_rel"][l + 1].rearrange("r d o -> d r o")).then_inc(layer_loads, 16)
                    for j in range(RING):
                        sp.wait_ge(z_stored[j], rounds_before(p, MAXIMA) * 16)
                    for k in HALVES:
                        sp.wait_ge(rel_stored[k], rounds_before(p, MAXIMA) * 16)
                    for j in range(RING):
                        sp.wait_ge(group_done[j], before_p + 1)
                    before_s = rounds_before(p, SUMS)

                    def load_member(i, j):
                        sp.wait_ge(er_top_ready[j % 2], i * 2 + (before_s * 2 + j // 2 + 1))
                        sp.dma_start(flat(member[j % 2]), member_d[:, bass.ds((i * RING + j) * (G * P), G * P)]).then_inc(member_in[j % 2], 16)

                    def load_round(i, last_round):
                        for j in range(RING):
                            if j < RING - 1:
                                load_member(i, j + 1)
                            elif not last_round:
                                load_member(i + 1, 0)
                            sp.wait_ge(msg_ready[j % 2], i * 2 + (before_s * 2 + j // 2 + 1))
                            sp.dma_start(flat(z_in[j % 2]), edge_z[:, bass.ds((i * RING + j) * (G * ZW), G * ZW)]).then_inc(z_loaded[j % 2], 16)

                    load_member(0, 0)
                    with sp.Fori(0, ROUNDS - 1) as i:
                        load_round(i, False)
                    load_round(ROUNDS - 1, True)
            sp.wait_ge(rows_ready, 2 * count + 1)
            sp.dma_start(out[0:full, :].rearrange("(b p) d -> p b d", p=P), x[:, 0:NT - 1, :]).then_inc(stored, 16)
            sp.dma_start(out[full:N, :], x[0:N - full, NT - 1, :]).then_inc(stored, 16)
            sp.wait_ge(stored, 32)


        @block.gpsimd
        def _(pool):
            def passed():
                nc.gpsimd.sem_inc(pool_passed, 1)

            nc.gpsimd.iota(lane[:, :], [[1, P]], base=0, channel_multiplier=0, allow_small_or_imprecise_dtypes=True)
            nc.gpsimd.iota(part[:, :], [[0, 1]], base=0, channel_multiplier=1, allow_small_or_imprecise_dtypes=True)
            nc.gpsimd.iota(tile_no[:, :], [[1, TILES]], base=0, channel_multiplier=0, allow_small_or_imprecise_dtypes=True)
            nc.gpsimd.memset(x[:, NT - 1, :], 0.0)
            nc.gpsimd.memset(blank, 0.0)
            nc.gpsimd.drain()
            nc.gpsimd.memset(blank[:, :, 1:2], -1.0)
            nc.gpsimd.drain().then_inc(constants, 1)
            pool.wait_ge(constants, 1)
            pool.wait_ge(blank_stored, 16)
            pool.wait_ge(slots_ready, 1)
            staged = Steps(index_staged)

            def stage_put(i, k):
                cols = bass.ds(i * (2 * G) + k * G, G)
                nc.gpsimd.tensor_copy(index[k][0:EP, :], slot[:, cols]).then_inc(index_staged, 1)
                nc.gpsimd.tensor_copy(put_rec[k][0:EP, :, :], rec[:, cols, :]).then_inc(index_staged, 1)
                pool.wait_ge(index_staged, staged.add(2))
                passed()
                for g in range(G):
                    nc.gpsimd.indirect_dma_start(
                        out=records, out_offset=bass.IndirectOffsetOnAxis(ap=index[k][0:EP, g:g + 1], axis=0),
                        in_=put_rec[k][0:EP, g, :], in_offset=None).then_inc(put_done[k], 16)

            for k in HALVES:
                stage_put(0, k)
            staged_first = staged.now
            with pool.Fori(1, DEG_ITERS) as i:
                staged.now = i * 4
                for k in HALVES:
                    pool.wait_ge(put_done[k], i * (16 * G))
                    passed()
                    stage_put(i, k)
            staged.now = staged_first * DEG_ITERS

            pool.wait_ge(grouped_ready, 1)
            stores = 0
            for p, kind in enumerate(ORDER):
                before_p = rounds_before(p, LINEAR, MAXIMA, SUMS)
                before_m = rounds_before(p, MAXIMA)
                table, rows_of, width = {LINEAR: (node_rows, src_row, D), MAXIMA: (attention_rows, src_row, ZW),
                                         SUMS: (relation_rows, rel_row, D)}[kind]

                def stage_index(group, j):
                    nc.gpsimd.tensor_copy(index[j][:, :], rows_of[:, bass.ds(group * G, G)]).then_inc(index_staged, 1)
                    return staged.add()

                def gather_round(i, first):
                    for j in range(RING):
                        ahead = (j + 1) % RING
                        here = staged.now
                        if p or not first or ahead == 0:
                            pool.wait_ge(gathered[ahead], i * (16 * G) + (before_p + (j + 1) // RING) * 16 * G)
                            passed()
                        stage_index(i * RING + (j + 1), ahead)
                        pool.wait_ge(group_done[j], i + (before_p + 1))
                        passed()
                        if kind == MAXIMA and not first:
                            pool.wait_ge(z_stored[j], i * 16 + before_m * 16)
                            passed()
                        pool.wait_ge(index_staged, here)
                        passed()
                        for g in range(G):
                            nc.gpsimd.indirect_dma_start(
                                out=ring[j][:, g, 0:width], out_offset=None, in_=table,
                                in_offset=bass.IndirectOffsetOnAxis(ap=index[j][:, g:g + 1], axis=0)).then_inc(gathered[j], 16)

                if kind in (LINEAR, MAXIMA):
                    stores += 1
                    pool.wait_ge(rows_stored, 32 * stores)
                if kind == SUMS:
                    for k in HALVES:
                        pool.wait_ge(rel_stored[k], 16 * before_m)
                    for j in range(RING):
                        pool.wait_ge(z_stored[j], 16 * before_m)
                pool.wait_ge(group_done[0], before_p + 1)
                if p:
                    pool.wait_ge(index_staged, staged.now)
                stage_index(0, 0)
                base = staged.now
                first = 0
                if kind == MAXIMA or p == 0:
                    gather_round(0, True)
                    first = 1
                with pool.Fori(first, ROUNDS) as i:
                    staged.now = i * RING + base
                    gather_round(i, False)
                staged.now = base + RING * ROUNDS

        @block.scalar
        def _(act):
            def passed():
                nc.scalar.sem_inc(act_passed, 1)

            asked = [0]

            def asked_for():
                asked[0] += 1
                act.wait_ge(act_go, asked[0])

            def norm_root():
                asked_for()
                nc.scalar.activation(stat[:, 3, :], stat[:, 2, :], ACT.Sqrt).then_inc(act_done, 1)

            def back(to, bank, c, n, turned, done):
                act.wait_ge(turned, n + c + 1)
                nc.scalar.copy(to[:, chunk(c), :], chunk_ps(bank, c)).then_inc(done, 1)

            def node_stage(l):
                for s in range(CHUNKS + 6):
                    c = s
                    if l > 0 and c < CHUNKS:
                        n, wide_c = (l - 1) * CHUNKS, min(CHUNK, NT - c * CHUNK)
                        act.wait_ge(sums_turned, n + c + 1)
                        nc.scalar.copy(turned_sums[c % 2][0][:, 0:wide_c, :], chunk_ps(SELF_BANK, c))
                        nc.scalar.copy(turned_sums[c % 2][1][:, 0:wide_c, :], chunk_ps(GAT_BANK, c)).then_inc(sums_back, 1)
                    if l == 1 and 0 <= s - 2 < CHUNKS:
                        back(hT, HC_BANK, s - 2, 0, hc_turned, hc_back)
                    if l == 1 and 0 <= s - 3 < CHUNKS:
                        c = s - 3
                        act.wait_ge(gate_in, c + 1)
                        here = gate[c % 2][:, 0:min(CHUNK, NT - c * CHUNK), :]
                        nc.scalar.activation(here, here, ACT.Sigmoid).then_inc(gate_out, 1)
                    c = s - H_LAG[l] if l < L else -1
                    if 0 <= c < CHUNKS:
                        back(hT, H_BANK, c, l * CHUNKS, h_turned, h_back)

            asked_for()
            nc.scalar.activation(stat[:, 4:6, :], stat[:, 6:8, :], ACT.Sqrt).then_inc(act_done, 1)
            norm_root()
            with act.Fori(0, 2 * ROUNDS) as i:
                for k in HALVES:
                    cols = bass.ds((i * 2 + k) * (G * P), G * P)
                    act.wait_ge(member_made[k], i + 1)
                    passed()
                    act.dma_start(member_d[:, cols], flat(member[k])).then_inc(member_out[k], 16)
                for k in HALVES:
                    act.wait_ge(member_out[k], i * 16 + 16)
                    nc.scalar.sem_inc(member_free[k], 1)
            for p, kind in enumerate(ORDER):
                l = rounds_before(p, MAXIMA) // ROUNDS
                before_p = rounds_before(p, LINEAR, MAXIMA, SUMS)
                before_m, before_s = rounds_before(p, MAXIMA), rounds_before(p, SUMS)
                if kind == MAXIMA:
                    if l == 0:
                        node_stage(0)

                    def rows_back(i, j):
                        k = j % 2
                        act.wait_ge(elT_ps_ready[k], i * 2 + (before_m * 2 + j // 2 + 1))
                        for head in range(HEADS):
                            last = nc.scalar.activation(elT[k][:, :, head, :], elT_ps[k], ACT.Copy, scale=of_head[:, head:head + 1])
                        last.then_inc(elT_ready[k], 1)

                    def maxima_round(i, first, last_round):
                        for j in range(RING):
                            k, s = j % 2, j // 2
                            if k == 0:
                                nc.scalar.copy(hT_tile[s][:, :], hT[:, bass.ds(i * 2 + s, 1), :]).then_inc(hT_staged, 1)
                            if j < RING - 1:
                                rows_back(i, j + 1)
                            elif not last_round:
                                rows_back(i + 1, 0)
                            if k == 0 and not first:
                                act.wait_ge(rel_stored[s], i * 16 + before_m * 16)
                                passed()
                            elif k == 0 and before_m:
                                act.wait_ge(rel_stored[s], before_m * 16)
                            act.wait_ge(rel_ps_full, i * RING + (before_m * RING + j + 1))
                            nc.scalar.copy(stage[s][:, 1024 * k:1024 * (k + 1)], rel_ps).then_inc(rel_taken, 1)

                    act.wait_ge(pass_go, p + 1)
                    rows_back(0, 0)
                    maxima_round(0, True, False)
                    with act.Fori(1, ROUNDS - 1) as i:
                        maxima_round(i, False, False)
                    maxima_round(ROUNDS - 1, False, True)
                if kind == SUMS:
                    with act.Fori(0, ROUNDS) as i:
                        for j in range(RING):
                            k = j % 2
                            act.wait_ge(score_ready[k], i * 2 + (before_s * 2 + j // 2 + 1))
                            nc.scalar.activation(score[k][:, :, :], score[k][:, :, :], ACT.Relu).then_inc(clipped, 1)
                            act.wait_ge(clipped, i * RING + (before_s * RING + j + 1))
                            passed()
                            nc.scalar.activation(score[k][:, :, :], score[k][:, :, :], ACT.Exp, scale=-1.0).then_inc(exp_ready[k], 1)
                            act.wait_ge(*half_before(i, j, before_p))
                            passed()
                            for g in range(G):
                                nc.scalar.activation(onehot[k][:, g, :], lane[:, :], ACT.Square,
                                                     bias=minus_local[:, bass.ds((i * RING + j) * G + g, 1)]).then_inc(squared, 1)
                            act.wait_ge(squared, i * (RING * G) + (before_s * RING * G + (j + 1) * G))
                            nc.scalar.activation(flat(onehot[k]), flat(onehot[k]), ACT.Relu, bias=ones[:, 0:1], scale=-1.0).then_inc(onehot_ready[k], 1)
                    node_stage(l)
                    if l == L:
                        norm_root()
                if kind == LINEAR and p in (0, 2, len(ORDER) - 1):
                    norm_root()

        @block.tensor
        def _(pe):
            asked = [0]

            def asked_for():
                asked[0] += 1
                pe.wait_ge(pe_go, asked[0])

            def transpose_nodes(src):
                asked_for()
                for b in range(NT):
                    last = nc.tensor.transpose(sums3[:, b, :], src[:, b, 0:D], ident[:, :])
                last.then_inc(pe_done, 1)

            def multiply_nodes(*pairs):
                asked_for()
                for b in range(NT):
                    for n, (turned, w) in enumerate(pairs):
                        last = nc.tensor.matmul(sums3[:, b, :], turned[:, b, :], w, start=n == 0, stop=n == len(pairs) - 1)
                last.then_inc(pe_done, 1)

            def turn_chunk(src, bank, c, done):
                for b in range(NT)[chunk(c)]:
                    last = nc.tensor.transpose(chunk_ps(bank, c)[:, b - c * CHUNK, :], src[:, b, 0:D], ident[:, :])
                if done:
                    last.then_inc(done, 1)

            def node_stage(l):
                for s in range(CHUNKS + 7):
                    h_c = s - H_LAG[l] if l < L else -1
                    c = h_c - 1
                    if l < L and 0 <= c < CHUNKS:
                        pe.wait_ge(h_back, l * CHUNKS + c + 1)
                        if c:
                            pe.wait_ge(z_taken, l * CHUNKS + c)
                        for b in range(NT)[chunk(c)]:
                            last = nc.tensor.matmul(chunk_ps(Z_BANK, c, D + 2 * HEADS)[:, b - c * CHUNK, :], hT[:, b, :], w_gat[:, l, :], start=True, stop=True)
                        last.then_inc(z_made, 1)
                    if 0 <= h_c < CHUNKS:
                        pe.wait_ge(h_made, l * CHUNKS + h_c + 1)
                        turn_chunk(h if l else x, H_BANK, h_c, h_turned)
                    c = s - 3
                    if l == 1 and 0 <= c < CHUNKS:
                        pe.wait_ge(hc_back, c + 1)
                        if c:
                            pe.wait_ge(gate_in, c)
                        for b in range(NT)[chunk(c)]:
                            last = nc.tensor.matmul(chunk_ps(GATE_BANK, c)[:, b - c * CHUNK, :], hT[:, b, :], w_gate[:, :], start=True, stop=True)
                        last.then_inc(gate_sum, 1)
                    c = s - 2
                    if l == 1 and 0 <= c < CHUNKS:
                        pe.wait_ge(hc_made, c + 1)
                        turn_chunk(h, HC_BANK, c, hc_turned)
                    c = s - 1
                    if l > 0 and 0 <= c < CHUNKS:
                        pe.wait_ge(sums_back, (l - 1) * CHUNKS + c + 1)
                        if c:
                            pe.wait_ge(*((hc_made, c) if l == 1 else (h_made, l * CHUNKS + c)))
                        for b in range(NT)[chunk(c)]:
                            for n in range(2):
                                last = nc.tensor.matmul(chunk_ps(FUSED_BANK, c)[:, b - c * CHUNK, :], turned_sums[c % 2][n][:, b - c * CHUNK, :],
                                                        w_fuse[:, n, :], start=n == 0, stop=n == 1)
                        last.then_inc(fused, 1)
                    c = s
                    if l > 0 and c < CHUNKS:
                        pe.wait_ge(sums_made, (l - 1) * CHUNKS + c + 1)
                        turn_chunk(self_term, SELF_BANK, c, None)
                        turn_chunk(gat, GAT_BANK, c, sums_turned)

            def clear(width):
                for at in range(0, width, 512):
                    n = min(512, width - at)
                    last = nc.tensor.matmul(ps[:, at:at + n], zeros_b[:, 0:P], zeros_b[:, 0:n], start=True, stop=True)
                return last

            asked_for()
            nc.tensor.matmul(ps[0:EP, 0:NT], below[0:EP, 0:EP], total[0:EP, :], start=True, stop=True)
            nc.tensor.matmul(ps[:, 512:512 + NT], ones[0:EP, :], total[0:EP, :], start=True, stop=True).then_inc(pe_done, 1)
            asked_for()
            for at in (0, 512):
                nc.tensor.matmul(ps[:, at:at + NT], zeros_b[:, 0:P], zeros_b[:, 0:NT], start=True, stop=True)
            with pe.Fori(0, DEG_ITERS) as i:
                for k in HALVES:
                    pe.wait_ge(degree_hot[k], i + 1)
                    for g in range(G):
                        nc.tensor.matmul(ps[:, 0:NT], src_low[k][:, g, :], src_high[k][:, g, :], start=False, stop=True, skip_group_check=True)
                        last = nc.tensor.matmul(ps[:, 512:512 + NT], dst_low[k][:, g, :], dst_high[k][:, g, :], start=False, stop=True, skip_group_check=True)
                    last.then_inc(degree_used[k], 1)
            nc.tensor.matmul(ps[:, 1024:1025], ones[0:EP, :], weight_sum[0:EP, :], start=True, stop=True).then_inc(pe_done, 1)
            asked_for()
            nc.tensor.transpose(ps[:, 0:P], wt["L0_gnn_W"][:, :], ident[:, :]).then_inc(pe_done, 1)

            def tiles_of(i, j):
                return destinations(mybir.EngineType.PE, *((at_sums, D) if kind == LINEAR else (at_er_top, 6 * HEADS)), i, j)

            passes = [0]

            def start_pass():
                passes[0] += 1
                pe.wait_ge(pass_go, passes[0])

            transpose_nodes(tmp)
            multiply_nodes((hT, w0T[:, :]))
            asked_for()
            quarter = TILES // 4
            for q in range(4):
                last = nc.tensor.transpose(ps[0:quarter, P * q:P * (q + 1)], local[:, quarter * q:quarter * (q + 1)], ident[:, :])
            last.then_inc(pe_done, 1)
            for p, kind in enumerate(ORDER):
                before_p = rounds_before(p, LINEAR, MAXIMA, SUMS)
                before_m, before_s = rounds_before(p, MAXIMA), rounds_before(p, SUMS)
                before_hot = rounds_before(p, LINEAR, SUMS)
                l = before_m // ROUNDS
                if kind == MAXIMA:
                    if l == 0:
                        node_stage(0)
                    multiply_nodes((hT, w_loop[:, l, :]))
                    if l:
                        pe.wait_ge(layer_loads, 16 * l)
                start_pass()
                if kind == LINEAR:
                    clear(NPAD)
                    with pe.Fori(0, ROUNDS) as i:
                        for j in range(RING):
                            k = j % 2
                            columns = tiles_of(i, j)
                            pe.wait_ge(gathered[j], i * (16 * G) + (before_p + 1) * 16 * G)
                            pe.wait_ge(onehot_ready[k], i * 2 + (before_hot * 2 + j // 2 + 1))
                            for g in range(G):
                                last = nc.tensor.matmul(sums[:, bass.ds(columns[g], D)], onehot[k][:, g, :], ring[j][:, g, 0:D],
                                                        start=False, stop=True, skip_group_check=True)
                            last.then_inc(group_done[j], 1)
                if kind == MAXIMA:
                    def turn_edges(i, j):
                        k = j % 2
                        pe.wait_ge(el_split[k], i * 2 + (before_m * 2 + j // 2 + 1))
                        for q in range(G // BLOCKS):
                            last = nc.tensor.transpose(elT_ps[k][:, q, :], flat(el_parts[k])[:, q * P:(q + 1) * P], ident_b[:, :])
                        last.then_inc(elT_ps_ready[k], 1)

                    def relation_quarter(i, j, q):
                        if q == 0:
                            pe.wait_ge(hT_staged, i * 2 + (before_m * 2 + j // 2 + 1))
                            pe.wait_ge(rel_taken, i * RING + (before_m * RING + j + 1))
                        first = R // 2 * (j % 2) + 4 * q
                        made = nc.tensor.matmul(rel_ps[:, 512 * q:512 * (q + 1)], hT_tile[j // 2][:, :],
                                                w_rel[:, first:first + 4, :], start=True, stop=True)
                        if q == 1:
                            made.then_inc(rel_ps_full, 1)

                    def maxima_round(i, last_round):
                        for j in range(RING):
                            k = j % 2
                            pe.wait_ge(elT_ready[k], i * 2 + (before_m * 2 + j // 2 + 1))
                            for g in range(G):
                                pair, s = el_ps[g // 2 % PAIRS], g % 2
                                if s == 0:
                                    pe.wait_ge(el_taken, i * (RING * G // 2) + ((before_m * RING + j) * G // 2 + g // 2 + 1))
                                last = nc.tensor.matmul(pair[:, s, :, :], pick[:, g % BLOCKS, :], elT[k][:, g // BLOCKS, :, :],
                                                        start=True, stop=True)
                                if s == 1:
                                    last.then_inc(el_wide, 1)
                                if g == 3:
                                    relation_quarter(i, j, 0)
                                if g == 5:
                                    if j < RING - 1:
                                        turn_edges(i, j + 1)
                                    elif not last_round:
                                        turn_edges(i + 1, 0)
                                    relation_quarter(i, j, 1)

                    turn_edges(0, 0)
                    with pe.Fori(0, ROUNDS - 1) as i:
                        maxima_round(i, False)
                    maxima_round(ROUNDS - 1, True)
                if kind == SUMS:
                    def edge_terms(i, j):
                        k = j % 2
                        columns = tiles_of(i, j)
                        for g in range(G):
                            yield
                            if g == 0:
                                pe.wait_ge(member_in[k], i * 32 + (before_s * 32 + (j // 2 + 1) * 16))
                                pe.wait_ge(er_top_taken[k], i * 2 + (before_s * 2 + j // 2 + 1))
                            for n in range(3):
                                last = nc.tensor.matmul(er_top_ps[k][:, g, :], member[k][:, g, :],
                                                        er_top_flat[:, bass.ds(columns[g] + n * 2 * HEADS, 2 * HEADS)],
                                                        start=n == 0, stop=n == 2)
                            if g == G - 1:
                                last.then_inc(er_top_ready[k], 1)

                    def sums_round(i, last_round):
                        for j in range(RING):
                            k = j % 2
                            terms = iter(())
                            if j == 0:
                                terms = edge_terms(i, 3)
                            elif not last_round:
                                terms = edge_terms(i + 1, j - 1)
                            next(terms, None)
                            pe.wait_ge(gathered[j], i * (16 * G) + (before_p + 1) * 16 * G)
                            pe.wait_ge(onehot_ready[k], i * 2 + (before_hot * 2 + j // 2 + 1))
                            pe.wait_ge(msg_ready[k], i * 2 + (before_s * 2 + j // 2 + 2))
                            for g in range(G):
                                pe.wait_ge(z_added, i * (RING * G) + ((before_s * RING + j) * G + g + 1))
                                slot_ps = msg_ps[g % MSG_SLOTS]
                                nc.tensor.matmul(slot_ps[:, 0:D], onehot[k][:, g, :], ring[j][:, g, 0:D], start=True, stop=True)
                                nc.tensor.matmul(slot_ps[:, D:D + ZW], onehot[k][:, g, :], z_msg[k][:, g, :], start=True, stop=True).then_inc(z_sum, 1)
                                next(terms, None)

                    for j in range(3):
                        for _ in edge_terms(0, j):
                            pass
                    with pe.Fori(0, ROUNDS - 1) as i:
                        sums_round(i, False)
                    sums_round(ROUNDS - 1, True)
                    node_stage(l)
                if kind == LINEAR and p > 2:
                    transpose_nodes(tmp)
                    multiply_nodes((hT, wt[f"L3_gnn_W{p - len(ORDER) + 3}"][:, :]))

        @block.vector
        def _(dve_):
            v = nc.vector
            steps = Steps(dve)

            def link(ins):
                ins.then_inc(dve, 1)
                dve_.wait_ge(dve, steps.add())

            def tell(s, k=1):
                v.sem_inc(s, k)

            asked = {"pe": 0, "act": 0}

            def ask_pe():
                tell(pe_go)
                asked["pe"] += 1
                dve_.wait_ge(pe_done, asked["pe"])

            def ask_act():
                tell(act_go)
                asked["act"] += 1
                dve_.wait_ge(act_done, asked["act"])

            for k in HALVES:
                for s in (wide_used, degree_used, member_free, er_top_taken, er_top_ready, msg_ready):
                    v.sem_inc(s[k], 1)
            for j in range(RING):
                v.sem_inc(group_done[j], 1)
            v.sem_inc(rel_taken, 1)
            v.sem_inc(el_taken, PAIRS)
            v.sem_inc(z_added, MSG_SLOTS)

            dve_.wait_ge(constants, 1)
            tell(blank_ready)
            v.memset(zeros_b[:, :], 0.0)
            v.memset(ones[:, :], 1.0)
            v.memset(hT[:, NT:2 * ROUNDS, :], 0.0)
            v.memset(src_row[:, TILES:TILES + G], 0)
            v.memset(rel_row[:, TILES:TILES + G], 0)
            for k in HALVES:
                v.memset(el_parts[k][:, :, NOT_BITS + BITS:ROWS], 0.0)
            v.tensor_scalar(ident[:, :], lane[:, :], part[:, :], None, ALU.is_equal)
            v.tensor_scalar(ident_b[:, :], lane[:, :], part[:, :], None, ALU.is_equal)
            v.tensor_scalar(below[:, :], lane[:, :], part[:, :], None, ALU.is_gt)
            dve_.wait_ge(loads, 64)
            v.tensor_copy(rec[:, :, 0], src_i)
            v.tensor_copy(rec[:, :, 1], dst_i)
            v.tensor_copy(rec[:, :, 2], typ_i)
            v.tensor_copy(rec[:, :, 3], w_in)
            v.tensor_scalar(dtile_i, dst_i, 7, None, ALU.logical_shift_right)
            v.tensor_scalar(tmp_i, src_i, 7, None, ALU.logical_shift_right)
            v.memset(pos, 0.0)
            link(v.tensor_reduce(weight_sum[0:EP, :], w_in, AX.X, ALU.add))
            v.tensor_copy(dtile, dtile_i)
            link(v.tensor_copy(stile, tmp_i))
            v.scalar_tensor_tensor(dlow, dtile, -float(P), rec[:, :, 1], ALU.mult, ALU.add)
            link(v.scalar_tensor_tensor(slow, stile, -float(P), rec[:, :, 0], ALU.mult, ALU.add))
            for b in steps.rounds(dve_, NT, 4):
                link(v.tensor_scalar(hit, dtile, tile_no[0:EP, bass.ds(b, 1)], None, ALU.is_equal))
                link(v.tensor_tensor_scan(run, ones[0:EP, 0:1].to_broadcast([EP, EC]), hit, 0.0, ALU.mult, ALU.add))
                v.tensor_scalar(total[0:EP, bass.ds(b, 1)], run[:, EC - 1:EC], 1.0, None, ALU.mult)
                link(v.tensor_tensor(hit, hit, run, ALU.mult))
                link(v.tensor_tensor(pos, pos, hit, ALU.add))
            ask_pe()
            link(v.tensor_scalar(tiles_i[:, :], ps[:, 512:512 + NT], float(P - 1), None, ALU.add))
            link(v.tensor_scalar(tiles_i[:, :], tiles_i[:, :], 7, None, ALU.logical_shift_right))
            link(v.tensor_copy(tiles[:, :], tiles_i[:, :]))
            link(v.tensor_tensor_scan(first_tile[:, :], ones[:, 0:1].to_broadcast([P, NT]), tiles[:, :], 0.0, ALU.mult, ALU.add))
            link(v.tensor_tensor(first_tile[:, :], first_tile[:, :], tiles[:, :], ALU.subtract))
            link(v.scalar_tensor_tensor(before[0:EP, :], first_tile[0:EP, :], float(P), ps[0:EP, 0:NT], ALU.mult, ALU.add))
            link(v.tensor_scalar(before[0:EP, :], before[0:EP, :], -1.0, None, ALU.add))
            for b in steps.rounds(dve_, NT, 2):
                cols = bass.ds(b, 1)
                link(v.tensor_scalar(hit, dtile, tile_no[0:EP, cols], before[0:EP, cols], ALU.is_equal, ALU.mult))
                link(v.tensor_tensor(pos, pos, hit, ALU.add))
            link(v.tensor_copy(slot_i, pos))
            v.tensor_scalar(hi_i, slot_i, 7, None, ALU.logical_shift_right)
            link(v.tensor_scalar(tmp_i, slot_i, P - 1, None, ALU.bitwise_and))
            link(v.scalar_tensor_tensor(slot, tmp_i, float(TILES), hi_i, ALU.mult, ALU.add))
            tell(slots_ready)
            link(v.memset(dst_tile[:, :], 0.0))
            for b in steps.rounds(dve_, NT - 1, 1):
                link(v.scalar_tensor_tensor(dst_tile[:, :], tile_no[:, :], first_tile[:, bass.ds(b + 1, 1)], dst_tile[:, :], ALU.is_ge, ALU.add))
            v.tensor_scalar(at_sums[:, :], dst_tile[:, :], float(D), None, ALU.mult)
            v.tensor_scalar(at_er_top[:, :], dst_tile[:, :], float(6 * HEADS), None, ALU.mult)
            v.tensor_scalar(at_agg[:, :], dst_tile[:, :], float(D + ZW), None, ALU.mult)
            v.memset(new_tile[:, 0:1], -BIG)
            link(v.tensor_tensor(new_tile[:, 1:TILES], dst_tile[:, 1:TILES], dst_tile[:, 0:TILES - 1], ALU.not_equal))
            link(v.tensor_scalar(new_tile[:, 1:TILES], new_tile[:, 1:TILES], -BIG, None, ALU.mult))
            link(v.tensor_tensor(before[:, :], first_tile[:, :], tiles[:, :], ALU.add))
            link(v.tensor_scalar(before[:, :], before[:, :], -1.0, 0.0, ALU.add, ALU.max))
            link(v.tensor_scalar(last_tile_i[:, :], before[:, :], float(HEADS), None, ALU.mult))
            tell(pe_go)
            asked["pe"] += 1
            for i in steps.rounds(dve_, DEG_ITERS, 2):
                for k in HALVES:
                    cols = bass.ds((i * 2 + k) * G, G)
                    dve_.wait_ge(degree_used[k], i + 1)
                    v.tensor_tensor(src_low[k], spread(slow[:, cols], P), across(lane[0:EP, :], G), ALU.is_equal)
                    v.tensor_tensor(dst_low[k], spread(dlow[:, cols], P), across(lane[0:EP, :], G), ALU.is_equal)
                    v.tensor_tensor(src_high[k], spread(stile[:, cols], NT), across(lane[0:EP, 0:NT], G), ALU.is_equal)
                    link(v.tensor_tensor(dst_high[k], spread(dtile[:, cols], NT), across(lane[0:EP, 0:NT], G), ALU.is_equal))
                    tell(degree_hot[k])
            dve_.wait_ge(pe_done, asked["pe"])
            v.tensor_scalar(stat[:, 6, :], ps[:, 0:NT], 1.0, None, ALU.max)
            v.tensor_scalar(stat[:, 7, :], ps[:, 512:512 + NT], 1.0, None, ALU.max)
            v.tensor_scalar(in_norm0[:, :], ps[:, 512:512 + NT], 0.0, None, ALU.is_gt)
            link(v.tensor_scalar(weight_mean[:, :], ps[:, 1024:1025], 1.0 / E, None, ALU.mult))
            ask_act()
            v.reciprocal(out_norm[:, :], stat[:, 4, :])
            link(v.reciprocal(in_norm[:, :], stat[:, 5, :]))
            link(v.tensor_tensor(in_norm0[:, :], in_norm0[:, :], in_norm[:, :], ALU.mult))

            dve_.wait_ge(late_loads, LATE_LOADS * 16)
            ask_pe()
            link(v.tensor_copy(w0T[:, :], ps[:, 0:P]))
            for l in range(L):
                for n, attn in enumerate((attn_l, attn_r)):
                    link(v.tensor_tensor(stage[0][:, 0:D], w_gat[:, l, 0:D], attn[:, l, :], ALU.mult))
                    link(v.tensor_reduce(w_gat[:, l, D + HEADS * n:D + HEADS * (n + 1)],
                                         stage[0][:, 0:D].rearrange("p (h d) -> p h d", h=HEADS), AX.X, ALU.add))
            link(v.scalar_tensor_tensor(gate_row[:, :], gate_row[:, :], weight_mean[:, :], row["L2_gnn_b_gate"][:, :], ALU.mult, ALU.add))

            def layer_norm(src, to):
                link(v.tensor_reduce(stat[:, 0, :], src[:, :, :], AX.X, ALU.add))
                link(v.tensor_scalar(stat[:, 0, :], stat[:, 0, :], 1.0 / D, None, ALU.mult))
                link(v.tensor_tensor(src[:, :, :], src[:, :, :], spread(stat[:, 0, :], D), ALU.subtract))
                link(v.tensor_tensor(to[:, :, :], src[:, :, :], src[:, :, :], ALU.mult))
                link(v.tensor_reduce(stat[:, 1, :], to[:, :, :], AX.X, ALU.add))
                link(v.tensor_scalar(stat[:, 2, :], stat[:, 1, :], 1.0 / D, LN_EPS, ALU.mult, ALU.add))
                ask_act()
                link(v.reciprocal(stat[:, 1, :], stat[:, 3, :]))
                link(v.tensor_tensor(to[:, :, :], src[:, :, :], spread(stat[:, 1, :], D), ALU.mult))

            def scaled(to, src, norm):
                link(v.tensor_tensor(to[:, :, :], src, spread(norm[:, :], D), ALU.mult))

            def make_rows(src, norm):
                for part_of in PARTS:
                    link(v.tensor_tensor(tmp[:, part_of, :], src[:, part_of, :], spread(norm[:, part_of], D), ALU.mult))
                    tell(rows_ready)

            def plus_row(to, src, r, op=ALU.add):
                link(v.tensor_tensor(to[:, :, :], src, across(r, NT), op))

            def add(to, one, other):
                link(v.tensor_tensor(to[:, :, :], one[:, :, :], other[:, :, :], ALU.add))

            def split(parts, src, rest):
                link(v.tensor_copy(parts[0], src))
                link(v.tensor_tensor(rest, src, parts[0], ALU.subtract))
                link(v.tensor_copy(parts[1], rest))
                link(v.tensor_tensor(rest, rest, parts[1], ALU.subtract))
                link(v.tensor_copy(parts[2], rest))

            def make_onehot(i, j, before_hot, before_p, weighted):
                k = j % 2
                dve_.wait_ge(*half_before(i, j, before_p))
                v.sem_inc(dve_passed, 1)
                cols = bass.ds((i * RING + j) * G, G)
                link(v.tensor_tensor(onehot[k][:, :, :], spread(local[:, cols], P), across(lane[:, :], G), ALU.is_equal))
                if weighted:
                    link(v.tensor_tensor(onehot[k][:, :, :], onehot[k][:, :, :], spread(weight[:, cols], P), ALU.mult))
                tell(onehot_ready[k])

            def make_members(i, j):
                k = j % 2
                dve_.wait_ge(wide_in[k], i * 32 + (16 + 16 * (j // 2)))
                v.sem_inc(dve_passed, 1)
                dve_.wait_ge(member_free[k], i * 2 + (1 + j // 2))
                v.sem_inc(dve_passed, 1)
                link(v.tensor_scalar(flat(member[k]), wide[k], part[:, :], None, ALU.is_equal))
                tell(wide_used[k])
                tell(member_made[k])

            def destination_rows():
                scratch = [flat(tmp2)[:, TILES * n:TILES * (n + 1)] for n in range(2)]
                whole, bit = (t.bitcast(i32) for t in scratch)
                link(v.tensor_scalar(scratch[1], local[:, :], 0.0, None, ALU.max))
                link(v.tensor_copy(whole, scratch[1]))
                for b in range(BITS):
                    link(v.tensor_scalar(bit, whole, b, 1, ALU.logical_shift_right, ALU.bitwise_and))
                    link(v.tensor_copy(bits[:, :, b], bit))
                link(v.tensor_scalar(bits[:, :, BITS], local[:, :], 0.0, None, ALU.is_lt))
                columns = flat(tmp2)[:, 2 * TILES:2 * TILES + P]
                part_i, low_i = columns[:, 0:1].bitcast(i32), columns[:, 1:2].bitcast(i32)
                row_no, block_no, head_no, from_bits, from_not, const = (columns[:, n:n + 1] for n in range(2, 8))
                coef, minus = columns[:, 8:8 + BITS], columns[:, 16:16 + BITS]
                in_block = columns[:, 24:24 + BLOCKS]
                link(v.tensor_copy(part_i, part[:, :]))
                for to, shift, low in ((row_no, 0, ROWS - 1), (block_no, 5, BLOCKS - 1), (head_no, 0, HEADS - 1)):
                    link(v.tensor_scalar(low_i, part_i, shift, low, ALU.logical_shift_right, ALU.bitwise_and))
                    link(v.tensor_copy(to, low_i))
                link(v.tensor_scalar(from_bits, row_no, float(SCORES), None, ALU.is_ge))
                link(v.tensor_scalar(from_not, row_no, float(NOT_BITS), None, ALU.is_ge))
                link(v.tensor_scalar(of_head[:, :], lane[:, 0:HEADS], head_no, None, ALU.is_equal))
                link(v.tensor_tensor(of_head[:, :], of_head[:, :], from_bits.to_broadcast([P, HEADS]), ALU.max))
                link(v.tensor_scalar(in_block, lane[:, 0:BLOCKS], block_no, None, ALU.is_equal))
                link(v.tensor_tensor(const, from_not, from_bits, ALU.subtract))
                link(v.tensor_scalar(const, const, BIG, None, ALU.mult))
                link(v.tensor_scalar(from_bits, from_bits, -1.0, 1.0, ALU.mult, ALU.add))
                link(v.tensor_tensor(const, const, from_bits, ALU.add))
                link(v.tensor_scalar(coef, lane[:, SCORES:FLAG], row_no, None, ALU.is_equal))
                link(v.tensor_scalar(minus, lane[:, NOT_BITS:NOT_BITS + BITS], row_no, None, ALU.is_equal))
                link(v.tensor_tensor(coef, coef, minus, ALU.subtract))
                link(v.tensor_scalar(coef, coef, BIG, None, ALU.mult))
                lowered = flat(tmp2)[:, 2 * TILES + P:2 * TILES + 2 * P]
                lane_i, lane_bit, lane_b = (flat(tmp2)[:, 2 * TILES + n * P:2 * TILES + (n + 1) * P] for n in (2, 3, 4))
                link(v.tensor_copy(lane_i.bitcast(i32), lane[:, :]))
                link(v.tensor_copy(lowered, const.to_broadcast([P, P])))
                for b in range(BITS):
                    link(v.tensor_scalar(lane_bit.bitcast(i32), lane_i.bitcast(i32), b, 1, ALU.logical_shift_right, ALU.bitwise_and))
                    link(v.tensor_copy(lane_b, lane_bit.bitcast(i32)))
                    link(v.scalar_tensor_tensor(lowered, lane_b, coef[:, b:b + 1], lowered, ALU.mult, ALU.add))
                for g in range(BLOCKS):
                    link(v.tensor_scalar(pick[:, g, :], lowered, in_block[:, g:g + 1], None, ALU.mult))

            def end_pass(p):
                for j in range(RING):
                    dve_.wait_ge(group_done[j], rounds_before(p + 1, LINEAR, MAXIMA, SUMS) + 1)

            def edge_sums(p):
                tell(pass_go)
                if p == 1:
                    destination_rows()
                each = (2 if WEIGHTED[p] else 1) + (1 if p == 0 else 0)
                for i in steps.rounds(dve_, ROUNDS, RING * each):
                    for j in range(RING):
                        make_onehot(i, j, rounds_before(p, LINEAR, SUMS), rounds_before(p, LINEAR, MAXIMA, SUMS), WEIGHTED[p])
                        if p == 0:
                            make_members(i, j)
                end_pass(p)

            def turn(src_to):
                ask_pe()
                link(v.tensor_copy(src_to[:, 0:NT, :], sums3))

            link(v.tensor_copy(tmp2[:, :, :], x[:, :, :]))
            layer_norm(tmp2, tmp)
            plus_row(tmp, tmp[:, :, :], row["L0_gnn_ln_gamma"][:, :], ALU.mult)
            plus_row(tmp, tmp[:, :, :], row["L0_gnn_ln_beta"][:, :])
            turn(hT)
            ask_pe()
            plus_row(tmp, sums3, row["L0_gnn_b"][:, :])
            dve_.wait_ge(grouped_loaded, 16)
            v.scalar_tensor_tensor(local[:, :], dst_tile[:, :], -float(P), grouped[:, :, 1], ALU.mult, ALU.add)
            v.scalar_tensor_tensor(minus_local[:, :], dst_tile[:, :], float(P), grouped[:, :, 1], ALU.mult, ALU.subtract)
            v.tensor_copy(src_row[:, 0:TILES], grouped[:, :, 0])
            v.scalar_tensor_tensor(rel_row[:, 0:TILES], grouped[:, :, 0], float(R), grouped[:, :, 2], ALU.mult, ALU.add)
            link(v.tensor_copy(weight[:, :], grouped[:, :, 3]))
            tell(grouped_ready)
            ask_pe()
            link(v.tensor_copy(local_T, ps[0:TILES // 4, 0:4 * P].rearrange("p (k e) -> p k e", k=4)))
            tell(local_ready)
            tell(rows_ready, len(PARTS))
            edge_sums(0)
            link(v.scalar_tensor_tensor(flat(tmp2), sums, 0.0, flat(x), ALU.max, ALU.add))
            add(tmp2, tmp2, x)
            layer_norm(tmp2, x)

            make_rows(x, in_norm0)
            edge_sums(1)
            scaled(h, sums3, in_norm0)
            make_rows(h, in_norm0)
            add(self_term, x, h)
            edge_sums(2)
            scaled(tmp2, sums3, in_norm0)
            add(tmp2, tmp2, self_term)
            link(v.scalar_tensor_tensor(flat(tmp2), flat(tmp2), 1.0 / 3, flat(x), ALU.mult, ALU.add))
            layer_norm(tmp2, x)
            tell(h_made, CHUNKS)

            def node_stage(l):
                def heads(ap):
                    return ap.rearrange("p b (h d) -> p b h d", h=HEADS)

                def close_sums(c):
                    cs = chunk(c)
                    v.tensor_tensor(heads(gat[:, cs, 0:D]), heads(agg[:, cs, D:2 * D]), spread(sc[:, cs, :], DH), ALU.mult)
                    link(v.tensor_tensor(self_term[:, cs, :], agg[:, cs, 0:D], self_term[:, cs, :], ALU.add))
                    link(v.tensor_tensor(gat[:, cs, 0:D], gat[:, cs, 0:D], across(b_gat[:, l - 1, :], cs.stop - cs.start), ALU.add))
                    tell(sums_made)

                if l:
                    link(v.tensor_scalar(sc[:, :, :], agg[:, :, 2 * D:D + ZW], 1e-30, None, ALU.max))
                    link(v.reciprocal(sc[:, :, :], sc[:, :, :]))
                    close_sums(0)
                for s in range(CHUNKS + 7):
                    if l and s + 1 < CHUNKS:
                        close_sums(s + 1)
                    c = s - 4
                    if l == 1 and 0 <= c < CHUNKS:
                        dve_.wait_ge(gate_out, c + 1)
                        link(v.scalar_tensor_tensor(h[:, chunk(c), :], h[:, chunk(c), :], 0.0,
                                                    gate[c % 2][:, 0:len(range(NT)[chunk(c)]), :], ALU.max, ALU.mult))
                        tell(h_made)
                    c = s - 1
                    if l and 0 <= c < CHUNKS:
                        here, width = h[:, chunk(c), :], len(range(NT)[chunk(c)])
                        dve_.wait_ge(fused, (l - 1) * CHUNKS + c + 1)
                        link(v.tensor_tensor(here, chunk_ps(FUSED_BANK, c), across(row["L2_gnn_b_fuse"][:, :], width), ALU.add))
                        if l == 1:
                            tell(hc_made)
                        else:
                            link(v.tensor_scalar(here, here, 0.0, None, ALU.max))
                            tell(h_made)
                    c = s - 3
                    if l == 1 and 0 <= c < CHUNKS:
                        width = len(range(NT)[chunk(c)])
                        dve_.wait_ge(gate_sum, c + 1)
                        link(v.tensor_tensor(gate[c % 2][:, 0:width, :], chunk_ps(GATE_BANK, c), across(gate_row[:, :], width), ALU.add))
                        tell(gate_in)
                    c = s - H_LAG[l] - 1 if l < L else -1
                    if 0 <= c < CHUNKS:
                        made = chunk_ps(Z_BANK, c, D + 2 * HEADS)
                        dve_.wait_ge(z_made, l * CHUNKS + c + 1)
                        v.tensor_copy(gat[:, chunk(c), :], made[:, :, 0:ZW])
                        link(v.tensor_copy(er[:, chunk(c), :], made[:, :, ZW:ZW + HEADS]))
                        tell(z_taken)
                        if chunk(c).stop in (FIRST_PART, NT):
                            tell(rows_ready)

            node_stage(0)

            for l in range(L):
                p = 3 + 2 * l
                before_p, before_m, before_s = rounds_before(p, LINEAR, MAXIMA, SUMS), l * ROUNDS, l * ROUNDS
                ask_pe()
                plus_row(self_term, sums3, b_rel[:, l, :])
                tell(pass_go)

                def split_scores(i, j):
                    k = j % 2
                    dve_.wait_ge(gathered[j], i * (16 * G) + (before_p + 1) * 16 * G)
                    v.sem_inc(dve_passed, 1)
                    dve_.wait_ge(*half_before(i, j, before_p))
                    v.sem_inc(dve_passed, 1)
                    here = bits[:, bass.ds((i * RING + j) * G, G), :]
                    v.tensor_copy(el_parts[k][:, :, SCORES:FLAG + 1], here)
                    v.tensor_scalar(el_parts[k][:, :, NOT_BITS:NOT_BITS + BITS], here[:, :, 0:BITS], -1.0, 1.0, ALU.mult, ALU.add)
                    split([el_parts[k][:, :, HEADS * n:HEADS * (n + 1)] for n in range(3)], ring[j][:, :, D:ZW], score[k][:, :, :])
                    tell(el_split[k])

                def maxima_round(i, last_round):
                    for j in range(RING):
                        for g in range(0, G, 2):
                            n = i * (RING * G // 2) + ((before_m * RING + j) * G // 2 + g // 2 + 1)
                            dve_.wait_ge(el_wide, n)
                            v.sem_inc(dve_passed, 1)
                            at = bass.ds(((i * RING + j) * G + g) * HEADS, 2 * HEADS)
                            v.tensor_reduce(flat(tile_top)[:, at], el_ps[g // 2 % PAIRS].rearrange("p g h e -> p (g h) e"), AX.X, ALU.max).then_inc(el_taken, 1)
                            if g == 0:
                                if j < RING - 1:
                                    split_scores(i, j + 1)
                                elif not last_round:
                                    split_scores(i + 1, 0)
                        dve_.wait_ge(el_taken, n + PAIRS)
                        tell(group_done[j])

                split_scores(0, 0)
                for i in steps.rounds(dve_, ROUNDS - 1, RING * 5):
                    maxima_round(i, False)
                maxima_round(ROUNDS - 1, True)
                tell(layer_free)
                for head in range(HEADS):
                    v.tensor_tensor_scan(run_top[:, :, head], new_tile[:, :], tile_top[:, :, head], 0.0, ALU.add, ALU.max).then_inc(dve, 1)
                    steps.add()
                dve_.wait_ge(dve, steps.now)
                for b in range(0, NT, 5):
                    _, columns = nc.values_load_multi_w_load_instructions(
                        last_tile_i[0:1, b:b + 5], engines=[mybir.EngineType.DVE], min_val=0, max_val=HEADS * (TILES - 1),
                        skip_runtime_bounds_check_because="the last edge tile of a destination tile, clamped at 0")
                    for n in range(5):
                        v.tensor_copy(top[:, b + n, :], flat(run_top)[:, bass.ds(columns[n], HEADS)]).then_inc(dve, 1)
                        steps.add()
                dve_.wait_ge(dve, steps.now)
                link(v.tensor_tensor(top[:, :, :], top[:, :, :], er[:, :, :], ALU.add))
                link(v.scalar_tensor_tensor(top[:, :, :], top[:, :, :], 0.2, top[:, :, :], ALU.mult, ALU.max))
                split([er_top[:, :, n, 0:HEADS] for n in range(3)], er[:, :, :], sc[:, :, :])
                split([er_top[:, :, n, HEADS:2 * HEADS] for n in range(3)], top[:, :, :], sc[:, :, :])
                link(v.memset(agg_flat, 0.0))
                p += 1
                before_p, before_hot = rounds_before(p, LINEAR, MAXIMA, SUMS), rounds_before(p, LINEAR, SUMS)
                tell(pass_go)


                def scores(i, j):
                    k = j % 2
                    use = i * 2 + (before_s * 2 + j // 2 + 1)
                    dve_.wait_ge(z_loaded[k], i * 32 + (before_s * 32 + 16 * (j // 2 + 1)))
                    v.sem_inc(dve_passed, 1)
                    dve_.wait_ge(er_top_ready[k], use + 1)
                    v.sem_inc(dve_passed, 1)
                    e = score[k][:, :, :]
                    link(v.tensor_tensor(e, z_in[k][:, :, D:ZW], er_top_ps[k][:, :, 0:HEADS], ALU.add))
                    link(v.scalar_tensor_tensor(e, e, 0.2, e, ALU.mult, ALU.max))
                    link(v.tensor_tensor(e, er_top_ps[k][:, :, HEADS:2 * HEADS], e, ALU.subtract))
                    tell(er_top_taken[k])
                    tell(score_ready[k])

                def messages(i, j):
                    k = j % 2
                    dve_.wait_ge(exp_ready[k], i * 2 + (before_s * 2 + j // 2 + 1))
                    v.sem_inc(dve_passed, 1)
                    v.tensor_copy(z_msg[k][:, :, D:ZW], score[k][:, :, :])
                    link(v.tensor_tensor(z_msg[k][:, :, 0:D].rearrange("p g (h d) -> p g h d", h=HEADS),
                                         z_in[k][:, :, 0:D].rearrange("p g (h d) -> p g h d", h=HEADS),
                                         spread(score[k][:, :, :], DH), ALU.mult))
                    tell(msg_ready[k])

                def sums_round(i, last_round):
                    for j in range(RING):
                        if j < RING - 1:
                            messages(i, j + 1)
                        elif not last_round:
                            messages(i + 1, 0)
                        columns = destinations(mybir.EngineType.DVE, at_agg, D + ZW, i, j)
                        for g in range(G):
                            n = i * (RING * G) + ((before_s * RING + j) * G + g + 1)
                            if g % 2 == 0:
                                dve_.wait_ge(z_sum, n + 1)
                                v.sem_inc(dve_passed, 1)
                            at = agg_flat[:, bass.ds(columns[g], D + ZW)]
                            v.tensor_tensor(at, at, msg_ps[g % MSG_SLOTS], ALU.add).then_inc(z_added, 1)
                            dve_.wait_ge(z_added, n + MSG_SLOTS)
                            if g == G // 2 - 1:
                                if j < 2:
                                    scores(i, j + 2)
                                elif not last_round:
                                    scores(i + 1, j - 2)
                        tell(group_done[j])

                scores(0, 0)
                scores(0, 1)
                messages(0, 0)
                for i in steps.rounds(dve_, ROUNDS - 1, RING * 4):
                    sums_round(i, False)
                sums_round(ROUNDS - 1, True)
                end_pass(p)
                node_stage(l + 1)
            add(tmp2, x, h)
            layer_norm(tmp2, x)

            for c in range(2):
                make_rows(h if c else x, out_norm)
                if c == 0:
                    link(v.tensor_copy(h[:, :, :], x[:, :, :]))
                edge_sums(3 + 2 * L + c)
                scaled(tmp, sums3, in_norm)
                turn(hT)
                ask_pe()
                plus_row(tmp, sums3, row[f"L3_gnn_b{c + 1}"][:, :])
                link(v.scalar_tensor_tensor(flat(h), flat(tmp), 0.0, flat(h), ALU.max, ALU.add))
            add(tmp2, x, h)
            layer_norm(tmp2, x)
            tell(rows_ready)


_INS = ["x", "src", "dst", "edge_type_16", "edge_weight", "L0_gnn_ln_gamma", "L0_gnn_ln_beta", "L0_gnn_W", "L0_gnn_b",
        "L2_gnn_W_rel", "L2_gnn_b_rel", "L2_gnn_W_loop", "L2_gnn_W_gat", "L2_gnn_attn_l", "L2_gnn_attn_r",
        "L2_gnn_b_gat", "L2_gnn_W_fuse", "L2_gnn_b_fuse", "L2_gnn_W_gate", "L2_gnn_b_gate", "L3_gnn_W1", "L3_gnn_b1",
        "L3_gnn_W2", "L3_gnn_b2"]


def kernel(**inputs):
    import numpy as _np
    import concourse.bacc as _bacc
    from concourse import mybir as _mybir
    from concourse.bass_utils import run_bass_kernel_spmd as _run

    nc = _bacc.Bacc("TRN2", target_bir_lowering=False, num_devices=1)
    arrays, args = {}, {}
    for name in _INS:
        a = _np.ascontiguousarray(inputs[name])
        arrays[f"in_{name}"] = a
        args[name] = nc.dram_tensor(f"in_{name}", a.shape, _mybir.dt.from_np(a.dtype), kind="ExternalInput").ap()
    out = nc.dram_tensor("out_0", (N, D), _mybir.dt.float32, kind="ExternalOutput").ap()
    gnn_stack(nc, args, out)
    r = _run(nc, [arrays], core_ids=[0])
    return r.results[0]["out_0"]
```
